# Optimizing a Trainium2 kernel written in Bass

```python
import numpy as np
import jax
import jax.numpy as jnp

def _softmax(x, axis=-1):
    return jax.nn.softmax(x, axis=axis)

def _gelu(x):
    return jax.nn.gelu(x, approximate=True)

def _silu(x):
    return jax.nn.silu(x)

def _sigmoid(x):
    return jax.nn.sigmoid(x)

def _layernorm(x, axis=-1, eps=1e-05):
    m = jnp.mean(x, axis=axis, keepdims=True)
    v = jnp.var(x, axis=axis, keepdims=True)
    return (x - m) / jnp.sqrt(v + eps)

def _scatter_add(tgt, idx, src, axis=0):
    return tgt.at[idx].add(src)

def _segment_sum(src, seg, n):
    return jax.ops.segment_sum(src, seg, n)
kernel_name = 'mk_xattn_ffn_d2_seqx_r8_dfef68'

def setup_inputs(seed: int=0):
    np.random.seed(seed)
    _w = jnp.asarray

    def _rec_inputs():
        import jax
        import jax.numpy as jnp
        _rk = jax.random.key(seed)
        x = -0.0003929 + 0.9999 * jax.random.normal(jax.random.fold_in(_rk, 1), (1, 1024, 128), jnp.float32)
        _lenS = 1024 - jax.random.randint(jax.random.fold_in(_rk, 7), (1,), 0, max(1, 1024 // 4) + 1, jnp.int32)
        _lenS2 = 6404 - jax.random.randint(jax.random.fold_in(_rk, 8), (1,), 0, max(1, 6404 // 4) + 1, jnp.int32)
        _ctx_1024P = jax.random.normal(jax.random.fold_in(_rk, 11), (1, 16, 128), jnp.float32)
        _ctx_1024c = jax.random.dirichlet(jax.random.fold_in(_rk, 511), 0.3 * jnp.ones((16,), jnp.float32), (1, 6404))
        _ctx_1024t = jnp.einsum('bsk,bkd->bsd', _ctx_1024c, _ctx_1024P)
        _ctx_1024t = _ctx_1024t * jax.lax.rsqrt(jnp.mean(jnp.square(_ctx_1024t)) + 1e-12) * 0.953939
        ctx_1024 = 2.81802e-05 + 1.00001 * (_ctx_1024t + 0.3 * jax.random.normal(jax.random.fold_in(_rk, 611), (1, 6404, 128), jnp.float32))
        return (x, ctx_1024)
    x, ctx_1024 = _rec_inputs()

    def _L0_xattn_setup():
        import jax, jax.numpy as jnp
        import numpy as np
        D1, D2, D3 = (128, 128, 128)
        key = jax.random.key(seed)
        k1, k2, kw, kb = jax.random.split(key, 4)
        x1 = jax.random.normal(k1, (8, 256, D1), dtype=jnp.float32)
        x2 = jax.random.normal(k2, (8, 256, D2), dtype=jnp.float32)
        bound = 1.0 / np.sqrt(D1 + D2)
        W = jax.random.uniform(kw, (D3, D1 + D2), minval=-bound, maxval=bound, dtype=jnp.float32)
        b = jax.random.uniform(kb, (D3,), minval=-bound, maxval=bound, dtype=jnp.float32)
        return {'x1': x1, 'x2': x2, 'W': W, 'b': b}
    _L0_xattn_all = _L0_xattn_setup()
    _L0_xattn_in = {k: v for k, v in _L0_xattn_all.items() if k in ('W', 'b')}
    del _L0_xattn_all

    def _L0_ffn_setup():
        import jax, jax.numpy as jnp
        import numpy as np
        E, D, F, GATE_DIM = (8, 128, 512, 16)
        B, T = (2, 256)
        key = jax.random.key(seed)
        ks = jax.random.split(key, 7)
        s = 0.02
        return {'hidden_states': jax.random.normal(ks[0], (B, T, D), dtype=jnp.float32), 'w_red': jax.random.normal(ks[1], (D, GATE_DIM), dtype=jnp.float32) * s, 'wg': jax.random.normal(ks[2], (E, GATE_DIM), dtype=jnp.float32), 'w1': jax.random.normal(ks[3], (E, D, F), dtype=jnp.float32) * s, 'b1': jax.random.normal(ks[4], (E, F), dtype=jnp.float32) * s, 'w2': jax.random.normal(ks[5], (E, F, D), dtype=jnp.float32) * s, 'b2': jax.random.normal(ks[6], (E, D), dtype=jnp.float32) * s}
    _L0_ffn_all = _L0_ffn_setup()
    _L0_ffn_in = {k: v for k, v in _L0_ffn_all.items() if k in ('w_red', 'wg', 'w1', 'b1', 'w2', 'b2')}
    del _L0_ffn_all

    def _L1_xattn_setup():
        import jax, jax.numpy as jnp
        import numpy as np
        B, S, D, H, DK = (4, 256, 128, 16, 64)

        def _proj(x, W, b):
            y = jnp.einsum('bsd,ed->bse', x, W) + b
            return y.reshape(x.shape[0], x.shape[1], H, DK).transpose(0, 2, 1, 3)
        key = jax.random.key(seed)
        ks = jax.random.split(key, 10)
        scale = 1.0 / np.sqrt(D)
        return {'input_Q': jax.random.normal(ks[0], (B, S, D), jnp.float32), 'input_K': jax.random.normal(ks[1], (B, S, D), jnp.float32), 'input_V': jax.random.normal(ks[2], (B, S, D), jnp.float32), 'Wq': jax.random.normal(ks[3], (H * DK, D), jnp.float32) * scale, 'bq': jax.random.normal(ks[4], (H * DK,), jnp.float32) * scale, 'Wk': jax.random.normal(ks[5], (H * DK, D), jnp.float32) * scale, 'bk': jax.random.normal(ks[6], (H * DK,), jnp.float32) * scale, 'Wv': jax.random.normal(ks[7], (H * DK, D), jnp.float32) * scale, 'bv': jax.random.normal(ks[8], (H * DK,), jnp.float32) * scale, 'Wo': jax.random.normal(ks[9], (D, H * DK), jnp.float32) * scale}
    _L1_xattn_all = _L1_xattn_setup()
    _L1_xattn_in = {k: v for k, v in _L1_xattn_all.items() if k in ('Wq', 'bq', 'Wk', 'bk', 'Wv', 'bv', 'Wo')}
    del _L1_xattn_all

    def _L1_ffn_setup():
        import jax, jax.numpy as jnp
        import numpy as np
        HIDDEN = 128
        INTER = 512
        N_EXPERTS = 8

        def geglu(x, w1, w2, w3):
            return jax.nn.gelu(x @ w1, approximate=False) * (x @ w2) @ w3
        key = jax.random.key(seed)
        ks = jax.random.split(key, 8)
        s = 0.02
        x = jax.random.normal(ks[0], (2, 256, HIDDEN), dtype=jnp.float32)
        w1s = jax.random.normal(ks[1], (HIDDEN, INTER), dtype=jnp.float32) * s
        w2s = jax.random.normal(ks[2], (HIDDEN, INTER), dtype=jnp.float32) * s
        w3s = jax.random.normal(ks[3], (INTER, HIDDEN), dtype=jnp.float32) * s
        W1 = jax.random.normal(ks[4], (N_EXPERTS, HIDDEN, INTER), dtype=jnp.float32) * s
        W2 = jax.random.normal(ks[5], (N_EXPERTS, HIDDEN, INTER), dtype=jnp.float32) * s
        W3 = jax.random.normal(ks[6], (N_EXPERTS, INTER, HIDDEN), dtype=jnp.float32) * s
        Wg = jax.random.normal(ks[7], (HIDDEN, N_EXPERTS), dtype=jnp.float32) * s
        return {'x': x, 'w1s': w1s, 'w2s': w2s, 'w3s': w3s, 'W1': W1, 'W2': W2, 'W3': W3, 'Wg': Wg}
    _L1_ffn_all = _L1_ffn_setup()
    _L1_ffn_in = {k: v for k, v in _L1_ffn_all.items() if k in ('w1s', 'w2s', 'w3s', 'W1', 'W2', 'W3', 'Wg')}
    del _L1_ffn_all
    return {'x': x, 'ctx_1024': ctx_1024, 'L0_xattn_W': _L0_xattn_in['W'], 'L0_xattn_b': _L0_xattn_in['b'], 'L0_ffn_w_red': _L0_ffn_in['w_red'], 'L0_ffn_wg': _L0_ffn_in['wg'], 'L0_ffn_w1': _L0_ffn_in['w1'], 'L0_ffn_b1': _L0_ffn_in['b1'], 'L0_ffn_w2': _L0_ffn_in['w2'], 'L0_ffn_b2': _L0_ffn_in['b2'], 'L1_xattn_Wq': _L1_xattn_in['Wq'], 'L1_xattn_bq': _L1_xattn_in['bq'], 'L1_xattn_Wk': _L1_xattn_in['Wk'], 'L1_xattn_bk': _L1_xattn_in['bk'], 'L1_xattn_Wv': _L1_xattn_in['Wv'], 'L1_xattn_bv': _L1_xattn_in['bv'], 'L1_xattn_Wo': _L1_xattn_in['Wo'], 'L1_ffn_w1s': _L1_ffn_in['w1s'], 'L1_ffn_w2s': _L1_ffn_in['w2s'], 'L1_ffn_w3s': _L1_ffn_in['w3s'], 'L1_ffn_W1': _L1_ffn_in['W1'], 'L1_ffn_W2': _L1_ffn_in['W2'], 'L1_ffn_W3': _L1_ffn_in['W3'], 'L1_ffn_Wg': _L1_ffn_in['Wg']}

def reference(x, ctx_1024, L0_xattn_W, L0_xattn_b, L0_ffn_w_red, L0_ffn_wg, L0_ffn_w1, L0_ffn_b1, L0_ffn_w2, L0_ffn_b2, L1_xattn_Wq, L1_xattn_bq, L1_xattn_Wk, L1_xattn_bk, L1_xattn_Wv, L1_xattn_bv, L1_xattn_Wo, L1_ffn_w1s, L1_ffn_w2s, L1_ffn_w3s, L1_ffn_W1, L1_ffn_W2, L1_ffn_W3, L1_ffn_Wg):
    import jax
    import jax.numpy as jnp

    def _L0_xattn_ref(x1, x2, W, b):
        import jax, jax.numpy as jnp
        import numpy as np
        D1, D2, D3 = (128, 128, 128)
        d1 = x1.shape[-1]
        W1 = W[:, :d1]
        W2 = W[:, d1:]
        part1 = jnp.einsum('bld,ed->ble', x1, W1)
        part2 = jnp.einsum('bld,ed->be', x2, W2) / x2.shape[1]
        return part1 + part2[:, None, :] + b

    def _L0_ffn_ref(hidden_states, w_red, wg, w1, b1, w2, b2):
        import jax, jax.numpy as jnp
        import numpy as np
        E, D, F, GATE_DIM = (8, 128, 512, 16)
        B, T = (2, 256)
        b, t, c = hidden_states.shape
        x = hidden_states.reshape(-1, c)
        red = x @ w_red
        wg_n = wg / jnp.maximum(jnp.linalg.norm(wg, axis=1, keepdims=True), 0.0001)
        logits = red @ wg_n.T
        gates = jax.nn.softmax(logits, axis=1)
        idx = jnp.argmax(gates, axis=1)
        scores = jnp.take_along_axis(gates, idx[:, None], axis=1)
        h = jax.nn.gelu(jnp.einsum('td,edf->etf', x, w1) + b1[:, None, :], approximate=False)
        y = jnp.einsum('etf,efd->etd', h, w2) + b2[:, None, :]
        out = jnp.take_along_axis(y, idx[None, :, None], axis=0)[0]
        out = out * scores
        return out.reshape(b, t, c)

    def _L1_xattn_ref(input_Q, input_K, input_V, Wq, bq, Wk, bk, Wv, bv, Wo):
        import jax, jax.numpy as jnp
        import numpy as np
        B, S, D, H, DK = (4, 256, 128, 16, 64)

        def _proj(x, W, b):
            y = jnp.einsum('bsd,ed->bse', x, W) + b
            return y.reshape(x.shape[0], x.shape[1], H, DK).transpose(0, 2, 1, 3)
        Q = _proj(input_Q, Wq, bq)
        K = _proj(input_K, Wk, bk)
        V = _proj(input_V, Wv, bv)
        scores = jnp.einsum('bhqd,bhkd->bhqk', Q, K) / np.sqrt(DK).astype(np.float32)
        attn = jax.nn.softmax(scores, axis=-1)
        context = jnp.einsum('bhqk,bhkd->bhqd', attn, V)
        context = context.transpose(0, 2, 1, 3).reshape(input_Q.shape[0], -1, H * DK)
        return jnp.einsum('bse,de->bsd', context, Wo)

    def _L1_ffn_ref(x, w1s, w2s, w3s, W1, W2, W3, Wg):
        import jax, jax.numpy as jnp
        import numpy as np
        HIDDEN = 128
        INTER = 512
        N_EXPERTS = 8

        def geglu(x, w1, w2, w3):
            return jax.nn.gelu(x @ w1, approximate=False) * (x @ w2) @ w3
        B, T, C = x.shape
        xf = x.reshape(-1, C)
        shared = geglu(xf, w1s, w2s, w3s)
        logits = xf @ Wg
        idx = jnp.argmax(logits, axis=-1)
        final = jnp.zeros_like(xf)
        for e in range(N_EXPERTS):
            y = geglu(xf, W1[e], W2[e], W3[e])
            final = final + jnp.where((idx == e)[:, None], y, 0.0)
        return (shared + final).reshape(B, T, C)
    x = x + _L0_xattn_ref(_layernorm(x, axis=-1), ctx_1024, L0_xattn_W, L0_xattn_b)
    x = x + _L0_ffn_ref(_layernorm(x, axis=-1), L0_ffn_w_red, L0_ffn_wg, L0_ffn_w1, L0_ffn_b1, L0_ffn_w2, L0_ffn_b2)
    x = x + _L1_xattn_ref(_layernorm(x, axis=-1), ctx_1024, ctx_1024, L1_xattn_Wq, L1_xattn_bq, L1_xattn_Wk, L1_xattn_bk, L1_xattn_Wv, L1_xattn_bv, L1_xattn_Wo)
    x = x + _L1_ffn_ref(_layernorm(x, axis=-1), L1_ffn_w1s, L1_ffn_w2s, L1_ffn_w3s, L1_ffn_W1, L1_ffn_W2, L1_ffn_W3, L1_ffn_Wg)
    return x

_drawn_inputs = setup_inputs


def setup_inputs(seed=0):
    import zlib

    import numpy as np

    out = dict(_drawn_inputs(seed))
    spreads = {}
    factors = {'L0_xattn_b': 2.774,
     'L0_ffn_w_red': 8.0,
     'L0_ffn_wg': 8.0,
     'L0_ffn_w1': 8.0,
     'L0_ffn_b1': 8.0,
     'L0_ffn_w2': 8.0,
     'L0_ffn_b2': 8.0,
     'L1_xattn_bk': 8.0,
     'L1_ffn_w1s': 8.0,
     'L1_ffn_w2s': 8.0,
     'L1_ffn_w3s': 8.0,
     'L1_ffn_W1': 8.0,
     'L1_ffn_W2': 8.0,
     'L1_ffn_W3': 8.0,
     'L1_ffn_Wg': 8.0}
    for name, (base, spread) in spreads.items():
        noise = np.random.default_rng([zlib.crc32(name.encode()), seed]).standard_normal(out[name].shape)
        drawn = base * np.exp(spread * noise) if base else spread * noise
        out[name] = jnp.asarray(drawn.astype(out[name].dtype))
    for name, factor in factors.items():
        out[name] = (out[name] * factor).astype(out[name].dtype)
    return out
```

```python
import concourse.bass as bass
from concourse import mybir
from contextlib import ExitStack

FP32 = mybir.dt.float32
FP16 = mybir.dt.float16
ALU = mybir.AluOpType
ACT = mybir.ActivationFunctionType
AX = mybir.AxisListType.X

P = 128
D = 128
TOK = 1024
TT = TOK // P
HALF = 512
KEYS = 6404
KT = -(-KEYS // P)
KPAD = KT * P
HEADS, DK = 16, 64
PAIRS = HEADS // 2
FF = 512
FC = FF // P
EPS = 1e-5

C_SCALE = 0.5
W_SCALE = 16.0
QKV_SCALE = C_SCALE * W_SCALE
WQ_SCALE = QKV_SCALE
MOE_SCALE = 16.0
EXP_SCALE = 1.0 / (QKV_SCALE * QKV_SCALE * DK ** 0.5)
MAX_STEP = 1024.0

CHUNK_TILES = 4
CHUNKS = -(-KT // CHUNK_TILES)
STEPS = -(-KT // 2)
SLOTS = 4
V_W = 2 * DK + 1


class Linear:

    def __init__(self, variable=None, terms=(), constant=0):
        self.terms = list(terms) if variable is None else [(1, variable)]
        self.constant = constant

    def __add__(self, other):
        if isinstance(other, Linear):
            terms = list(self.terms)
            for k, v in other.terms:
                same = [n for n, (_, w) in enumerate(terms) if w is v]
                if same:
                    terms[same[0]] = (terms[same[0]][0] + k, v)
                else:
                    terms.append((k, v))
            return Linear(terms=terms, constant=self.constant + other.constant)
        return Linear(terms=self.terms, constant=self.constant + other)

    def __sub__(self, other):
        return self + -other

    def __mul__(self, k):
        return Linear(terms=[(c * k, v) for c, v in self.terms], constant=self.constant * k)

    __radd__, __rmul__ = __add__, __mul__

    def value(self):
        total = self.constant
        for k, v in self.terms:
            total = v * k + total
        return total


def value(x):
    return x.value() if isinstance(x, Linear) else x


def ds(start, size):
    return bass.ds(value(start), size)


def wait(engine, semaphore, count):
    if not (isinstance(count, int) and count <= 0):
        engine.wait_ge(semaphore, value(count))


def passed(engine, semaphore):
    engine.sem_inc(semaphore, 1)


def chunk_tiles(last):
    return KT - CHUNK_TILES * (CHUNKS - 1) if last else CHUNK_TILES


def split_lo(vec, lo, src, scale, hi):
    return vec.scalar_tensor_tensor(out=lo, in0=src, scalar=scale, in1=hi, op0=ALU.mult, op1=ALU.subtract)


def layernorm_block(nc, name, x_res, ident, xT, xTh, xTl):
    with ExitStack() as ctx:
        stats = ctx.enter_context(nc.sbuf_tensor(f"{name}_stats", [P, TT, 6], FP32))
        mv = ctx.enter_context(nc.sbuf_tensor(f"{name}_mv", [P, TT, 2], FP32))
        rstd = ctx.enter_context(nc.sbuf_tensor(f"{name}_rstd", [P, TT], FP32))
        xn = ctx.enter_context(nc.sbuf_tensor(f"{name}_xn", [P, TT, D], FP32))
        tp = [ctx.enter_context(nc.psum_tensor(f"{name}_tp{i}", [P, HALF], FP32)) for i in range(2)]
        chain = ctx.enter_context(nc.semaphore(f"{name}_chain"))
        var_ready = ctx.enter_context(nc.semaphore(f"{name}_var_ready"))
        rooted = ctx.enter_context(nc.semaphore(f"{name}_rooted"))
        normed = ctx.enter_context(nc.semaphore(f"{name}_normed"))
        turned = ctx.enter_context(nc.semaphore(f"{name}_turned"))
        hi_done = ctx.enter_context(nc.semaphore(f"{name}_hi_done"))
        block = ctx.enter_context(nc.Block())

        @block.vector
        def _(dve):
            for t in range(TT):
                nc.vector.bn_stats(stats[:, t, :], x_res[:, t, :]).then_inc(chain, 1)
            dve.wait_ge(chain, TT)
            for t in range(TT):
                nc.vector.bn_aggr(mv[:, t, :], stats[:, t, :]).then_inc(chain, 1)
            dve.wait_ge(chain, 2 * TT)
            nc.vector.tensor_scalar(rstd[:], mv[:, :, 1], EPS, None, ALU.add).then_inc(var_ready, 1)
            dve.wait_ge(rooted, 1)
            nc.vector.reciprocal(rstd[:], rstd[:]).then_inc(chain, 1)
            dve.wait_ge(chain, 2 * TT + 1)
            for t in range(TT):
                nc.vector.tensor_scalar(xn[:, t, :], x_res[:, t, :], mv[:, t, 0:1], rstd[:, t:t + 1],
                                        ALU.subtract, ALU.mult).then_inc(normed, 1)
            if xTl is not None:
                for i in range(2):
                    dve.wait_ge(hi_done, i + 1)
                    split_lo(nc.vector, xTl[:, i * HALF:(i + 1) * HALF], tp[i][:], 1.0,
                             xTh[:, i * HALF:(i + 1) * HALF])

        @block.tensor
        def _(pe):
            for t in range(TT):
                pe.wait_ge(normed, t + 1)
                nc.tensor.transpose(tp[t // 4][:, (t % 4) * P:(t % 4 + 1) * P], xn[:, t, :],
                                    ident[:]).then_inc(turned, 1)

        @block.scalar
        def _(act):
            act.wait_ge(var_ready, 1)
            nc.scalar.activation(rstd[:], rstd[:], ACT.Sqrt).then_inc(rooted, 1)
            for i in range(2):
                act.wait_ge(turned, 4 * (i + 1))
                if xT is not None:
                    nc.scalar.activation(xT[:, i * HALF:(i + 1) * HALF], tp[i][:], ACT.Copy)
                if xTh is not None:
                    nc.scalar.activation(xTh[:, i * HALF:(i + 1) * HALF], tp[i][:], ACT.Copy).then_inc(hi_done, 1)


def one_hot_first_max(nc, link, logits, peak, rank, value, hot, E):
    bc = lambda ap: ap.unsqueeze(2).to_broadcast([P, TT, E])
    link(nc.vector.reduce_max(peak[:], logits[:], AX))
    link(nc.vector.tensor_tensor(hot[:], logits[:], bc(peak[:]), ALU.is_equal))
    link(nc.vector.tensor_tensor(value[:], hot[:], rank[:].unsqueeze(1).to_broadcast([P, TT, E]), ALU.mult))
    link(nc.vector.reduce_max(peak[:], value[:], AX))
    link(nc.vector.tensor_tensor(hot[:], value[:], bc(peak[:]), ALU.is_equal))



def moe_block(nc, name, E, gated, xTh, xTl, w_up, w_gate, w_down, b_up, gates, x_res):
    NW = 3 if gated else 2
    with ExitStack() as ctx:
        sb = lambda n, s, dt: ctx.enter_context(nc.sbuf_tensor(f"{name}_{n}", s, dt))
        ps = lambda n: [ctx.enter_context(nc.psum_tensor(f"{name}_{n}{i}", [P, HALF], FP32)) for i in range(2)]
        sem = lambda n: ctx.enter_context(nc.semaphore(f"{name}_{n}"))
        raw = sb("raw", [P, 2 * NW * FF], FP32)
        wh = sb("wh", [P, 2 * NW * FF], FP16)
        wl = sb("wl", [P, 2 * NW * FF], FP16)
        gelu = sb("gelu", [P, 2, HALF], FP32)
        hidden = sb("hidden", [P, 2, HALF], FP32) if gated else gelu
        hh = sb("hh", [P, 2, FC * HALF], FP16)
        hl = sb("hl", [P, 2, FC * HALF], FP16)
        up, down = ps("up"), ps("down")
        gate = ps("gate") if gated else None
        w_loaded, whi_done, w_split = sem("w_loaded"), sem("whi_done"), sem("w_split")
        up_full, gelu_done, hidden_done = sem("up_full"), sem("gelu_done"), sem("hidden_done")
        hi_done, lo_done = sem("hi_done"), sem("lo_done")
        down_full, added = sem("down_full"), sem("added")
        act_passed, sp_passed = sem("act_passed"), sem("sp_passed")
        if not gated:
            hidden_done = gelu_done
        block = ctx.enter_context(nc.Block())
        WSET = NW * FF
        DOWN = (NW - 1) * FF
        sources = [w_up, w_gate, w_down] if gated else [w_up, w_down]

        @block.sync
        def _(sp):
            def load(e):
                wait(sp, w_split, e - 1)
                for n, src in enumerate(sources):
                    sp.dma_start(raw[:, ds(value(e) % 2 * WSET + n * FF, FF)],
                                 src[:, ds(e * FF, FF)]).then_inc(w_loaded, 16)
                wait(sp, w_loaded, 16 * NW * (e + 1))
                passed(sp, sp_passed)

            load(0)
            load(1)
            with sp.Fori(0, E - 2) as n:
                load(Linear(n) + 2)

        @block.tensor
        def _(pe):
            def up_item(e, h):
                if h == 0:
                    wait(pe, w_split, e + 1)
                for f in range(FC):
                    wait(pe, hidden_done, (2 * e + h) * FC + f - 1)
                    for n, bank in enumerate([up, gate] if gated else [up]):
                        col = ds(value(e) % 2 * WSET + n * FF + f * P, P)
                        tok = slice(h * HALF, (h + 1) * HALF)
                        nc.tensor.matmul(bank[f % 2][:], wh[:, col], xTh[:, tok], start=True, stop=False)
                        nc.tensor.matmul(bank[f % 2][:], wh[:, col], xTl[:, tok], start=False, stop=False)
                        last = nc.tensor.matmul(bank[f % 2][:], wl[:, col], xTh[:, tok], start=False, stop=True)
                    last.then_inc(up_full, 1)

            def down_item(e, h):
                wait(pe, lo_done, (2 * e + h + 1) * FC)
                wait(pe, added, 2 * e + h - 1)
                for j in range(HALF // P):
                    out = down[h][:, j * P:(j + 1) * P]
                    for f in range(FC):
                        lhs = slice(f * HALF + j * P, f * HALF + (j + 1) * P)
                        col = ds(value(e) % 2 * WSET + DOWN + f * P, P)
                        nc.tensor.matmul(out, hh[:, h, lhs], wh[:, col], start=f == 0, stop=False)
                        nc.tensor.matmul(out, hh[:, h, lhs], wl[:, col], start=False, stop=False)
                        last = nc.tensor.matmul(out, hl[:, h, lhs], wh[:, col], start=False, stop=f == FC - 1)
                last.then_inc(down_full, 1)

            up_item(0, 0)
            up_item(0, 1)
            down_item(0, 0)
            with pe.Fori(0, E - 1) as n:
                e = Linear(n) + 1
                up_item(e, 0)
                down_item(e - 1, 1)
                up_item(e, 1)
                down_item(e, 0)
            down_item(E - 1, 1)

        @block.scalar
        def _(act):
            def split_hi(e):
                wait(act, w_loaded, 16 * NW * (e + 1))
                wait(act, down_full, 2 * (e - 1))
                cols = ds(value(e) % 2 * WSET, WSET)
                nc.scalar.activation(wh[:, cols], raw[:, cols], ACT.Copy, scale=MOE_SCALE).then_inc(whi_done, 1)

            def cast(e, h, f):
                if f == 0:
                    wait(act, down_full, 2 * e + h - 1)
                wait(act, hidden_done, (2 * e + h) * FC + f + 1)
                nc.scalar.activation(hh[:, h, f * HALF:(f + 1) * HALF], hidden[:, f % 2, :],
                                     ACT.Copy).then_inc(hi_done, 1)

            def item(e, h):
                for f in range(FC):
                    n = (2 * e + h) * FC + f
                    wait(act, up_full, n + 1)
                    wait(act, hidden_done if gated else lo_done, n - 1)
                    if b_up is not None:
                        passed(act, act_passed)
                    bias = b_up[:, ds(e * FC + f, 1)] if b_up is not None else 0.0
                    nc.scalar.activation(gelu[:, f % 2, :], up[f % 2][:], ACT.Gelu, bias=bias,
                                         scale=1.0 / MOE_SCALE).then_inc(gelu_done, 1)
                    if f:
                        cast(e, h, f - 1)
                cast(e, h, FC - 1)

            split_hi(0)
            item(0, 0)
            split_hi(1)
            item(0, 1)
            with act.Fori(0, E - 2) as n:
                e = Linear(n) + 1
                item(e, 0)
                split_hi(e + 1)
                item(e, 1)
            item(E - 1, 0)
            item(E - 1, 1)

        @block.vector
        def _(dve):
            def split_rest(e):
                wait(dve, whi_done, e + 1)
                cols = ds(value(e) % 2 * WSET, WSET)
                split_lo(nc.vector, wl[:, cols], raw[:, cols], MOE_SCALE, wh[:, cols]).then_inc(w_split, 1)

            def rest(e, h, f):
                wait(dve, hi_done, (2 * e + h) * FC + f + 1)
                nc.vector.tensor_tensor(hl[:, h, f * HALF:(f + 1) * HALF], hidden[:, f % 2, :],
                                        hh[:, h, f * HALF:(f + 1) * HALF], ALU.subtract).then_inc(lo_done, 1)

            def add(e, h):
                wait(dve, down_full, 2 * e + h + 1)
                wait(dve, added, 2 * e + h - 1)
                for j in range(HALF // P):
                    t = h * (HALF // P) + j
                    last = nc.vector.scalar_tensor_tensor(
                        out=x_res[:, t, :], in0=down[h][:, j * P:(j + 1) * P],
                        scalar=gates[:, ds(e * TT + t, 1)], in1=x_res[:, t, :], op0=ALU.mult, op1=ALU.add)
                last.then_inc(added, 1)

            def item(e, h, before):
                for f in range(FC):
                    if gated:
                        n = (2 * e + h) * FC + f
                        wait(dve, gelu_done, n + 1)
                        wait(dve, lo_done, n - 1)
                        nc.vector.scalar_tensor_tensor(out=hidden[:, f % 2, :], in0=gate[f % 2][:],
                                                       scalar=1.0 / MOE_SCALE, in1=gelu[:, f % 2, :],
                                                       op0=ALU.mult, op1=ALU.mult).then_inc(hidden_done, 1)
                    if f:
                        rest(e, h, f - 1)
                    if f == 1 and before is not None:
                        add(*before)
                rest(e, h, FC - 1)

            split_rest(0)
            item(0, 0, None)
            split_rest(1)
            item(0, 1, None)
            item(1, 0, (0, 0))
            split_rest(2)
            item(1, 1, (0, 1))
            with dve.Fori(0, E - 3) as n:
                e = Linear(n) + 2
                item(e, 0, (e - 1, 0))
                split_rest(e + 1)
                item(e, 1, (e - 1, 1))
            item(E - 1, 0, (E - 2, 0))
            item(E - 1, 1, (E - 2, 1))
            add(E - 1, 0)
            add(E - 1, 1)


def load_block(nc, name, loads, scale=()):
    with ExitStack() as ctx:
        loaded = ctx.enter_context(nc.semaphore(f"loaded_{name}"))
        block = ctx.enter_context(nc.Block())

        @block.sync
        def _(sp):
            for dst, src in loads:
                sp.dma_start(dst, src).then_inc(loaded, 16)
            sp.wait_ge(loaded, 16 * len(loads))

        @block.vector
        def _(dve):
            dve.wait_ge(loaded, 16 * len(loads))
            for tile, factor in scale:
                nc.vector.tensor_scalar(tile[:], tile[:], factor, None, ALU.mult)


def identity_block(nc, ident, rank8):
    with ExitStack() as ctx:
        made = ctx.enter_context(nc.semaphore("identity_made"))
        block = ctx.enter_context(nc.Block())

        @block.gpsimd
        def _(pool):
            nc.gpsimd.memset(ident[:], 0.0).then_inc(made, 1)
            pool.wait_ge(made, 1)
            nc.gpsimd.affine_select(out=ident[:], in_=ident[:], compare_op=ALU.not_equal, fill=1.0, base=0,
                                    pattern=[[-1, P]], channel_multiplier=1)

        @block.vector
        def _(dve):
            for e in range(8):
                nc.vector.memset(rank8[:, e:e + 1], float(8 - e))


def l0_linear_block(nc, x_res, xT, ctx_d, ctx_h, ctx_l, w1T, w2T, bias):
    PIECES = 4
    PIECE = KEYS // PIECES
    with ExitStack() as ctx:
        sb = lambda n, s, dt: ctx.enter_context(nc.sbuf_tensor(f"l0_{n}", s, dt))
        raw = sb("ctx_raw", [P, KEYS], FP32)
        sums = sb("ctx_sums", [P, PIECES], FP32)
        mean = sb("ctx_mean", [P, 1], FP32)
        mean_rows = sb("mean_rows", [P, P], FP32)
        ones = sb("ones", [P, P], FP32)
        out = [ctx.enter_context(nc.psum_tensor(f"l0_out{i}", [P, HALF], FP32)) for i in range(2)]
        loaded = [ctx.enter_context(nc.semaphore(f"l0_ctx_loaded{i}")) for i in range(PIECES)]
        hi_done = ctx.enter_context(nc.semaphore("l0_hi_done"))
        chain = ctx.enter_context(nc.semaphore("l0_chain"))
        mean_ready = ctx.enter_context(nc.semaphore("l0_mean_ready"))
        product = ctx.enter_context(nc.semaphore("l0_product"))
        block = ctx.enter_context(nc.Block())
        piece = lambda i: slice(i * PIECE, (i + 1) * PIECE)

        @block.sync
        def _(sp):
            for i in range(PIECES):
                sp.dma_start(raw[:, piece(i)], ctx_d[:, piece(i)]).then_inc(loaded[i], 16)

        @block.scalar
        def _(act):
            for i in range(PIECES):
                act.wait_ge(loaded[i], 16)
                nc.scalar.activation(ctx_h[:, piece(i)], raw[:, piece(i)], ACT.Copy, scale=C_SCALE).then_inc(hi_done, 1)

        @block.vector
        def _(dve):
            nc.vector.memset(ones[:], 1.0).then_inc(chain, 1)
            nc.vector.memset(ctx_h[:, KEYS:KPAD], 0.0)
            nc.vector.memset(ctx_l[:, KEYS:KPAD], 0.0)
            for i in range(PIECES):
                dve.wait_ge(loaded[i], 16)
                nc.vector.reduce_sum(sums[:, i:i + 1], raw[:, piece(i)], AX).then_inc(chain, 1)
                dve.wait_ge(hi_done, i + 1)
                split_lo(nc.vector, ctx_l[:, piece(i)], raw[:, piece(i)], C_SCALE, ctx_h[:, piece(i)])
            dve.wait_ge(chain, PIECES + 1)
            nc.vector.reduce_sum(mean[:], sums[:], AX).then_inc(chain, 1)
            dve.wait_ge(chain, PIECES + 2)
            nc.vector.tensor_scalar(mean_rows[:], ones[:], mean[:], 1.0 / KEYS, ALU.mult, ALU.mult).then_inc(mean_ready, 1)
            for t in range(TT):
                nc.vector.tensor_tensor(x_res[:, t, :], x_res[:, t, :], bias[:], ALU.add).then_inc(chain, 1)
            for t in range(TT):
                dve.wait_ge(product, 4 * (t // 4 + 1))
                dve.wait_ge(chain, PIECES + 3 + t)
                nc.vector.tensor_tensor(x_res[:, t, :], x_res[:, t, :], out[t // 4][:, (t % 4) * P:(t % 4 + 1) * P], ALU.add)

        @block.tensor
        def _(pe):
            pe.wait_ge(mean_ready, 1)
            for t in range(TT):
                o = out[t // 4][:, (t % 4) * P:(t % 4 + 1) * P]
                nc.tensor.matmul(o, xT[:, t * P:(t + 1) * P], w1T[:], start=True, stop=False)
                nc.tensor.matmul(o, mean_rows[:], w2T[:], start=False, stop=True).then_inc(product, 1)


def l0_router_block(nc, x_res, xT, w_red, wg, b2, ident, rank8, gates):
    E, G = 8, 16
    with ExitStack() as ctx:
        sb = lambda n, s: ctx.enter_context(nc.sbuf_tensor(f"r0_{n}", s, FP32))
        sq, ss, wgn, wgnT, redT = sb("sq", [E, G]), sb("ss", [E, 1]), sb("wgn", [E, G]), sb("wgnT", [G, E]), sb("redT", [G, TOK])
        logits, value, hot, ex, score = sb("logits", [P, TT, E]), sb("value", [P, TT, E]), sb("hot", [P, TT, E]), sb("ex", [P, TT, E]), sb("score", [P, TT])
        peak, top, scoreT = sb("peak", [P, TT]), sb("top", [P, TT]), sb("scoreT", [E, TOK])
        wT_ps = ctx.enter_context(nc.psum_tensor("r0_wT", [P, HALF], FP32))
        red_ps = [ctx.enter_context(nc.psum_tensor(f"r0_red{i}", [P, HALF], FP32)) for i in range(2)]
        lg_ps = ctx.enter_context(nc.psum_tensor("r0_lg", [P, HALF], FP32))
        sT_ps = [ctx.enter_context(nc.psum_tensor(f"r0_sT{i}", [P, HALF], FP32)) for i in range(2)]
        b2_ps = [ctx.enter_context(nc.psum_tensor(f"r0_b2{i}", [P, HALF], FP32)) for i in range(2)]
        chain = ctx.enter_context(nc.semaphore("r0_chain"))
        squared = ctx.enter_context(nc.semaphore("r0_squared"))
        rooted = ctx.enter_context(nc.semaphore("r0_rooted"))
        wgn_ready = ctx.enter_context(nc.semaphore("r0_wgn_ready"))
        turned = ctx.enter_context(nc.semaphore("r0_turned"))
        red_done = ctx.enter_context(nc.semaphore("r0_red_done"))
        evacuated = ctx.enter_context(nc.semaphore("r0_evacuated"))
        logits_done = ctx.enter_context(nc.semaphore("r0_logits_done"))
        shifted = ctx.enter_context(nc.semaphore("r0_shifted"))
        exped = ctx.enter_context(nc.semaphore("r0_exped"))
        scored = ctx.enter_context(nc.semaphore("r0_scored"))
        sT_done = ctx.enter_context(nc.semaphore("r0_sT_done"))
        sT_copied = ctx.enter_context(nc.semaphore("r0_sT_copied"))
        b2_done = ctx.enter_context(nc.semaphore("r0_b2_done"))
        block = ctx.enter_context(nc.Block())
        col = lambda t: slice((t % 4) * P, (t % 4 + 1) * P)

        @block.vector
        def _(dve):
            n = [0]

            def link(instruction):
                n[0] += 1
                instruction.then_inc(chain, 1)
                dve.wait_ge(chain, n[0])

            link(nc.vector.tensor_tensor(sq[:], wg[:], wg[:], ALU.mult))
            nc.vector.reduce_sum(ss[:], sq[:], AX).then_inc(squared, 1)
            dve.wait_ge(rooted, 1)
            link(nc.vector.tensor_scalar(ss[:], ss[:], 1e-4, None, ALU.max))
            link(nc.vector.reciprocal(ss[:], ss[:]))
            nc.vector.tensor_scalar(wgn[:], wg[:], ss[:], None, ALU.mult).then_inc(wgn_ready, 1)
            dve.wait_ge(turned, 1)
            nc.vector.tensor_copy(wgnT[:], wT_ps[0:G, 0:E]).then_inc(evacuated, 1)
            for i in range(2):
                dve.wait_ge(red_done, i + 1)
                nc.vector.tensor_copy(redT[:, i * HALF:(i + 1) * HALF], red_ps[i][0:G, :]).then_inc(evacuated, 1)
            dve.wait_ge(logits_done, 1)
            link(nc.vector.tensor_copy(logits[:], lg_ps[:, 0:TT * E].rearrange("p (t e) -> p t e", e=E)))
            link(nc.vector.reduce_max(top[:], logits[:], AX))
            nc.vector.tensor_tensor(ex[:], logits[:], top[:].unsqueeze(2).to_broadcast([P, TT, E]),
                                    ALU.subtract).then_inc(shifted, 1)
            one_hot_first_max(nc, link, logits, peak, rank8, value, hot, E)
            dve.wait_ge(exped, 1)
            link(nc.vector.reduce_sum(score[:], ex[:], AX))
            link(nc.vector.reciprocal(score[:], score[:]))
            link(nc.vector.tensor_tensor(hot[:], hot[:], score[:].unsqueeze(2).to_broadcast([P, TT, E]), ALU.mult))
            nc.vector.tensor_scalar(gates[:, 0:E * TT].rearrange("p (e t) -> p t e", t=TT), hot[:], 1.0 / MOE_SCALE,
                                    None, ALU.mult).then_inc(scored, 1)
            for i in range(2):
                dve.wait_ge(sT_done, i + 1)
                nc.vector.tensor_copy(scoreT[:, i * HALF:(i + 1) * HALF], sT_ps[i][0:E, :]).then_inc(sT_copied, 1)
            for t in range(TT):
                dve.wait_ge(b2_done, 4 * (t // 4 + 1))
                nc.vector.tensor_tensor(x_res[:, t, :], x_res[:, t, :], b2_ps[t // 4][:, col(t)], ALU.add)

        @block.scalar
        def _(act):
            act.wait_ge(squared, 1)
            nc.scalar.activation(ss[:], ss[:], ACT.Sqrt).then_inc(rooted, 1)
            act.wait_ge(shifted, 1)
            nc.scalar.activation(ex[:], ex[:], ACT.Exp).then_inc(exped, 1)

        @block.tensor
        def _(pe):
            pe.wait_ge(wgn_ready, 1)
            nc.tensor.transpose(wT_ps[0:G, 0:E], wgn[:], ident[0:E, 0:E]).then_inc(turned, 1)
            for i in range(2):
                nc.tensor.matmul(red_ps[i][0:G, :], w_red[:], xT[:, i * HALF:(i + 1) * HALF],
                                 start=True, stop=True).then_inc(red_done, 1)
            pe.wait_ge(evacuated, 3)
            for t in range(TT):
                last = nc.tensor.matmul(lg_ps[:, t * E:(t + 1) * E], redT[:, t * P:(t + 1) * P], wgnT[:],
                                        start=True, stop=True)
            last.then_inc(logits_done, 1)
            pe.wait_ge(scored, 1)
            for t in range(TT):
                last = nc.tensor.transpose(sT_ps[t // 4][0:E, col(t)], hot[:, t, :], ident[:])
                if t % 4 == 3:
                    last.then_inc(sT_done, 1)
            for t in range(TT):
                pe.wait_ge(sT_copied, t // 4 + 1)
                nc.tensor.matmul(b2_ps[t // 4][:, col(t)], scoreT[:, t * P:(t + 1) * P], b2[:],
                                 start=True, stop=True).then_inc(b2_done, 1)


def l1_router_block(nc, xT, wg, rank8, gates):
    E = 8
    with ExitStack() as ctx:
        sb = lambda n, s: ctx.enter_context(nc.sbuf_tensor(f"r1_{n}", s, FP32))
        logits, value, hot, peak = sb("logits", [P, TT, E]), sb("value", [P, TT, E]), sb("hot", [P, TT, E]), sb("peak", [P, TT])
        lg_ps = ctx.enter_context(nc.psum_tensor("r1_lg", [P, HALF], FP32))
        chain = ctx.enter_context(nc.semaphore("r1_chain"))
        logits_done = ctx.enter_context(nc.semaphore("r1_logits_done"))
        block = ctx.enter_context(nc.Block())

        @block.tensor
        def _(pe):
            for t in range(TT):
                last = nc.tensor.matmul(lg_ps[:, t * E:(t + 1) * E], xT[:, t * P:(t + 1) * P], wg[:],
                                        start=True, stop=True)
            last.then_inc(logits_done, 1)

        @block.vector
        def _(dve):
            n = [0]

            def link(instruction):
                n[0] += 1
                instruction.then_inc(chain, 1)
                dve.wait_ge(chain, n[0])

            nc.vector.memset(gates[:, 0:TT], 1.0 / MOE_SCALE)
            dve.wait_ge(logits_done, 1)
            link(nc.vector.tensor_copy(logits[:], lg_ps[:, 0:TT * E].rearrange("p (t e) -> p t e", e=E)))
            one_hot_first_max(nc, link, logits, peak, rank8, value, hot, E)
            nc.vector.tensor_scalar(gates[:, TT:(E + 1) * TT].rearrange("p (e t) -> p t e", t=TT), hot[:],
                                    1.0 / MOE_SCALE, None, ALU.mult)


def q_block(nc, xTh, xTl, wqT, bq8, q_dram):
    with ExitStack() as ctx:
        sb = lambda n, s, dt: ctx.enter_context(nc.sbuf_tensor(f"q_{n}", s, dt))
        wh, wl = sb("wh", [P, HEADS * DK], FP16), sb("wl", [P, HEADS * DK], FP16)
        qh, ql = sb("qh", [P, 2, TOK], FP16), sb("ql", [P, 2, TOK], FP16)
        ps = [ctx.enter_context(nc.psum_tensor(f"q_ps{i}", [P, HALF], FP32)) for i in range(2)]
        whi, wsplit, full = (ctx.enter_context(nc.semaphore(f"q_{n}")) for n in ("whi", "wsplit", "full"))
        hi_done, lo_done, stored = (ctx.enter_context(nc.semaphore(f"q_{n}")) for n in ("hi_done", "lo_done", "stored"))
        block = ctx.enter_context(nc.Block())

        @block.scalar
        def _(act):
            nc.scalar.activation(wh[:], wqT[:], ACT.Copy, scale=WQ_SCALE).then_inc(whi, 1)
            for p in range(PAIRS):
                for i in range(2):
                    act.wait_ge(full, 2 * p + i + 1)
                    if p >= 2 and i == 0:
                        act.wait_ge(stored, 32 * (p - 1))
                    nc.scalar.activation(qh[:, p % 2, i * HALF:(i + 1) * HALF], ps[i][:], ACT.Identity,
                                         bias=bq8[:, p:p + 1]).then_inc(hi_done, 1)

        @block.vector
        def _(dve):
            dve.wait_ge(whi, 1)
            split_lo(nc.vector, wl[:], wqT[:], WQ_SCALE, wh[:]).then_inc(wsplit, 1)
            for p in range(PAIRS):
                for i in range(2):
                    dve.wait_ge(hi_done, 2 * p + i + 1)
                    cols = slice(i * HALF, (i + 1) * HALF)
                    nc.vector.scalar_tensor_tensor(out=ql[:, p % 2, cols], in0=ps[i][:], scalar=bq8[:, p:p + 1],
                                                   in1=qh[:, p % 2, cols], op0=ALU.add,
                                                   op1=ALU.subtract).then_inc(lo_done, 1)

        @block.tensor
        def _(pe):
            pe.wait_ge(wsplit, 1)
            for p in range(PAIRS):
                w = slice(p * P, (p + 1) * P)
                for i in range(2):
                    x = slice(i * HALF, (i + 1) * HALF)
                    if p:
                        pe.wait_ge(lo_done, 2 * p + i - 1)
                    nc.tensor.matmul(ps[i][:], wh[:, w], xTh[:, x], start=True, stop=False)
                    nc.tensor.matmul(ps[i][:], wh[:, w], xTl[:, x], start=False, stop=False)
                    nc.tensor.matmul(ps[i][:], wl[:, w], xTh[:, x], start=False, stop=True).then_inc(full, 1)

        @block.sync
        def _(sp):
            for p in range(PAIRS):
                sp.wait_ge(lo_done, 2 * p + 2)
                sp.dma_start(q_dram[p, 0], qh[:, p % 2, :]).then_inc(stored, 16)
                sp.dma_start(q_dram[p, 1], ql[:, p % 2, :]).then_inc(stored, 16)
                sp.wait_ge(stored, 32 * (p + 1))


def wo_block(nc, x_res, ctx_dram, woT, ident):
    EC = HEADS * DK // P
    with ExitStack() as ctx:
        sb = lambda n, s, dt: ctx.enter_context(nc.sbuf_tensor(f"wo_{n}", s, dt))
        rows = sb("rows", [P, TT, HEADS * DK], FP32)
        turned_sb = sb("turned", [P, 2, EC * P], FP32)
        tp = [ctx.enter_context(nc.psum_tensor(f"wo_tp{i}", [P, 2 * HALF], FP32)) for i in range(2)]
        out = [ctx.enter_context(nc.psum_tensor(f"wo_out{i}", [P, P], FP32)) for i in range(2)]
        loaded = [ctx.enter_context(nc.semaphore(f"wo_loaded{i}")) for i in range(2)]
        turned, copied, product, added = (ctx.enter_context(nc.semaphore(f"wo_{n}")) for n in ("turned_s", "copied", "product", "added"))
        block = ctx.enter_context(nc.Block())

        @block.sync
        def _(sp):
            for i in range(2):
                for j in range(TT // 2):
                    sp.dma_start(rows[:, i * 4 + j, :].rearrange("p (h d) -> p h d", d=DK),
                                 ctx_dram[:, i, :, j, :].rearrange("h p d -> p h d")).then_inc(loaded[i], 16)

        @block.tensor
        def _(pe):
            def turn(t):
                if t % 4 == 0:
                    pe.wait_ge(loaded[t // 4], 64)
                if t >= 2:
                    pe.wait_ge(copied, t - 1)
                for e in range(EC):
                    last = nc.tensor.transpose(tp[t % 2][:, e * P:(e + 1) * P], rows[:, t, e * P:(e + 1) * P], ident[:])
                last.then_inc(turned, 1)

            turn(0)
            for t in range(TT):
                if t + 1 < TT:
                    turn(t + 1)
                pe.wait_ge(copied, t + 1)
                if t >= 2:
                    pe.wait_ge(added, t - 1)
                for e in range(EC):
                    last = nc.tensor.matmul(out[t % 2][:], turned_sb[:, t % 2, e * P:(e + 1) * P],
                                            woT[:, e * P:(e + 1) * P], start=e == 0, stop=e == EC - 1)
                last.then_inc(product, 1)

        @block.scalar
        def _(act):
            for t in range(TT):
                act.wait_ge(turned, t + 1)
                if t >= 2:
                    act.wait_ge(product, t - 1)
                nc.scalar.activation(turned_sb[:, t % 2, :], tp[t % 2][:], ACT.Copy).then_inc(copied, 1)

        @block.vector
        def _(dve):
            for t in range(TT):
                dve.wait_ge(product, t + 1)
                nc.vector.tensor_tensor(x_res[:, t, :], x_res[:, t, :], out[t % 2][:], ALU.add).then_inc(added, 1)


def attention_block(nc, ctx_h, ctx_l, wkT_d, wvT_d, bk_d, bv_d, q_dram, ctx_dram, ident):
    with ExitStack() as ctx:
        sb = lambda n, s, dt=FP32: ctx.enter_context(nc.sbuf_tensor(n, s, dt))
        ps = lambda n, s: ctx.enter_context(nc.psum_tensor(n, s, FP32))
        sem = lambda n: ctx.enter_context(nc.semaphore(n))

        k_both = [sb(f"k_both{i}", [P, KPAD], FP16) for i in range(2)]
        k_step = [sb(f"k_step{i}", [P, KPAD], FP16) for i in range(2)]
        k_hi, k_lo = sb("k_hi", [P, KPAD], FP16), sb("k_lo", [P, KPAD], FP16)
        q_both = [sb(f"q_both{i}", [P, TOK], FP16) for i in range(2)]
        q_step = [sb(f"q_step{i}", [P, TOK], FP16) for i in range(2)]
        v_sb = [sb(f"v{i}", [P, KT * V_W], FP16) for i in range(2)]
        wk_h, wk_l, wv_h, wv_l = (sb(n, [P, HEADS * DK], FP16) for n in ("wk_h", "wk_l", "wv_h", "wv_l"))
        bk8, bv_bc = sb("bk8", [P, PAIRS]), sb("bv_bc", [P, HEADS * DK])
        prob = sb("prob", [P, 2, 2 * HALF])
        prob_h, prob_l = sb("prob_h", [P, SLOTS * 2 * HALF], FP16), sb("prob_l", [P, SLOTS * 2 * HALF], FP16)
        chunk_max, row_max = sb("chunk_max", [P, 4 * CHUNKS]), sb("row_max", [P, 4])
        max_diag, ones = sb("max_diag", [P, 4, P]), sb("ones", [P, P])
        denom, rests, out_sb = sb("denom", [P, 4]), sb("rests", [P, 4, DK]), sb("out_sb", [P, 4, DK])

        score = [ps(f"score{i}", [P, 2 * HALF]) for i in range(2)]
        pv = ps("pv", [P, 2, HALF])
        aux = [ps(f"aux{i}", [P, HALF]) for i in range(2)]

        loaded_w, w_hi, w_split, consts = sem("loaded_w"), sem("w_hi"), sem("w_split"), sem("consts")
        head_loaded = [sem("head_a_loaded"), sem("head_b_loaded")]
        score_full, exp_done, cast_done = sem("score_full"), sem("exp_done"), sem("cast_done")
        rest_pool, rest_dve, pv_done = sem("rest_pool"), sem("rest_dve"), sem("pv_done")
        aux_full = [sem("aux_full0"), sem("aux_full1")]
        aux_free = [sem("aux_free0"), sem("aux_free1")]
        hi_done, k_padded, zeroed = sem("hi_done"), sem("k_padded"), sem("zeroed")
        diag_ready, pv_free, out_ready, stored = sem("diag_ready"), sem("pv_free"), sem("out_ready"), sem("out_stored")
        shift_chain, out_chain = sem("shift_chain"), sem("out_chain")
        act_passed, sp_passed = sem("act_passed"), sem("sp_passed")
        block = ctx.enter_context(nc.Block())

        WORK = ("v", "k", "v", None)
        LOADS = 6
        CONSTS = 2
        PRO_AUX0, PRO_AUX1 = 2 * CHUNKS + 2 * CHUNKS, 2 * CHUNKS + 1

        def stage_no(p, t):
            return 4 * p + t

        def aux_count(bank, p, t, last):
            work = lambda u: CHUNKS if WORK[u] and not (last and u) else 0
            if bank:
                return PRO_AUX1 + (2 * CHUNKS + 1) * (4 * p + t)
            before = sum(2 * CHUNKS + work(u) for u in range(t))
            return PRO_AUX0 + (8 * CHUNKS + 3 * CHUNKS) * p + before

        def has_work(t, last):
            return WORK[t] if not (last and t) else None

        def has_max(t, last):
            return not (last and t == 3)

        def hi_count(p, t, last):
            return 2 * CHUNKS + 3 * CHUNKS * p + sum(CHUNKS for u in range(t) if has_work(u, last))

        def width(c):
            return P * chunk_tiles(isinstance(c, int) and c == CHUNKS - 1)

        def step_tiles(g):
            return 1 if isinstance(g, int) and g == STEPS - 1 else 2

        def chunks(engine, body):
            body(0, 0)
            body(1, 1)
            with engine.Fori(0, (CHUNKS - 3) // 2) as m:
                body(2 * Linear(m) + 2, 0)
                body(2 * Linear(m) + 3, 1)
            body(CHUNKS - 1, 0)

        def stages(engine, stage):
            stage(0, 0, True, False)
            with engine.Fori(0, PAIRS - 1) as pair:
                p = Linear(pair)
                for t in (1, 2, 3):
                    stage(p, t, False, False)
                stage(p + 1, 0, False, False)
            for t in (1, 2, 3):
                stage(PAIRS - 1, t, False, True)

        def slot(odd, t, k):
            return (((odd + t) % 2) * 2 + k) * 2 * HALF

        @block.sync
        def _(sp):
            def load_head(p, b):
                rows = slice(b * DK, (b + 1) * DK)
                done = head_loaded[b]
                sp.dma_start(k_both[b][0:DK, :], k_hi[rows, :]).then_inc(done, 16)
                sp.dma_start(k_both[b][DK:P, :], k_lo[rows, :]).then_inc(done, 16)
                sp.dma_start(k_step[b][0:DK, :], k_hi[rows, :]).then_inc(done, 16)
                q = q_dram[ds(p, 1), :, rows, :].rearrange("o c r n -> (o c) r n")
                sp.dma_start(q_both[b][0:DK, :], q[0]).then_inc(done, 16)
                sp.dma_start(q_both[b][DK:P, :], q[0]).then_inc(done, 16)
                sp.dma_start(q_step[b][0:DK, :], q[1]).then_inc(done, 16)

            def store(p, t):
                wait(sp, out_ready, stage_no(p, t) + 1)
                head = 2 * p + t // 2
                sp.dma_start(ctx_dram[ds(head, 1), t % 2].rearrange("o p j d -> (o p) j d"),
                             out_sb[:]).then_inc(stored, 16)

            def stage(p, t, first, last):
                if t in (0, 2) and not (last and t):
                    b = 1 if t == 0 else 0
                    wait(sp, score_full, STEPS * stage_no(p, t) + 1)
                    passed(sp, sp_passed)
                    wait(sp, k_padded, p + (1 if t == 0 else 2))
                    passed(sp, sp_passed)
                    load_head(p if t == 0 else p + 1, b)
                if t:
                    store(p, t - 1)
                elif not first:
                    store(p - 1, 3)

            sp.dma_start(prob[:, 0, :], wkT_d).then_inc(loaded_w, 16)
            sp.dma_start(prob[:, 1, :], wvT_d).then_inc(loaded_w, 16)
            sp.dma_start(bk8[:], bk_d).then_inc(loaded_w, 16)
            sp.dma_start(bv_bc[:], bv_d.to_broadcast([P, HEADS * DK])).then_inc(loaded_w, 16)
            wait(sp, k_padded, 1)
            load_head(0, 0)
            stages(sp, stage)
            store(PAIRS - 1, 3)
            wait(sp, stored, 16 * 4 * PAIRS)

        @block.tensor
        def _(pe):
            def scores(p, t, c, k, last):
                g = 2 * c + k
                n = STEPS * stage_no(p, t) + g
                b = t // 2
                if isinstance(g, int) and g == 0:
                    wait(pe, aux_free[1], aux_count(1, p, t, last))
                wait(pe, exp_done, n - 1)
                q = slice((t % 2) * HALF, (t % 2 + 1) * HALF)
                for i in range(step_tiles(g)):
                    keys = ds((2 * g + i) * P, P)
                    out = score[k][:, i * HALF:(i + 1) * HALF]
                    nc.tensor.matmul(out, k_both[b][:, keys], q_both[b][:, q], start=True, stop=False)
                    done = nc.tensor.matmul(out, k_step[b][:, keys], q_step[b][:, q], start=False, stop=True)
                done.then_inc(score_full, 1)

            def maxima(p, t, c, k, base, head_ready=None):
                b = t // 2
                for i in range(2):
                    tile = (t % 2) * 4 + 2 * k + i
                    wait(pe, aux_free[i], base[i])
                    nc.tensor.matmul(aux[i][:, 0:width(c)], q_both[b][:, tile * P:(tile + 1) * P],
                                     k_both[b][:, ds(c * HALF, width(c))],
                                     start=True, stop=True).then_inc(aux_full[i], 1)

            def project_k(p, c, base):
                wait(pe, aux_free[0], base)
                w, keys = ds(p * P, P), ds(c * HALF, width(c))
                out = aux[0][:, 0:width(c)]
                nc.tensor.matmul(out, wk_h[:, w], ctx_h[:, keys], start=True, stop=False)
                nc.tensor.matmul(out, wk_h[:, w], ctx_l[:, keys], start=False, stop=False)
                nc.tensor.matmul(out, wk_l[:, w], ctx_h[:, keys], start=False, stop=True).then_inc(aux_full[0], 1)

            def project_v(head, c, base):
                wait(pe, aux_free[0], base)
                w = ds(head * DK, DK)
                for i in range(width(c) // P):
                    keys = ds(c * HALF + i * P, P)
                    out = aux[0][:, i * DK:(i + 1) * DK]
                    nc.tensor.matmul(out, ctx_h[:, keys], wv_h[:, w], start=True, stop=False)
                    nc.tensor.matmul(out, ctx_h[:, keys], wv_l[:, w], start=False, stop=False)
                    last = nc.tensor.matmul(out, ctx_l[:, keys], wv_h[:, w], start=False, stop=True)
                last.then_inc(aux_full[0], 1)

            def project(p, t, c, base):
                if WORK[t] == "k":
                    project_k(p + 1, c, base)
                else:
                    project_v(2 * p + (1 if t == 0 else 2), c, base)

            def shift(s, base):
                wait(pe, diag_ready, s + 1)
                wait(pe, aux_free[1], base)
                nc.tensor.matmul(aux[1][:], ones[:], max_diag[:].rearrange("p i q -> p (i q)"),
                                 start=True, stop=True).then_inc(aux_full[1], 1)

            def weigh(p, t, c, odd, k, last, tiles=(0, 1)):
                g = 2 * c + k
                s = stage_no(p, t)
                n = STEPS * s + g
                b = t // 2
                if isinstance(g, int) and g == 0:
                    wait(pe, pv_free, s)
                    wait(pe, aux_free[0], aux_count(0, p, t, last))
                if 0 in tiles:
                    wait(pe, rest_pool, n + 1)
                    if k == 1 and not (isinstance(c, int) and c == CHUNKS - 1):
                        wait(pe, rest_dve, (CHUNKS - 1) * s + c + 1)
                count = step_tiles(g)
                for i in tiles:
                    if i >= count:
                        continue
                    for j in range(4):
                        cols = ds(slot(odd, t, k) + i * HALF + j * P, P)
                        out = pv[:, j // 2, (j % 2) * V_W:(j % 2 + 1) * V_W]
                        v = (2 * g + i) * V_W
                        start = isinstance(g, int) and g == 0 and i == 0 and j % 2 == 0
                        stop = isinstance(g, int) and g == STEPS - 1
                        nc.tensor.matmul(out, prob_h[:, cols], v_sb[b][:, ds(v, V_W)],
                                         start=start, stop=False, skip_group_check=True)
                        done = nc.tensor.matmul(out[:, 0:DK + 1], prob_l[:, cols], v_sb[b][:, ds(v, DK + 1)],
                                                start=False, stop=stop, skip_group_check=True)
                if tiles[-1] == count - 1 or len(tiles) == 2:
                    done.then_inc(pv_done, 1)

            def stage(p, t, first, last):
                work, find = has_work(t, last), has_max(t, last)
                before = (p, t - 1) if t else (p - 1, 3)
                after = (p, t + 1) if t < 3 else (p + 1, 0)
                a0, a1 = aux_count(0, p, t, last), aux_count(1, p, t, last)
                per0 = 2 + (1 if work else 0)
                if find and t in (1, 3):
                    wait(pe, head_loaded[after[1] // 2], 16 * LOADS * (after[0] + 1))

                def chunk(c, odd):
                    opening = isinstance(c, int) and c == 0
                    closing = isinstance(c, int) and c == CHUNKS - 1
                    mx0 = lambda: find and maxima(*after, c, 0, (a0 + per0 * c, a1 + 2 * c))
                    pr = lambda: work and project(p, t, c, a0 + per0 * c + (1 if find else 0))
                    mx1 = lambda: find and maxima(*after, c, 1, (a0 + per0 * c + per0 - 1, a1 + 2 * c + 1))
                    if opening:
                        if not first:
                            weigh(*before, CHUNKS - 1, 0, 0, False)
                        scores(p, t, c, 0, last)
                        mx0()
                        if not first:
                            weigh(*before, CHUNKS - 1, 0, 1, False)
                        pr()
                        scores(p, t, c, 1, last)
                        mx1()
                        return
                    scores(p, t, c, 0, last)
                    mx0()
                    weigh(p, t, c - 1, 1 - odd, 0, last, (0,))
                    pr()
                    if closing:
                        mx1()
                    weigh(p, t, c - 1, 1 - odd, 0, last, (1,))
                    scores(p, t, c, 1, last)
                    if not closing:
                        mx1()
                    weigh(p, t, c - 1, 1 - odd, 1, last)

                chunks(pe, chunk)
                if find:
                    shift(stage_no(p, t) + 1, a1 + 2 * CHUNKS)

            wait(pe, w_split, 2)
            n0 = n1 = 0
            for c in range(CHUNKS):
                project_k(0, c, n0)
                project_v(0, c, n0 + 1)
                n0 += 2
            wait(pe, head_loaded[0], 16 * LOADS)
            for c in range(CHUNKS):
                for k in range(2):
                    maxima(0, 0, c, k, (n0, n1))
                    n0 += 1
                    n1 += 1
            wait(pe, consts, CONSTS)
            shift(0, n1)
            stages(pe, stage)
            for k in range(2):
                weigh(PAIRS - 1, 3, CHUNKS - 1, 0, k, True)

        @block.scalar
        def _(act):
            def probabilities(p, t, c, odd, k):
                g = 2 * c + k
                s = stage_no(p, t)
                n = STEPS * s + g
                w = step_tiles(g) * HALF
                wait(act, score_full, n + 1)
                wait(act, rest_pool, n - 1)
                if k == 1 and not (isinstance(c, int) and c == 0):
                    wait(act, rest_dve, (CHUNKS - 1) * s + c)
                nc.scalar.activation(prob[:, k, 0:w], score[k][:, 0:w], ACT.Exp, scale=EXP_SCALE).then_inc(exp_done, 1)
                wait(act, exp_done, n + 1)
                wait(act, pv_done, n - SLOTS + 1)
                nc.scalar.activation(prob_h[:, ds(slot(odd, t, k), w)], prob[:, k, 0:w],
                                     ACT.Copy).then_inc(cast_done, 1)

            def high_part(kind, p, head, c, base):
                wait(act, aux_full[0], base + 1)
                passed(act, act_passed)
                w = width(c)
                if kind == "k":
                    nc.scalar.activation(k_hi[:, ds(c * HALF, w)], aux[0][:, 0:w], ACT.Identity,
                                         bias=bk8[:, ds(p, 1)]).then_inc(hi_done, 1)
                else:
                    n = w // P
                    v = v_sb[head][:, ds(c * CHUNK_TILES * V_W, n * V_W)].rearrange("p (i w) -> p i w", w=V_W)
                    nc.scalar.activation(v[:, :, 0:DK], aux[0][:, 0:n * DK].rearrange("p (i w) -> p i w", w=DK),
                                         ACT.Copy).then_inc(hi_done, 1)

            def stage(p, t, first, last):
                work = has_work(t, last)
                a0 = aux_count(0, p, t, last)
                find = 1 if has_max(t, last) else 0
                if work == "k":
                    wait(act, head_loaded[1], 16 * LOADS * (p + 1))

                def chunk(c, odd):
                    probabilities(p, t, c, odd, 0)
                    if work:
                        high_part(work, p + 1, 1 if t == 0 else 0, c, a0 + 3 * c + find)
                    probabilities(p, t, c, odd, 1)

                chunks(act, chunk)

            wait(act, loaded_w, 64)
            nc.scalar.activation(wk_h[:], prob[:, 0, :], ACT.Copy, scale=W_SCALE).then_inc(w_hi, 1)
            nc.scalar.activation(wv_h[:], prob[:, 1, :], ACT.Copy, scale=W_SCALE).then_inc(w_hi, 1)
            for c in range(CHUNKS):
                if c == 0:
                    wait(act, consts, CONSTS)
                high_part("k", 0, None, c, 2 * c)
                high_part("v", None, 0, c, 2 * c + 1)
            stages(act, stage)

        @block.gpsimd
        def _(pool):
            nc.gpsimd.memset(ones[:], 1.0).then_inc(consts, 1)

            def stage(p, t, first, last):
                def chunk(c, odd):
                    for k in range(2):
                        g = 2 * c + k
                        n = STEPS * stage_no(p, t) + g
                        w = 2 * HALF if k == 0 else HALF
                        wait(pool, cast_done, n + 1)
                        hl = ds(slot(odd, t, k), w)
                        nc.gpsimd.tensor_tensor(prob_l[:, hl], prob[:, k, 0:w], prob_h[:, hl],
                                                ALU.subtract).then_inc(rest_pool, 1)

                chunks(pool, chunk)

            stages(pool, stage)

        @block.vector
        def _(dve):
            def rest_share(p, t, c, odd):
                s = stage_no(p, t)
                wait(dve, cast_done, STEPS * s + 2 * c + 2)
                hl = ds(slot(odd, t, 1) + HALF, HALF)
                nc.vector.tensor_tensor(prob_l[:, hl], prob[:, 1, HALF:], prob_h[:, hl],
                                        ALU.subtract).then_inc(rest_dve, 1)

            def maxima(c, k, base):
                for i in range(2):
                    wait(dve, aux_full[i], base[i] + 1)
                    nc.vector.reduce_max(chunk_max[:, ds((2 * k + i) * CHUNKS + c, 1)],
                                         aux[i][:, 0:width(c)], AX).then_inc(aux_free[i], 1)

            def rest_part(kind, p, head, c, his):
                wait(dve, hi_done, his + 1)
                w = width(c)
                if kind == "k":
                    keys = ds(c * HALF, w)
                    nc.vector.scalar_tensor_tensor(out=k_lo[:, keys], in0=aux[0][:, 0:w], scalar=bk8[:, ds(p, 1)],
                                                   in1=k_hi[:, keys], op0=ALU.add, op1=ALU.subtract).then_inc(aux_free[0], 1)
                else:
                    n = w // P
                    v = v_sb[head][:, ds(c * CHUNK_TILES * V_W, n * V_W)].rearrange("p (i w) -> p i w", w=V_W)
                    nc.vector.tensor_tensor(v[:, :, DK + 1:V_W], aux[0][:, 0:n * DK].rearrange("p (i w) -> p i w", w=DK),
                                            v[:, :, 0:DK], ALU.subtract).then_inc(aux_free[0], 1)

            def pad_keys(n):
                wait(dve, aux_free[0], n)
                for m, tile in enumerate((k_hi, k_lo)):
                    last = nc.vector.tensor_copy(tile[:, KEYS:KPAD], tile[:, KEYS - 1:KEYS].to_broadcast([P, KPAD - KEYS]))
                last.then_inc(k_padded, 1)

            def row_shift(s, t, n1):
                wait(dve, aux_free[1], n1)
                nc.vector.reduce_max(row_max[:], chunk_max[:].rearrange("p (i c) -> p i c", c=CHUNKS),
                                     AX).then_inc(shift_chain, 1)
                wait(dve, shift_chain, 2 * s + 1)
                nc.vector.tensor_tensor(max_diag[:], ident[:].unsqueeze(1).to_broadcast([P, 4, P]),
                                        row_max[:].unsqueeze(2).to_broadcast([P, 4, P]), ALU.mult).then_inc(diag_ready, 1)
                wait(dve, aux_full[1], n1 + 1)
                q = slice((t % 2) * HALF, (t % 2 + 1) * HALF)
                both, rest = q_step[t // 2][DK:P, q], q_step[t // 2][DK + 32:P, q]
                nc.vector.tensor_scalar(both, aux[1][DK:P, :], -1.0 / MAX_STEP, None, ALU.mult).then_inc(shift_chain, 1)
                wait(dve, shift_chain, 2 * s + 2)
                nc.vector.scalar_tensor_tensor(out=rest, in0=rest, scalar=MAX_STEP, in1=aux[1][DK + 32:P, :],
                                               op0=ALU.mult, op1=ALU.add).then_inc(aux_free[1], 1)

            def evacuate(p, t):
                s = stage_no(p, t)
                head = 2 * p + t // 2
                acc = pv[:, :, 0:2 * V_W].rearrange("p b (j w) -> p b j w", w=V_W)
                four = lambda ap: ap.rearrange("p (b j) w -> p b j w", j=2)
                wait(dve, pv_done, STEPS * (s + 1))
                nc.vector.reciprocal(denom[:].rearrange("p (b j) -> p b j", j=2), acc[:, :, :, DK])
                nc.vector.tensor_copy(four(rests[:]), acc[:, :, :, DK + 1:V_W]).then_inc(out_chain, 1)
                wait(dve, out_chain, 2 * s + 1)
                nc.vector.tensor_tensor(four(rests[:]), acc[:, :, :, 0:DK], four(rests[:]), ALU.add).then_inc(pv_free, 1)
                wait(dve, pv_free, s + 1)
                nc.vector.tensor_tensor(rests[:], rests[:], denom[:].unsqueeze(2).to_broadcast([P, 4, DK]),
                                        ALU.mult).then_inc(out_chain, 1)
                wait(dve, out_chain, 2 * s + 2)
                bv = bv_bc[:, ds(head * DK, DK)].unsqueeze(1).to_broadcast([P, 4, DK])
                nc.vector.tensor_tensor(out_sb[:], rests[:], bv, ALU.add).then_inc(out_ready, 1)

            def stage(p, t, first, last):
                work, find = has_work(t, last), has_max(t, last)
                before = (p, t - 1) if t else (p - 1, 3)
                a0, a1 = aux_count(0, p, t, last), aux_count(1, p, t, last)
                his = hi_count(p, t, last)
                per0 = 2 + (1 if work else 0)
                s = stage_no(p, t)

                def chunk(c, odd):
                    opening = isinstance(c, int) and c == 0
                    closing = isinstance(c, int) and c == CHUNKS - 1
                    if find:
                        maxima(c, 0, (a0 + per0 * c, a1 + 2 * c))
                    if not opening:
                        rest_share(p, t, c - 1, 1 - odd)
                    elif not first:
                        evacuate(*before)
                    if work:
                        rest_part(work, p + 1, 1 if t == 0 else 0, c, his + c)
                        if work == "k" and closing:
                            pad_keys(a0 + per0 * c + 2)
                    if find:
                        maxima(c, 1, (a0 + per0 * c + per0 - 1, a1 + 2 * c + 1))

                chunks(dve, chunk)
                if find:
                    row_shift(s + 1, (t + 1) % 4, a1 + 2 * CHUNKS)
                wait(dve, stored, 16 * s)

            for b in range(2):
                nc.vector.memset(k_step[b][DK:P, :], 0.0).then_inc(zeroed, 1)
                nc.vector.memset(v_sb[b][:, (KT - 1) * V_W + DK:(KT - 1) * V_W + DK + 1], 0.0).then_inc(zeroed, 1)
            wait(dve, zeroed, 4)
            for b in range(2):
                nc.vector.memset(k_step[b][DK:DK + 1, :], MAX_STEP)
                nc.vector.memset(k_step[b][DK + 32:DK + 33, :], -1.0)
                column = v_sb[b][:].rearrange("p (i w) -> p i w", w=V_W)[:, :, DK:DK + 1]
                nc.vector.memset(column[:, 0:KT - 1, :], QKV_SCALE)
                nc.vector.memset(column[0:KEYS - (KT - 1) * P, KT - 1:KT, :], QKV_SCALE)
            wait(dve, loaded_w, 64)
            nc.vector.tensor_scalar(bk8[:], bk8[:], QKV_SCALE, None, ALU.mult).then_inc(consts, 1)
            for n, (lo, hi) in enumerate(((wk_l, wk_h), (wv_l, wv_h))):
                wait(dve, w_hi, n + 1)
                split_lo(nc.vector, lo[:], prob[:, n, :], W_SCALE, hi[:]).then_inc(w_split, 1)
            for c in range(CHUNKS):
                rest_part("k", 0, None, c, 2 * c)
                if c == CHUNKS - 1:
                    pad_keys(2 * c + 1)
                rest_part("v", None, 0, c, 2 * c + 1)
            for c in range(CHUNKS):
                for k in range(2):
                    maxima(c, k, (2 * CHUNKS + 2 * c + k, 2 * c + k))
            row_shift(0, 0, 2 * CHUNKS)
            stages(dve, stage)
            evacuate(PAIRS - 1, 3)


def build(nc, x_tok, ctx_t, w1T_d, w2T_d, b_d, w_red_d, wg0_d, up0, b1_d, down0, b2_d,
          wqT_d, bq8_d, wkT_d, bk8_d, wvT_d, bv_d, woT_d, up1, gate1, down1, wg1_d, out_d,
          parts=("l0", "attn", "l1")):
    q_dram = nc.dram_tensor("q_parts", [PAIRS, 2, P, TOK], FP16, kind="Internal").ap()
    ctx_dram = nc.dram_tensor("attn_out", [HEADS, 2, P, TT // 2, DK], FP32, kind="Internal").ap()
    with ExitStack() as ctx:
        sb = lambda n, s, dt=FP32: ctx.enter_context(nc.sbuf_tensor(n, s, dt))
        x_res = sb("x_res", [P, TT, D])
        ident = sb("ident", [P, P])
        rank8 = sb("rank8", [P, 8])
        identity_block(nc, ident, rank8)
        with ExitStack() as held:
            hb = lambda n, s, dt=FP32: held.enter_context(nc.sbuf_tensor(n, s, dt))
            ctx_h, ctx_l = hb("ctx_h", [P, KPAD], FP16), hb("ctx_l", [P, KPAD], FP16)
            with ExitStack() as first:
                fb = lambda n, s, dt=FP32: first.enter_context(nc.sbuf_tensor(n, s, dt))
                xT, xTh, xTl = fb("l0_xT", [P, TOK]), fb("l0_xTh", [P, TOK], FP16), fb("l0_xTl", [P, TOK], FP16)
                w1T, w2T, b = fb("l0_w1T", [P, D]), fb("l0_w2T", [P, D]), fb("l0_b", [P, D])
                w_red, wg, b1, b2 = fb("w_red", [P, 16]), fb("wg0", [8, 16]), fb("b1", [P, 8 * FC]), fb("b2", [8, D])
                gates = fb("gates0", [P, 8 * TT])
                load_block(nc, "a", [(x_res[:], x_tok), (w1T[:], w1T_d), (w2T[:], w2T_d), (b[:], b_d.to_broadcast([P, D])),
                                (w_red[:], w_red_d), (wg[:], wg0_d), (b1[:], b1_d), (b2[:], b2_d)])
                layernorm_block(nc, "ln0", x_res, ident, xT, None, None)
                l0_linear_block(nc, x_res, xT, ctx_t, ctx_h, ctx_l, w1T, w2T, b)
                layernorm_block(nc, "ln1", x_res, ident, xT, xTh, xTl)
                l0_router_block(nc, x_res, xT, w_red, wg, b2, ident, rank8, gates)
                moe_block(nc, "moe0", 8, False, xTh, xTl, up0, None, down0, b1, gates, x_res)
            with ExitStack() as second:
                qb = lambda n, s, dt=FP32: second.enter_context(nc.sbuf_tensor(n, s, dt))
                xTh, xTl = qb("l1_xTh", [P, TOK], FP16), qb("l1_xTl", [P, TOK], FP16)
                wqT, bq8 = qb("wqT", [P, HEADS * DK]), qb("bq8", [P, PAIRS])
                load_block(nc, "b", [(wqT[:], wqT_d), (bq8[:], bq8_d)], scale=[(bq8, QKV_SCALE)])
                layernorm_block(nc, "ln2", x_res, ident, None, xTh, xTl)
                q_block(nc, xTh, xTl, wqT, bq8, q_dram)
            if "attn" in parts:
                attention_block(nc, ctx_h, ctx_l, wkT_d, wvT_d, bk8_d, bv_d, q_dram, ctx_dram, ident)
        with ExitStack() as third:
            tb = lambda n, s, dt=FP32: third.enter_context(nc.sbuf_tensor(n, s, dt))
            woT, wg = tb("woT", [P, HEADS * DK]), tb("wg1", [P, 8])
            xT, xTh, xTl = tb("l2_xT", [P, TOK]), tb("l2_xTh", [P, TOK], FP16), tb("l2_xTl", [P, TOK], FP16)
            gates = tb("gates1", [P, 9 * TT])
            load_block(nc, "c", [(woT[:], woT_d), (wg[:], wg1_d)])
            if "attn" in parts:
                wo_block(nc, x_res, ctx_dram, woT, ident)
            layernorm_block(nc, "ln3", x_res, ident, xT, xTh, xTl)
            l1_router_block(nc, xT, wg, rank8, gates)
            moe_block(nc, "moe1", 9, True, xTh, xTl, up1, gate1, down1, None, gates, x_res)
        store_block(nc, x_res, out_d)


def store_block(nc, x_res, out_d):
    with ExitStack() as ctx:
        stored = ctx.enter_context(nc.semaphore("stored"))
        block = ctx.enter_context(nc.Block())

        @block.sync
        def _(sp):
            sp.dma_start(out_d, x_res[:]).then_inc(stored, 16)
            sp.wait_ge(stored, 16)


def lay_out(x, ctx_1024, L0_xattn_W, L0_xattn_b, L0_ffn_w_red, L0_ffn_wg, L0_ffn_w1, L0_ffn_b1, L0_ffn_w2, L0_ffn_b2,
            L1_xattn_Wq, L1_xattn_bq, L1_xattn_Wk, L1_xattn_bk, L1_xattn_Wv, L1_xattn_bv, L1_xattn_Wo,
            L1_ffn_w1s, L1_ffn_w2s, L1_ffn_w3s, L1_ffn_W1, L1_ffn_W2, L1_ffn_W3, L1_ffn_Wg):
    import numpy as np
    up = lambda w: w.transpose(1, 0, 2).reshape(D, -1)
    down = lambda w: w.reshape(-1, FC, P, D).transpose(2, 0, 1, 3).reshape(P, -1)
    shared = lambda one, many: np.concatenate([one[None], many])
    by_pair = lambda v: v.reshape(PAIRS, P).T
    return {
        "x_tok": x.reshape(TT, P, D).transpose(1, 0, 2), "ctx_t": ctx_1024[0].T,
        "w1T": L0_xattn_W[:, :D].T, "w2T": L0_xattn_W[:, D:].T, "b": L0_xattn_b[None],
        "w_red": L0_ffn_w_red, "wg0": L0_ffn_wg, "up0": up(L0_ffn_w1),
        "b1": L0_ffn_b1.reshape(8, FC, P).transpose(2, 0, 1).reshape(P, -1), "down0": down(L0_ffn_w2), "b2": L0_ffn_b2,
        "wqT": L1_xattn_Wq.T, "bq": by_pair(L1_xattn_bq), "wkT": L1_xattn_Wk.T, "bk": by_pair(L1_xattn_bk),
        "wvT": L1_xattn_Wv.T, "bv": L1_xattn_bv[None],
        "woT": L1_xattn_Wo.T.reshape(HEADS * DK // P, P, D).transpose(1, 0, 2).reshape(P, -1),
        "up1": up(shared(L1_ffn_w1s, L1_ffn_W1)), "gate1": up(shared(L1_ffn_w2s, L1_ffn_W2)),
        "down1": down(shared(L1_ffn_w3s, L1_ffn_W3)), "wg1": L1_ffn_Wg,
    }


def kernel(**inputs):
    import numpy as np
    import concourse.bacc as bacc
    from concourse.bass_utils import run_bass_kernel_spmd

    arrays = {"in_" + n: np.ascontiguousarray(a) for n, a in lay_out(**{k: np.asarray(v) for k, v in inputs.items()}).items()}
    nc = bacc.Bacc("TRN2", target_bir_lowering=False, num_devices=1)
    args = [nc.dram_tensor(n, a.shape, mybir.dt.from_np(a.dtype), kind="ExternalInput").ap() for n, a in arrays.items()]
    out = nc.dram_tensor("out", (P, TT, D), FP32, kind="ExternalOutput").ap()
    build(nc, *args, out)
    r = run_bass_kernel_spmd(nc, [arrays], core_ids=[0])
    return r.results[0]["out"].transpose(1, 0, 2).reshape(1, TOK, D)
```

```python
import concourse.bass as bass
from concourse import mybir
from contextlib import ExitStack

FP32 = mybir.dt.float32
FP16 = mybir.dt.float16
BF16 = mybir.dt.bfloat16
ALU = mybir.AluOpType
ACT = mybir.ActivationFunctionType
AX = mybir.AxisListType.X

P = 128
D = 128
TOK = 1024
TT = TOK // P
HALF = 512
KEYS = 6404
KT = -(-KEYS // P)
KPAD = KT * P
HEADS, DK = 16, 64
PAIRS = HEADS // 2
FF = 512
FC = FF // P
EPS = 1e-5

C_SCALE = 0.5
W_SCALE = 16.0
QKV_SCALE = C_SCALE * W_SCALE
WQ_SCALE = QKV_SCALE
MOE_SCALE = 16.0
EXP_SCALE = 1.0 / (QKV_SCALE * QKV_SCALE * DK ** 0.5)
MAX_STEP = 1024.0

CHUNK_TILES = 4
CHUNKS = -(-KT // CHUNK_TILES)
STEPS = -(-KT // 2)
SLOTS = 4
V_W = 2 * DK + 1


class Linear:

    def __init__(self, variable=None, terms=(), constant=0):
        self.terms = list(terms) if variable is None else [(1, variable)]
        self.constant = constant

    def __add__(self, other):
        if isinstance(other, Linear):
            terms = list(self.terms)
            for k, v in other.terms:
                same = [n for n, (_, w) in enumerate(terms) if w is v]
                if same:
                    terms[same[0]] = (terms[same[0]][0] + k, v)
                else:
                    terms.append((k, v))
            return Linear(terms=terms, constant=self.constant + other.constant)
        return Linear(terms=self.terms, constant=self.constant + other)

    def __sub__(self, other):
        return self + -other

    def __mul__(self, k):
        return Linear(terms=[(c * k, v) for c, v in self.terms], constant=self.constant * k)

    __radd__, __rmul__ = __add__, __mul__

    def value(self):
        total = self.constant
        for k, v in self.terms:
            total = v * k + total
        return total


def value(x):
    return x.value() if isinstance(x, Linear) else x


def ds(start, size):
    return bass.ds(value(start), size)


def wait(engine, semaphore, count):
    if not (isinstance(count, int) and count <= 0):
        engine.wait_ge(semaphore, value(count))


def passed(engine, semaphore):
    engine.sem_inc(semaphore, 1)


def chunk_tiles(last):
    return KT - CHUNK_TILES * (CHUNKS - 1) if last else CHUNK_TILES


def split_lo(vec, lo, src, scale, hi):
    return vec.scalar_tensor_tensor(out=lo, in0=src, scalar=scale, in1=hi, op0=ALU.mult, op1=ALU.subtract)


def layernorm_block(nc, name, x_res, ident, xT, xTh, xTl):
    with ExitStack() as ctx:
        stats = ctx.enter_context(nc.sbuf_tensor(f"{name}_stats", [P, TT, 6], FP32))
        mv = ctx.enter_context(nc.sbuf_tensor(f"{name}_mv", [P, TT, 2], FP32))
        rstd = ctx.enter_context(nc.sbuf_tensor(f"{name}_rstd", [P, TT], FP32))
        xn = ctx.enter_context(nc.sbuf_tensor(f"{name}_xn", [P, TT, D], FP32))
        tp = [ctx.enter_context(nc.psum_tensor(f"{name}_tp{i}", [P, HALF], FP32)) for i in range(2)]
        chain = ctx.enter_context(nc.semaphore(f"{name}_chain"))
        var_ready = ctx.enter_context(nc.semaphore(f"{name}_var_ready"))
        rooted = ctx.enter_context(nc.semaphore(f"{name}_rooted"))
        normed = ctx.enter_context(nc.semaphore(f"{name}_normed"))
        turned = ctx.enter_context(nc.semaphore(f"{name}_turned"))
        hi_done = ctx.enter_context(nc.semaphore(f"{name}_hi_done"))
        block = ctx.enter_context(nc.Block())

        @block.vector
        def _(dve):
            for t in range(TT):
                nc.vector.bn_stats(stats[:, t, :], x_res[:, t, :]).then_inc(chain, 1)
            dve.wait_ge(chain, TT)
            for t in range(TT):
                nc.vector.bn_aggr(mv[:, t, :], stats[:, t, :]).then_inc(chain, 1)
            dve.wait_ge(chain, 2 * TT)
            nc.vector.tensor_scalar(rstd[:], mv[:, :, 1], EPS, None, ALU.add).then_inc(var_ready, 1)
            dve.wait_ge(rooted, 1)
            nc.vector.reciprocal(rstd[:], rstd[:]).then_inc(chain, 1)
            dve.wait_ge(chain, 2 * TT + 1)
            for t in range(TT):
                nc.vector.tensor_scalar(xn[:, t, :], x_res[:, t, :], mv[:, t, 0:1], rstd[:, t:t + 1],
                                        ALU.subtract, ALU.mult).then_inc(normed, 1)
            if xTl is not None:
                for i in range(2):
                    dve.wait_ge(hi_done, i + 1)
                    split_lo(nc.vector, xTl[:, i * HALF:(i + 1) * HALF], tp[i][:], 1.0,
                             xTh[:, i * HALF:(i + 1) * HALF])

        @block.tensor
        def _(pe):
            for t in range(TT):
                pe.wait_ge(normed, t + 1)
                nc.tensor.transpose(tp[t // 4][:, (t % 4) * P:(t % 4 + 1) * P], xn[:, t, :],
                                    ident[:]).then_inc(turned, 1)

        @block.scalar
        def _(act):
            act.wait_ge(var_ready, 1)
            nc.scalar.activation(rstd[:], rstd[:], ACT.Sqrt).then_inc(rooted, 1)
            for i in range(2):
                act.wait_ge(turned, 4 * (i + 1))
                if xT is not None:
                    nc.scalar.activation(xT[:, i * HALF:(i + 1) * HALF], tp[i][:], ACT.Copy)
                if xTh is not None:
                    nc.scalar.activation(xTh[:, i * HALF:(i + 1) * HALF], tp[i][:], ACT.Copy).then_inc(hi_done, 1)


def one_hot_first_max(nc, link, logits, peak, rank, value, hot, E):
    bc = lambda ap: ap.unsqueeze(2).to_broadcast([P, TT, E])
    link(nc.vector.reduce_max(peak[:], logits[:], AX))
    link(nc.vector.tensor_tensor(hot[:], logits[:], bc(peak[:]), ALU.is_equal))
    link(nc.vector.tensor_tensor(value[:], hot[:], rank[:].unsqueeze(1).to_broadcast([P, TT, E]), ALU.mult))
    link(nc.vector.reduce_max(peak[:], value[:], AX))
    link(nc.vector.tensor_tensor(hot[:], value[:], bc(peak[:]), ALU.is_equal))



def moe_block(nc, name, E, gated, xTh, xTl, w_up, w_gate, w_down, b_up, gates, x_res):
    NW = 3 if gated else 2
    with ExitStack() as ctx:
        sb = lambda n, s, dt: ctx.enter_context(nc.sbuf_tensor(f"{name}_{n}", s, dt))
        ps = lambda n: [ctx.enter_context(nc.psum_tensor(f"{name}_{n}{i}", [P, HALF], FP32)) for i in range(2)]
        sem = lambda n: ctx.enter_context(nc.semaphore(f"{name}_{n}"))
        raw = sb("raw", [P, 2 * NW * FF], FP32)
        wh = sb("wh", [P, 2 * NW * FF], FP16)
        wl = sb("wl", [P, 2 * NW * FF], FP16)
        gelu = sb("gelu", [P, 2, HALF], FP32)
        hidden = sb("hidden", [P, 2, HALF], FP32) if gated else gelu
        hh = sb("hh", [P, 2, FC * HALF], FP16)
        hl = sb("hl", [P, 2, FC * HALF], FP16)
        up, down = ps("up"), ps("down")
        gate = ps("gate") if gated else None
        w_loaded, whi_done, w_split = sem("w_loaded"), sem("whi_done"), sem("w_split")
        up_full, gelu_done, hidden_done = sem("up_full"), sem("gelu_done"), sem("hidden_done")
        hi_done, lo_done = sem("hi_done"), sem("lo_done")
        down_full, added = sem("down_full"), sem("added")
        act_passed, sp_passed = sem("act_passed"), sem("sp_passed")
        if not gated:
            hidden_done = gelu_done
        block = ctx.enter_context(nc.Block())
        WSET = NW * FF
        DOWN = (NW - 1) * FF
        sources = [w_up, w_gate, w_down] if gated else [w_up, w_down]

        @block.sync
        def _(sp):
            def load(e):
                wait(sp, w_split, e - 1)
                for n, src in enumerate(sources):
                    sp.dma_start(raw[:, ds(value(e) % 2 * WSET + n * FF, FF)],
                                 src[:, ds(e * FF, FF)]).then_inc(w_loaded, 16)
                wait(sp, w_loaded, 16 * NW * (e + 1))
                passed(sp, sp_passed)

            load(0)
            load(1)
            with sp.Fori(0, E - 2) as n:
                load(Linear(n) + 2)

        @block.tensor
        def _(pe):
            def up_item(e, h):
                if h == 0:
                    wait(pe, w_split, e + 1)
                for f in range(FC):
                    wait(pe, hidden_done, (2 * e + h) * FC + f - 1)
                    for n, bank in enumerate([up, gate] if gated else [up]):
                        col = ds(value(e) % 2 * WSET + n * FF + f * P, P)
                        tok = slice(h * HALF, (h + 1) * HALF)
                        nc.tensor.matmul(bank[f % 2][:], wh[:, col], xTh[:, tok], start=True, stop=False)
                        nc.tensor.matmul(bank[f % 2][:], wh[:, col], xTl[:, tok], start=False, stop=False)
                        last = nc.tensor.matmul(bank[f % 2][:], wl[:, col], xTh[:, tok], start=False, stop=True)
                    last.then_inc(up_full, 1)

            def down_item(e, h):
                wait(pe, lo_done, (2 * e + h + 1) * FC)
                wait(pe, added, 2 * e + h - 1)
                for j in range(HALF // P):
                    out = down[h][:, j * P:(j + 1) * P]
                    for f in range(FC):
                        lhs = slice(f * HALF + j * P, f * HALF + (j + 1) * P)
                        col = ds(value(e) % 2 * WSET + DOWN + f * P, P)
                        nc.tensor.matmul(out, hh[:, h, lhs], wh[:, col], start=f == 0, stop=False)
                        nc.tensor.matmul(out, hh[:, h, lhs], wl[:, col], start=False, stop=False)
                        last = nc.tensor.matmul(out, hl[:, h, lhs], wh[:, col], start=False, stop=f == FC - 1)
                last.then_inc(down_full, 1)

            up_item(0, 0)
            up_item(0, 1)
            down_item(0, 0)
            with pe.Fori(0, E - 1) as n:
                e = Linear(n) + 1
                up_item(e, 0)
                down_item(e - 1, 1)
                up_item(e, 1)
                down_item(e, 0)
            down_item(E - 1, 1)

        @block.scalar
        def _(act):
            def split_hi(e):
                wait(act, w_loaded, 16 * NW * (e + 1))
                wait(act, down_full, 2 * (e - 1))
                cols = ds(value(e) % 2 * WSET, WSET)
                nc.scalar.activation(wh[:, cols], raw[:, cols], ACT.Copy, scale=MOE_SCALE).then_inc(whi_done, 1)

            def cast(e, h, f):
                if f == 0:
                    wait(act, down_full, 2 * e + h - 1)
                wait(act, hidden_done, (2 * e + h) * FC + f + 1)
                nc.scalar.activation(hh[:, h, f * HALF:(f + 1) * HALF], hidden[:, f % 2, :],
                                     ACT.Copy).then_inc(hi_done, 1)

            def item(e, h):
                for f in range(FC):
                    n = (2 * e + h) * FC + f
                    wait(act, up_full, n + 1)
                    wait(act, hidden_done if gated else lo_done, n - 1)
                    if b_up is not None:
                        passed(act, act_passed)
                    bias = b_up[:, ds(e * FC + f, 1)] if b_up is not None else 0.0
                    nc.scalar.activation(gelu[:, f % 2, :], up[f % 2][:], ACT.Gelu, bias=bias,
                                         scale=1.0 / MOE_SCALE).then_inc(gelu_done, 1)
                    if f:
                        cast(e, h, f - 1)
                cast(e, h, FC - 1)

            split_hi(0)
            item(0, 0)
            split_hi(1)
            item(0, 1)
            with act.Fori(0, E - 2) as n:
                e = Linear(n) + 1
                item(e, 0)
                split_hi(e + 1)
                item(e, 1)
            item(E - 1, 0)
            item(E - 1, 1)

        @block.vector
        def _(dve):
            def split_rest(e):
                wait(dve, whi_done, e + 1)
                cols = ds(value(e) % 2 * WSET, WSET)
                split_lo(nc.vector, wl[:, cols], raw[:, cols], MOE_SCALE, wh[:, cols]).then_inc(w_split, 1)

            def rest(e, h, f):
                wait(dve, hi_done, (2 * e + h) * FC + f + 1)
                nc.vector.tensor_tensor(hl[:, h, f * HALF:(f + 1) * HALF], hidden[:, f % 2, :],
                                        hh[:, h, f * HALF:(f + 1) * HALF], ALU.subtract).then_inc(lo_done, 1)

            def add(e, h):
                wait(dve, down_full, 2 * e + h + 1)
                wait(dve, added, 2 * e + h - 1)
                for j in range(HALF // P):
                    t = h * (HALF // P) + j
                    last = nc.vector.scalar_tensor_tensor(
                        out=x_res[:, t, :], in0=down[h][:, j * P:(j + 1) * P],
                        scalar=gates[:, ds(e * TT + t, 1)], in1=x_res[:, t, :], op0=ALU.mult, op1=ALU.add)
                last.then_inc(added, 1)

            def item(e, h, before):
                for f in range(FC):
                    if gated:
                        n = (2 * e + h) * FC + f
                        wait(dve, gelu_done, n + 1)
                        wait(dve, lo_done, n - 1)
                        nc.vector.scalar_tensor_tensor(out=hidden[:, f % 2, :], in0=gate[f % 2][:],
                                                       scalar=1.0 / MOE_SCALE, in1=gelu[:, f % 2, :],
                                                       op0=ALU.mult, op1=ALU.mult).then_inc(hidden_done, 1)
                    if f:
                        rest(e, h, f - 1)
                    if f == 1 and before is not None:
                        add(*before)
                rest(e, h, FC - 1)

            split_rest(0)
            item(0, 0, None)
            split_rest(1)
            item(0, 1, None)
            item(1, 0, (0, 0))
            split_rest(2)
            item(1, 1, (0, 1))
            with dve.Fori(0, E - 3) as n:
                e = Linear(n) + 2
                item(e, 0, (e - 1, 0))
                split_rest(e + 1)
                item(e, 1, (e - 1, 1))
            item(E - 1, 0, (E - 2, 0))
            item(E - 1, 1, (E - 2, 1))
            add(E - 1, 0)
            add(E - 1, 1)


def load_block(nc, name, loads, scale=()):
    with ExitStack() as ctx:
        loaded = ctx.enter_context(nc.semaphore(f"loaded_{name}"))
        block = ctx.enter_context(nc.Block())

        @block.sync
        def _(sp):
            for dst, src in loads:
                sp.dma_start(dst, src).then_inc(loaded, 16)
            sp.wait_ge(loaded, 16 * len(loads))

        @block.vector
        def _(dve):
            dve.wait_ge(loaded, 16 * len(loads))
            for tile, factor in scale:
                nc.vector.tensor_scalar(tile[:], tile[:], factor, None, ALU.mult)


def identity_block(nc, ident, rank8):
    with ExitStack() as ctx:
        made = ctx.enter_context(nc.semaphore("identity_made"))
        block = ctx.enter_context(nc.Block())

        @block.gpsimd
        def _(pool):
            nc.gpsimd.memset(ident[:], 0.0).then_inc(made, 1)
            pool.wait_ge(made, 1)
            nc.gpsimd.affine_select(out=ident[:], in_=ident[:], compare_op=ALU.not_equal, fill=1.0, base=0,
                                    pattern=[[-1, P]], channel_multiplier=1)

        @block.vector
        def _(dve):
            for e in range(8):
                nc.vector.memset(rank8[:, e:e + 1], float(8 - e))


def l0_linear_block(nc, x_res, xT, ctx_d, ctx_h, ctx_l, w1T, w2T, bias):
    PIECES = 4
    PIECE = KEYS // PIECES
    with ExitStack() as ctx:
        sb = lambda n, s, dt: ctx.enter_context(nc.sbuf_tensor(f"l0_{n}", s, dt))
        raw = sb("ctx_raw", [P, KEYS], FP32)
        sums = sb("ctx_sums", [P, PIECES], FP32)
        mean = sb("ctx_mean", [P, 1], FP32)
        mean_rows = sb("mean_rows", [P, P], FP32)
        ones = sb("ones", [P, P], FP32)
        out = [ctx.enter_context(nc.psum_tensor(f"l0_out{i}", [P, HALF], FP32)) for i in range(2)]
        loaded = [ctx.enter_context(nc.semaphore(f"l0_ctx_loaded{i}")) for i in range(PIECES)]
        hi_done = ctx.enter_context(nc.semaphore("l0_hi_done"))
        chain = ctx.enter_context(nc.semaphore("l0_chain"))
        mean_ready = ctx.enter_context(nc.semaphore("l0_mean_ready"))
        product = ctx.enter_context(nc.semaphore("l0_product"))
        block = ctx.enter_context(nc.Block())
        piece = lambda i: slice(i * PIECE, (i + 1) * PIECE)

        @block.sync
        def _(sp):
            for i in range(PIECES):
                sp.dma_start(raw[:, piece(i)], ctx_d[:, piece(i)]).then_inc(loaded[i], 16)

        @block.scalar
        def _(act):
            for i in range(PIECES):
                act.wait_ge(loaded[i], 16)
                nc.scalar.activation(ctx_h[:, piece(i)], raw[:, piece(i)], ACT.Copy, scale=C_SCALE).then_inc(hi_done, 1)

        @block.vector
        def _(dve):
            nc.vector.memset(ones[:], 1.0).then_inc(chain, 1)
            nc.vector.memset(ctx_h[:, KEYS:KPAD], 0.0)
            nc.vector.memset(ctx_l[:, KEYS:KPAD], 0.0)
            for i in range(PIECES):
                dve.wait_ge(loaded[i], 16)
                nc.vector.reduce_sum(sums[:, i:i + 1], raw[:, piece(i)], AX).then_inc(chain, 1)
                dve.wait_ge(hi_done, i + 1)
                split_lo(nc.vector, ctx_l[:, piece(i)], raw[:, piece(i)], C_SCALE, ctx_h[:, piece(i)])
            dve.wait_ge(chain, PIECES + 1)
            nc.vector.reduce_sum(mean[:], sums[:], AX).then_inc(chain, 1)
            dve.wait_ge(chain, PIECES + 2)
            nc.vector.tensor_scalar(mean_rows[:], ones[:], mean[:], 1.0 / KEYS, ALU.mult, ALU.mult).then_inc(mean_ready, 1)
            for t in range(TT):
                nc.vector.tensor_tensor(x_res[:, t, :], x_res[:, t, :], bias[:], ALU.add).then_inc(chain, 1)
            for t in range(TT):
                dve.wait_ge(product, 4 * (t // 4 + 1))
                dve.wait_ge(chain, PIECES + 3 + t)
                nc.vector.tensor_tensor(x_res[:, t, :], x_res[:, t, :], out[t // 4][:, (t % 4) * P:(t % 4 + 1) * P], ALU.add)

        @block.tensor
        def _(pe):
            pe.wait_ge(mean_ready, 1)
            for t in range(TT):
                o = out[t // 4][:, (t % 4) * P:(t % 4 + 1) * P]
                nc.tensor.matmul(o, xT[:, t * P:(t + 1) * P], w1T[:], start=True, stop=False)
                nc.tensor.matmul(o, mean_rows[:], w2T[:], start=False, stop=True).then_inc(product, 1)


def l0_router_block(nc, x_res, xT, w_red, wg, b2, ident, rank8, gates):
    E, G = 8, 16
    with ExitStack() as ctx:
        sb = lambda n, s: ctx.enter_context(nc.sbuf_tensor(f"r0_{n}", s, FP32))
        sq, ss, wgn, wgnT, redT = sb("sq", [E, G]), sb("ss", [E, 1]), sb("wgn", [E, G]), sb("wgnT", [G, E]), sb("redT", [G, TOK])
        logits, value, hot, ex, score = sb("logits", [P, TT, E]), sb("value", [P, TT, E]), sb("hot", [P, TT, E]), sb("ex", [P, TT, E]), sb("score", [P, TT])
        peak, top, scoreT = sb("peak", [P, TT]), sb("top", [P, TT]), sb("scoreT", [E, TOK])
        wT_ps = ctx.enter_context(nc.psum_tensor("r0_wT", [P, HALF], FP32))
        red_ps = [ctx.enter_context(nc.psum_tensor(f"r0_red{i}", [P, HALF], FP32)) for i in range(2)]
        lg_ps = ctx.enter_context(nc.psum_tensor("r0_lg", [P, HALF], FP32))
        sT_ps = [ctx.enter_context(nc.psum_tensor(f"r0_sT{i}", [P, HALF], FP32)) for i in range(2)]
        b2_ps = [ctx.enter_context(nc.psum_tensor(f"r0_b2{i}", [P, HALF], FP32)) for i in range(2)]
        chain = ctx.enter_context(nc.semaphore("r0_chain"))
        squared = ctx.enter_context(nc.semaphore("r0_squared"))
        rooted = ctx.enter_context(nc.semaphore("r0_rooted"))
        wgn_ready = ctx.enter_context(nc.semaphore("r0_wgn_ready"))
        turned = ctx.enter_context(nc.semaphore("r0_turned"))
        red_done = ctx.enter_context(nc.semaphore("r0_red_done"))
        evacuated = ctx.enter_context(nc.semaphore("r0_evacuated"))
        logits_done = ctx.enter_context(nc.semaphore("r0_logits_done"))
        shifted = ctx.enter_context(nc.semaphore("r0_shifted"))
        exped = ctx.enter_context(nc.semaphore("r0_exped"))
        scored = ctx.enter_context(nc.semaphore("r0_scored"))
        sT_done = ctx.enter_context(nc.semaphore("r0_sT_done"))
        sT_copied = ctx.enter_context(nc.semaphore("r0_sT_copied"))
        b2_done = ctx.enter_context(nc.semaphore("r0_b2_done"))
        block = ctx.enter_context(nc.Block())
        col = lambda t: slice((t % 4) * P, (t % 4 + 1) * P)

        @block.vector
        def _(dve):
            n = [0]

            def link(instruction):
                n[0] += 1
                instruction.then_inc(chain, 1)
                dve.wait_ge(chain, n[0])

            link(nc.vector.tensor_tensor(sq[:], wg[:], wg[:], ALU.mult))
            nc.vector.reduce_sum(ss[:], sq[:], AX).then_inc(squared, 1)
            dve.wait_ge(rooted, 1)
            link(nc.vector.tensor_scalar(ss[:], ss[:], 1e-4, None, ALU.max))
            link(nc.vector.reciprocal(ss[:], ss[:]))
            nc.vector.tensor_scalar(wgn[:], wg[:], ss[:], None, ALU.mult).then_inc(wgn_ready, 1)
            dve.wait_ge(turned, 1)
            nc.vector.tensor_copy(wgnT[:], wT_ps[0:G, 0:E]).then_inc(evacuated, 1)
            for i in range(2):
                dve.wait_ge(red_done, i + 1)
                nc.vector.tensor_copy(redT[:, i * HALF:(i + 1) * HALF], red_ps[i][0:G, :]).then_inc(evacuated, 1)
            dve.wait_ge(logits_done, 1)
            link(nc.vector.tensor_copy(logits[:], lg_ps[:, 0:TT * E].rearrange("p (t e) -> p t e", e=E)))
            link(nc.vector.reduce_max(top[:], logits[:], AX))
            nc.vector.tensor_tensor(ex[:], logits[:], top[:].unsqueeze(2).to_broadcast([P, TT, E]),
                                    ALU.subtract).then_inc(shifted, 1)
            one_hot_first_max(nc, link, logits, peak, rank8, value, hot, E)
            dve.wait_ge(exped, 1)
            link(nc.vector.reduce_sum(score[:], ex[:], AX))
            link(nc.vector.reciprocal(score[:], score[:]))
            link(nc.vector.tensor_tensor(hot[:], hot[:], score[:].unsqueeze(2).to_broadcast([P, TT, E]), ALU.mult))
            nc.vector.tensor_scalar(gates[:, 0:E * TT].rearrange("p (e t) -> p t e", t=TT), hot[:], 1.0 / MOE_SCALE,
                                    None, ALU.mult).then_inc(scored, 1)
            for i in range(2):
                dve.wait_ge(sT_done, i + 1)
                nc.vector.tensor_copy(scoreT[:, i * HALF:(i + 1) * HALF], sT_ps[i][0:E, :]).then_inc(sT_copied, 1)
            for t in range(TT):
                dve.wait_ge(b2_done, 4 * (t // 4 + 1))
                nc.vector.tensor_tensor(x_res[:, t, :], x_res[:, t, :], b2_ps[t // 4][:, col(t)], ALU.add)

        @block.scalar
        def _(act):
            act.wait_ge(squared, 1)
            nc.scalar.activation(ss[:], ss[:], ACT.Sqrt).then_inc(rooted, 1)
            act.wait_ge(shifted, 1)
            nc.scalar.activation(ex[:], ex[:], ACT.Exp).then_inc(exped, 1)

        @block.tensor
        def _(pe):
            pe.wait_ge(wgn_ready, 1)
            nc.tensor.transpose(wT_ps[0:G, 0:E], wgn[:], ident[0:E, 0:E]).then_inc(turned, 1)
            for i in range(2):
                nc.tensor.matmul(red_ps[i][0:G, :], w_red[:], xT[:, i * HALF:(i + 1) * HALF],
                                 start=True, stop=True).then_inc(red_done, 1)
            pe.wait_ge(evacuated, 3)
            for t in range(TT):
                last = nc.tensor.matmul(lg_ps[:, t * E:(t + 1) * E], redT[:, t * P:(t + 1) * P], wgnT[:],
                                        start=True, stop=True)
            last.then_inc(logits_done, 1)
            pe.wait_ge(scored, 1)
            for t in range(TT):
                last = nc.tensor.transpose(sT_ps[t // 4][0:E, col(t)], hot[:, t, :], ident[:])
                if t % 4 == 3:
                    last.then_inc(sT_done, 1)
            for t in range(TT):
                pe.wait_ge(sT_copied, t // 4 + 1)
                nc.tensor.matmul(b2_ps[t // 4][:, col(t)], scoreT[:, t * P:(t + 1) * P], b2[:],
                                 start=True, stop=True).then_inc(b2_done, 1)


def l1_router_block(nc, xT, wg, rank8, gates):
    E = 8
    with ExitStack() as ctx:
        sb = lambda n, s: ctx.enter_context(nc.sbuf_tensor(f"r1_{n}", s, FP32))
        logits, value, hot, peak = sb("logits", [P, TT, E]), sb("value", [P, TT, E]), sb("hot", [P, TT, E]), sb("peak", [P, TT])
        lg_ps = ctx.enter_context(nc.psum_tensor("r1_lg", [P, HALF], FP32))
        chain = ctx.enter_context(nc.semaphore("r1_chain"))
        logits_done = ctx.enter_context(nc.semaphore("r1_logits_done"))
        block = ctx.enter_context(nc.Block())

        @block.tensor
        def _(pe):
            for t in range(TT):
                last = nc.tensor.matmul(lg_ps[:, t * E:(t + 1) * E], xT[:, t * P:(t + 1) * P], wg[:],
                                        start=True, stop=True)
            last.then_inc(logits_done, 1)

        @block.vector
        def _(dve):
            n = [0]

            def link(instruction):
                n[0] += 1
                instruction.then_inc(chain, 1)
                dve.wait_ge(chain, n[0])

            nc.vector.memset(gates[:, 0:TT], 1.0 / MOE_SCALE)
            dve.wait_ge(logits_done, 1)
            link(nc.vector.tensor_copy(logits[:], lg_ps[:, 0:TT * E].rearrange("p (t e) -> p t e", e=E)))
            one_hot_first_max(nc, link, logits, peak, rank8, value, hot, E)
            nc.vector.tensor_scalar(gates[:, TT:(E + 1) * TT].rearrange("p (e t) -> p t e", t=TT), hot[:],
                                    1.0 / MOE_SCALE, None, ALU.mult)


def q_block(nc, xTh, xTl, wqT, bq8, q_dram):
    with ExitStack() as ctx:
        sb = lambda n, s, dt: ctx.enter_context(nc.sbuf_tensor(f"q_{n}", s, dt))
        wh, wl = sb("wh", [P, HEADS * DK], FP16), sb("wl", [P, HEADS * DK], FP16)
        qh, ql = sb("qh", [P, 2, TOK], FP16), sb("ql", [P, 2, TOK], FP16)
        ps = [ctx.enter_context(nc.psum_tensor(f"q_ps{i}", [P, HALF], FP32)) for i in range(2)]
        whi, wsplit, full = (ctx.enter_context(nc.semaphore(f"q_{n}")) for n in ("whi", "wsplit", "full"))
        hi_done, lo_done, stored = (ctx.enter_context(nc.semaphore(f"q_{n}")) for n in ("hi_done", "lo_done", "stored"))
        block = ctx.enter_context(nc.Block())

        @block.scalar
        def _(act):
            nc.scalar.activation(wh[:], wqT[:], ACT.Copy, scale=WQ_SCALE).then_inc(whi, 1)
            for p in range(PAIRS):
                for i in range(2):
                    act.wait_ge(full, 2 * p + i + 1)
                    if p >= 2 and i == 0:
                        act.wait_ge(stored, 32 * (p - 1))
                    nc.scalar.activation(qh[:, p % 2, i * HALF:(i + 1) * HALF], ps[i][:], ACT.Identity,
                                         bias=bq8[:, p:p + 1]).then_inc(hi_done, 1)

        @block.vector
        def _(dve):
            dve.wait_ge(whi, 1)
            split_lo(nc.vector, wl[:], wqT[:], WQ_SCALE, wh[:]).then_inc(wsplit, 1)
            for p in range(PAIRS):
                for i in range(2):
                    dve.wait_ge(hi_done, 2 * p + i + 1)
                    cols = slice(i * HALF, (i + 1) * HALF)
                    nc.vector.scalar_tensor_tensor(out=ql[:, p % 2, cols], in0=ps[i][:], scalar=bq8[:, p:p + 1],
                                                   in1=qh[:, p % 2, cols], op0=ALU.add,
                                                   op1=ALU.subtract).then_inc(lo_done, 1)

        @block.tensor
        def _(pe):
            pe.wait_ge(wsplit, 1)
            for p in range(PAIRS):
                w = slice(p * P, (p + 1) * P)
                for i in range(2):
                    x = slice(i * HALF, (i + 1) * HALF)
                    if p:
                        pe.wait_ge(lo_done, 2 * p + i - 1)
                    nc.tensor.matmul(ps[i][:], wh[:, w], xTh[:, x], start=True, stop=False)
                    nc.tensor.matmul(ps[i][:], wh[:, w], xTl[:, x], start=False, stop=False)
                    nc.tensor.matmul(ps[i][:], wl[:, w], xTh[:, x], start=False, stop=True).then_inc(full, 1)

        @block.sync
        def _(sp):
            for p in range(PAIRS):
                sp.wait_ge(lo_done, 2 * p + 2)
                sp.dma_start(q_dram[p, 0], qh[:, p % 2, :]).then_inc(stored, 16)
                sp.dma_start(q_dram[p, 1], ql[:, p % 2, :]).then_inc(stored, 16)
                sp.wait_ge(stored, 32 * (p + 1))


def wo_block(nc, x_res, ctx_dram, woT, ident):
    EC = HEADS * DK // P
    with ExitStack() as ctx:
        sb = lambda n, s, dt: ctx.enter_context(nc.sbuf_tensor(f"wo_{n}", s, dt))
        rows = sb("rows", [P, TT, HEADS * DK], FP32)
        turned_sb = sb("turned", [P, 2, EC * P], FP32)
        tp = [ctx.enter_context(nc.psum_tensor(f"wo_tp{i}", [P, 2 * HALF], FP32)) for i in range(2)]
        out = [ctx.enter_context(nc.psum_tensor(f"wo_out{i}", [P, P], FP32)) for i in range(2)]
        loaded = [ctx.enter_context(nc.semaphore(f"wo_loaded{i}")) for i in range(2)]
        turned, copied, product, added = (ctx.enter_context(nc.semaphore(f"wo_{n}")) for n in ("turned_s", "copied", "product", "added"))
        block = ctx.enter_context(nc.Block())

        @block.sync
        def _(sp):
            for i in range(2):
                for j in range(TT // 2):
                    sp.dma_start(rows[:, i * 4 + j, :].rearrange("p (h d) -> p h d", d=DK),
                                 ctx_dram[:, i, :, j, :].rearrange("h p d -> p h d")).then_inc(loaded[i], 16)

        @block.tensor
        def _(pe):
            def turn(t):
                if t % 4 == 0:
                    pe.wait_ge(loaded[t // 4], 64)
                if t >= 2:
                    pe.wait_ge(copied, t - 1)
                for e in range(EC):
                    last = nc.tensor.transpose(tp[t % 2][:, e * P:(e + 1) * P], rows[:, t, e * P:(e + 1) * P], ident[:])
                last.then_inc(turned, 1)

            turn(0)
            for t in range(TT):
                if t + 1 < TT:
                    turn(t + 1)
                pe.wait_ge(copied, t + 1)
                if t >= 2:
                    pe.wait_ge(added, t - 1)
                for e in range(EC):
                    last = nc.tensor.matmul(out[t % 2][:], turned_sb[:, t % 2, e * P:(e + 1) * P],
                                            woT[:, e * P:(e + 1) * P], start=e == 0, stop=e == EC - 1)
                last.then_inc(product, 1)

        @block.scalar
        def _(act):
            for t in range(TT):
                act.wait_ge(turned, t + 1)
                if t >= 2:
                    act.wait_ge(product, t - 1)
                nc.scalar.activation(turned_sb[:, t % 2, :], tp[t % 2][:], ACT.Copy).then_inc(copied, 1)

        @block.vector
        def _(dve):
            for t in range(TT):
                dve.wait_ge(product, t + 1)
                nc.vector.tensor_tensor(x_res[:, t, :], x_res[:, t, :], out[t % 2][:], ALU.add).then_inc(added, 1)


def attention_block(nc, ctx_h, ctx_l, wkT_d, wvT_d, bk_d, bv_d, q_dram, ctx_dram, ident):
    with ExitStack() as ctx:
        sb = lambda n, s, dt=FP32: ctx.enter_context(nc.sbuf_tensor(n, s, dt))
        ps = lambda n, s: ctx.enter_context(nc.psum_tensor(n, s, FP32))
        sem = lambda n: ctx.enter_context(nc.semaphore(n))

        k_both = [sb(f"k_both{i}", [P, KPAD], FP16) for i in range(2)]
        k_step = [sb(f"k_step{i}", [P, KPAD], FP16) for i in range(2)]
        k_hi, k_lo = sb("k_hi", [P, KPAD], FP16), sb("k_lo", [P, KPAD], FP16)
        q_both = [sb(f"q_both{i}", [P, TOK], FP16) for i in range(2)]
        q_step = [sb(f"q_step{i}", [P, TOK], FP16) for i in range(2)]
        v_sb = sb("v", [P, 3, KT * V_W], FP16)
        wk_h, wk_l, wv_h, wv_l = (sb(n, [P, HEADS * DK], FP16) for n in ("wk_h", "wk_l", "wv_h", "wv_l"))
        bk8, bv_bc = sb("bk8", [P, PAIRS]), sb("bv_bc", [P, HEADS * DK])
        prob, prob_l = sb("prob", [P, SLOTS * 2 * HALF]), sb("prob_l", [P, SLOTS * 2 * HALF], FP16)
        prob_h = prob[:].bitcast(BF16).rearrange("p (n two) -> p n two", two=2)[:, :, 1]
        chunk_max, row_max = sb("chunk_max", [P, 4 * CHUNKS]), sb("row_max", [P, 4])
        max_cols, ident_h = sb("max_cols", [P, 4, P], FP16), sb("ident_h", [P, P], FP16)
        acc = sb("acc", [P, 2, 2 * V_W])
        denom, sums, out_sb = sb("denom", [P, 4]), sb("sums", [P, 4, DK]), sb("out_sb", [P, 4, DK])

        score = [ps(f"score{i}", [P, 2 * HALF]) for i in range(2)]
        pv = ps("pv", [P, 2, HALF])
        aux = [ps(f"aux{i}", [P, HALF]) for i in range(2)]

        loaded_w, w_hi, w_split, consts = sem("loaded_w"), sem("w_hi"), sem("w_split"), sem("consts")
        head_loaded = [sem("head_a_loaded"), sem("head_b_loaded")]
        v_loaded = sem("v_loaded")
        score_full, exp_done = sem("score_full"), sem("exp_done")
        rest_pool, rest_dve, pv_done = sem("rest_pool"), sem("rest_dve"), sem("pv_done")
        aux_full = [sem("aux_full0"), sem("aux_full1")]
        aux_free = [sem("aux_free0"), sem("aux_free1")]
        hi_done, k_padded, zeroed = sem("hi_done"), sem("k_padded"), sem("zeroed")
        max_ready, pv_free, out_ready, stored = sem("diag_ready"), sem("pv_free"), sem("out_ready"), sem("out_stored")
        shift_chain, out_chain = sem("shift_chain"), sem("out_chain")
        act_passed, sp_passed = sem("act_passed"), sem("sp_passed")
        block = ctx.enter_context(nc.Block())

        WORK = (None, "k", "v", None)
        LOADS = 6
        CONSTS = 2
        PRO_AUX0, PRO_AUX1 = 2 * CHUNKS + 2 * CHUNKS, 2 * CHUNKS + 1

        def stage_no(p, t):
            return 4 * p + t

        def items(c, work, find):
            second, closing = isinstance(c, int) and c == 1, isinstance(c, int) and c == CHUNKS - 1
            beside = [[], [], [], []]
            if find and not closing:
                for i in range(4):
                    beside[i].append(("max", c, i, i % 2 if i or not work else 1))
                if second:
                    beside[1].append(("max", CHUNKS - 1, 0, 0))
                    beside[2].append(("max", CHUNKS - 1, 1, 1))
                    beside[3] = [("max", CHUNKS - 1, 2, 0)] + beside[3] + [("max", CHUNKS - 1, 3, 0)]
            if work:
                beside[0].append((work, c, None, 0))
            if find and closing:
                beside[1].append(("shift", None, None, 1))
            return beside

        def bank_items(c, work, find, bank):
            return sum(1 for group in items(c, work, find) for item in group if item[3] == bank)

        def before_chunk(c, work, find, bank):
            if isinstance(c, int):
                return sum(bank_items(n, work, find, bank) for n in range(c))
            return before_chunk(2, work, find, bank) + (c + -2) * bank_items(2, work, find, bank)

        def aux_count(bank, p, t, last):
            of = lambda u, l: before_chunk(CHUNKS, has_work(u, l), has_max(u, l), bank)
            return ((PRO_AUX1 if bank else PRO_AUX0) + sum(of(u, False) for u in range(4)) * p
                    + sum(of(u, last) for u in range(t)))

        def has_work(t, last):
            return WORK[t] if not last else None

        def has_max(t, last):
            return not (last and t == 3)

        def hi_count(p, t, last):
            return 2 * CHUNKS + 2 * CHUNKS * p + sum(CHUNKS for u in range(t) if has_work(u, last))

        def width(c):
            return P * chunk_tiles(isinstance(c, int) and c == CHUNKS - 1)

        def step_tiles(g):
            return 1 if isinstance(g, int) and g == STEPS - 1 else 2

        def chunks(engine, body):
            body(0, 0)
            body(1, 1)
            with engine.Fori(0, (CHUNKS - 3) // 2) as m:
                body(2 * Linear(m) + 2, 0)
                body(2 * Linear(m) + 3, 1)
            body(CHUNKS - 1, 0)

        def stages(engine, stage):
            stage(0, 0, True, False)
            with engine.Fori(0, PAIRS - 1) as pair:
                p = Linear(pair)
                for t in (1, 2, 3):
                    stage(p, t, False, False)
                stage(p + 1, 0, False, False)
            for t in (1, 2, 3):
                stage(PAIRS - 1, t, False, True)

        def pool_rests(s, c, k, i):
            return 3 * (CHUNKS * s + c) + 2 * k + i

        def v_rows(c):
            n = width(c) // P
            return v_sb[:, 0:2, ds(c * CHUNK_TILES * V_W, n * V_W)].rearrange("p h (i w) -> p h i w", w=V_W)

        def v_projected(c):
            return aux[0][:, 0:width(c)].rearrange("p (i h w) -> p h i w", h=2, w=DK)

        def slot(odd, t, k):
            return (((odd + t) % 2) * 2 + k) * 2 * HALF

        @block.sync
        def _(sp):
            def load_head(p, b):
                rows = slice(b * DK, (b + 1) * DK)
                done = head_loaded[b]
                sp.dma_start(k_both[b][0:DK, :], k_hi[rows, :]).then_inc(done, 16)
                sp.dma_start(k_both[b][DK:P, :], k_lo[rows, :]).then_inc(done, 16)
                sp.dma_start(k_step[b][0:DK, :], k_hi[rows, :]).then_inc(done, 16)
                q = q_dram[ds(p, 1), :, rows, :].rearrange("o c r n -> (o c) r n")
                sp.dma_start(q_both[b][0:DK, :], q[0]).then_inc(done, 16)
                sp.dma_start(q_both[b][DK:P, :], q[0]).then_inc(done, 16)
                sp.dma_start(q_step[b][0:DK, :], q[1]).then_inc(done, 16)

            def store(p, t):
                wait(sp, out_ready, stage_no(p, t) + 1)
                head = 2 * p + t // 2
                sp.dma_start(ctx_dram[ds(head, 1), t % 2].rearrange("o p j d -> (o p) j d"),
                             out_sb[:]).then_inc(stored, 16)

            def stage(p, t, first, last):
                if t in (0, 2) and not (last and t):
                    b = 1 if t == 0 else 0
                    wait(sp, score_full, STEPS * stage_no(p, t) + 1)
                    passed(sp, sp_passed)
                    wait(sp, k_padded, p + (1 if t == 0 else 2))
                    passed(sp, sp_passed)
                    load_head(p if t == 0 else p + 1, b)
                if t == 0:
                    wait(sp, pv_done, STEPS * stage_no(p, 0))
                    wait(sp, aux_free[0], aux_count(0, p, 0, last))
                    sp.dma_start(v_sb[:, 2, :], v_sb[:, 1, :]).then_inc(v_loaded, 16)
                if t:
                    store(p, t - 1)
                elif not first:
                    store(p - 1, 3)

            sp.dma_start(prob[:, 0:2 * HALF], wkT_d).then_inc(loaded_w, 16)
            sp.dma_start(prob[:, 2 * HALF:4 * HALF], wvT_d).then_inc(loaded_w, 16)
            sp.dma_start(bk8[:], bk_d).then_inc(loaded_w, 16)
            sp.dma_start(bv_bc[:], bv_d.to_broadcast([P, HEADS * DK])).then_inc(loaded_w, 16)
            wait(sp, k_padded, 1)
            load_head(0, 0)
            stages(sp, stage)
            store(PAIRS - 1, 3)
            wait(sp, stored, 16 * 4 * PAIRS)

        @block.tensor
        def _(pe):
            def scores(p, t, c, k, i, last):
                g = 2 * c + k
                n = STEPS * stage_no(p, t) + g
                b = t // 2
                if i == 0:
                    wait(pe, exp_done, n - 1)
                q = slice((t % 2) * HALF, (t % 2 + 1) * HALF)
                keys = ds((2 * g + i) * P, P)
                out = score[k][:, i * HALF:(i + 1) * HALF]
                nc.tensor.matmul(out, k_both[b][:, keys], q_both[b][:, q], start=True, stop=False)
                if isinstance(g, int) and g == 0 and i == 0:
                    wait(pe, aux_free[1], aux_count(1, p, t, last))
                done = nc.tensor.matmul(out, k_step[b][:, keys], q_step[b][:, q], start=False, stop=True)
                if i == step_tiles(g) - 1:
                    done.then_inc(score_full, 1)

            def maxima(p, t, c, i, bank, base):
                tile = (t % 2) * 4 + i
                wait(pe, aux_free[bank], base)
                nc.tensor.matmul(aux[bank][:, 0:width(c)], q_both[t // 2][:, tile * P:(tile + 1) * P],
                                 k_both[t // 2][:, ds(c * HALF, width(c))],
                                 start=True, stop=True).then_inc(aux_full[bank], 1)

            def project_k(p, c, base):
                wait(pe, aux_free[0], base)
                w, keys = ds(p * P, P), ds(c * HALF, width(c))
                out = aux[0][:, 0:width(c)]
                nc.tensor.matmul(out, wk_h[:, w], ctx_h[:, keys], start=True, stop=False)
                nc.tensor.matmul(out, wk_h[:, w], ctx_l[:, keys], start=False, stop=False)
                nc.tensor.matmul(out, wk_l[:, w], ctx_h[:, keys], start=False, stop=True).then_inc(aux_full[0], 1)

            def project_v(pair, c, base):
                wait(pe, aux_free[0], base)
                w = ds(pair * P, P)
                for i in range(width(c) // P):
                    keys = ds(c * HALF + i * P, P)
                    out = aux[0][:, i * P:(i + 1) * P]
                    nc.tensor.matmul(out, ctx_h[:, keys], wv_h[:, w], start=True, stop=False)
                    nc.tensor.matmul(out, ctx_h[:, keys], wv_l[:, w], start=False, stop=False)
                    last = nc.tensor.matmul(out, ctx_l[:, keys], wv_h[:, w], start=False, stop=True)
                last.then_inc(aux_full[0], 1)

            project = {"k": project_k, "v": project_v}

            def shift(s, base):
                wait(pe, max_ready, s + 1)
                wait(pe, aux_free[1], base)
                for i in range(4):
                    last = nc.tensor.matmul(aux[1][:, i * P:(i + 1) * P], max_cols[:, i, :], ident_h[:],
                                            start=True, stop=True)
                last.then_inc(aux_full[1], 1)

            def weigh(p, t, c, odd, k, i, last):
                g = 2 * c + k
                s = stage_no(p, t)
                b = t // 2
                if isinstance(g, int) and g == 0 and i == 0:
                    wait(pe, pv_free, s)
                    if b == 0:
                        wait(pe, aux_free[0], aux_count(0, p, t, last))
                    else:
                        wait(pe, v_loaded, 16 * (p + 1))
                if k and i:
                    wait(pe, rest_dve, (CHUNKS - 1) * s + c + 1)
                else:
                    wait(pe, rest_pool, pool_rests(s, c, k, i) + 1)
                for j in range(4):
                    cols = ds(slot(odd, t, k) + i * HALF + j * P, P)
                    out = pv[:, j // 2, (j % 2) * V_W:(j % 2 + 1) * V_W]
                    v = (2 * g + i) * V_W
                    start = isinstance(g, int) and g == 0 and i == 0 and j % 2 == 0
                    stop = isinstance(g, int) and g == STEPS - 1
                    nc.tensor.matmul(out, prob_h[:, cols], v_sb[:, 2 * b, ds(v, V_W)],
                                     start=start, stop=False, skip_group_check=True)
                    done = nc.tensor.matmul(out[:, 0:DK + 1], prob_l[:, cols], v_sb[:, 2 * b, ds(v, DK + 1)],
                                            start=False, stop=stop, skip_group_check=True)
                if i == step_tiles(g) - 1:
                    done.then_inc(pv_done, 1)

            def stage(p, t, first, last):
                work, find = has_work(t, last), has_max(t, last)
                before = (p, t - 1) if t else (p - 1, 3)
                after = (p, t + 1) if t < 3 else (p + 1, 0)
                count = [aux_count(bank, p, t, last) for bank in range(2)]
                if find and t in (1, 3):
                    wait(pe, head_loaded[after[1] // 2], 16 * LOADS * (after[0] + 1))

                def chunk(c, odd):
                    opening = isinstance(c, int) and c == 0
                    closing = isinstance(c, int) and c == CHUNKS - 1
                    at = [count[bank] + before_chunk(c, work, find, bank) for bank in range(2)]
                    for j, group in enumerate(items(c, work, find)):
                        k, i = j // 2, j % 2
                        if not (closing and j == 3):
                            scores(p, t, c, k, i, last)
                        for kind, of, tile, bank in group:
                            if kind == "max":
                                maxima(*after, of, tile, bank, at[bank])
                            elif kind == "shift":
                                shift(stage_no(p, t) + 1, at[bank])
                            else:
                                project[kind](p + 1, of, at[bank])
                            at[bank] = at[bank] + 1
                        if not opening:
                            weigh(p, t, c - 1, 1 - odd, k, i, last)
                        elif not first and j < 3:
                            weigh(*before, CHUNKS - 1, 0, k, i, False)

                chunks(pe, chunk)

            wait(pe, w_split, 2)
            n0 = n1 = 0
            for c in range(CHUNKS):
                project_k(0, c, n0)
                project_v(0, c, n0 + 1)
                n0 += 2
            wait(pe, head_loaded[0], 16 * LOADS)
            for c in range(CHUNKS):
                for i in range(4):
                    maxima(0, 0, c, i, i % 2, (n0, n1)[i % 2])
                    n0, n1 = n0 + 1 - i % 2, n1 + i % 2
            wait(pe, consts, CONSTS)
            shift(0, n1)
            stages(pe, stage)
            for j in range(KT - CHUNK_TILES * (CHUNKS - 1)):
                weigh(PAIRS - 1, 3, CHUNKS - 1, 0, j // 2, j % 2, True)

        @block.scalar
        def _(act):
            def probabilities(p, t, c, odd, k):
                g = 2 * c + k
                s = stage_no(p, t)
                n = STEPS * s + g
                w = step_tiles(g) * HALF
                wait(act, score_full, n + 1)
                wait(act, pv_done, n - SLOTS + 1)
                nc.scalar.activation(prob[:, ds(slot(odd, t, k), w)], score[k][:, 0:w], ACT.Exp,
                                     scale=EXP_SCALE).then_inc(exp_done, 1)

            def high_part(kind, p, c, base):
                wait(act, aux_full[0], base + 1)
                passed(act, act_passed)
                w = width(c)
                if kind == "k":
                    nc.scalar.activation(k_hi[:, ds(c * HALF, w)], aux[0][:, 0:w], ACT.Identity,
                                         bias=bk8[:, ds(p, 1)]).then_inc(hi_done, 1)
                else:
                    nc.scalar.activation(v_rows(c)[:, :, :, 0:DK], v_projected(c), ACT.Copy).then_inc(hi_done, 1)

            def shift(s, t, n1):
                wait(act, aux_full[1], n1 + 1)
                q = slice((t % 2) * HALF, (t % 2 + 1) * HALF)
                nc.scalar.activation(q_step[t // 2][DK:P, q], aux[1][DK:P, :], ACT.Copy).then_inc(aux_free[1], 1)

            def evacuate(s):
                wait(act, pv_done, STEPS * (s + 1))
                wait(act, out_ready, s)
                nc.scalar.activation(acc[:], pv[:, :, 0:2 * V_W], ACT.Copy).then_inc(pv_free, 1)

            def stage(p, t, first, last):
                work = has_work(t, last)
                a0 = aux_count(0, p, t, last)
                find = has_max(t, last)
                if work == "k":
                    wait(act, head_loaded[1], 16 * LOADS * (p + 1))
                if work == "v":
                    wait(act, v_loaded, 16 * (p + 1))

                def chunk(c, odd):
                    if work:
                        high_part(work, p + 1, c, a0 + before_chunk(c, work, find, 0))
                    probabilities(p, t, c, odd, 0)
                    if isinstance(c, int) and c == 0 and not first:
                        evacuate(stage_no(p, t) - 1)
                    if isinstance(c, int) and c == CHUNKS - 1 and find:
                        shift(stage_no(p, t) + 1, (t + 1) % 4,
                              aux_count(1, p, t, last) + before_chunk(c, work, find, 1))
                    probabilities(p, t, c, odd, 1)

                chunks(act, chunk)

            wait(act, loaded_w, 64)
            nc.scalar.activation(wk_h[:], prob[:, 0:2 * HALF], ACT.Copy, scale=W_SCALE).then_inc(w_hi, 1)
            nc.scalar.activation(wv_h[:], prob[:, 2 * HALF:4 * HALF], ACT.Copy, scale=W_SCALE).then_inc(w_hi, 1)
            for c in range(CHUNKS):
                if c == 0:
                    wait(act, consts, CONSTS)
                high_part("k", 0, c, 2 * c)
                high_part("v", 0, c, 2 * c + 1)
            shift(0, 0, 2 * CHUNKS)
            stages(act, stage)
            evacuate(4 * PAIRS - 1)

        @block.gpsimd
        def _(pool):
            nc.gpsimd.memset(max_cols[:], 0.0).then_inc(zeroed, 1)
            nc.gpsimd.tensor_copy(ident_h[:], ident[:]).then_inc(consts, 1)

            def stage(p, t, first, last):
                def chunk(c, odd):
                    for k, i in ((0, 0), (0, 1), (1, 0)):
                        if i == 0:
                            wait(pool, exp_done, STEPS * stage_no(p, t) + 2 * c + k + 1)
                        hl = ds(slot(odd, t, k) + i * HALF, HALF)
                        nc.gpsimd.tensor_tensor(prob_l[:, hl], prob[:, hl], prob_h[:, hl],
                                                ALU.subtract).then_inc(rest_pool, 1)

                chunks(pool, chunk)

            stages(pool, stage)

        @block.vector
        def _(dve):
            def rest_share(p, t, c, odd):
                s = stage_no(p, t)
                wait(dve, exp_done, STEPS * s + 2 * c + 2)
                hl = ds(slot(odd, t, 1) + HALF, HALF)
                nc.vector.tensor_tensor(prob_l[:, hl], prob[:, hl], prob_h[:, hl],
                                        ALU.subtract).then_inc(rest_dve, 1)

            def maxima(c, i, bank, base):
                wait(dve, aux_full[bank], base + 1)
                nc.vector.reduce_max(chunk_max[:, ds(i * CHUNKS + c, 1)],
                                     aux[bank][:, 0:width(c)], AX).then_inc(aux_free[bank], 1)

            def rest_part(kind, p, c, his):
                wait(dve, hi_done, his + 1)
                w = width(c)
                if kind == "k":
                    keys = ds(c * HALF, w)
                    nc.vector.scalar_tensor_tensor(out=k_lo[:, keys], in0=aux[0][:, 0:w], scalar=bk8[:, ds(p, 1)],
                                                   in1=k_hi[:, keys], op0=ALU.add, op1=ALU.subtract).then_inc(aux_free[0], 1)
                else:
                    rows = v_rows(c)
                    nc.vector.tensor_tensor(rows[:, :, :, DK + 1:V_W], v_projected(c), rows[:, :, :, 0:DK],
                                            ALU.subtract).then_inc(aux_free[0], 1)

            def pad_keys(n):
                wait(dve, aux_free[0], n)
                for m, tile in enumerate((k_hi, k_lo)):
                    last = nc.vector.tensor_copy(tile[:, KEYS:KPAD], tile[:, KEYS - 1:KEYS].to_broadcast([P, KPAD - KEYS]))
                last.then_inc(k_padded, 1)

            def row_maxima(s, n1):
                wait(dve, aux_free[1], n1)
                nc.vector.reduce_max(row_max[:], chunk_max[:].rearrange("p (i c) -> p i c", c=CHUNKS),
                                     AX).then_inc(shift_chain, 1)
                wait(dve, shift_chain, 2 * s + 1)
                m = row_max[:].unsqueeze(2).to_broadcast([P, 4, 32])
                high, rest = max_cols[:, :, DK:DK + 32], max_cols[:, :, DK + 32:P]
                nc.vector.tensor_scalar(high, m, -1.0 / MAX_STEP, None, ALU.mult).then_inc(shift_chain, 1)
                wait(dve, shift_chain, 2 * s + 2)
                nc.vector.scalar_tensor_tensor(out=rest, in0=high, scalar=MAX_STEP, in1=m,
                                               op0=ALU.mult, op1=ALU.add).then_inc(max_ready, 1)

            def finish(p, t):
                s = stage_no(p, t)
                head = 2 * p + t // 2
                part = acc[:].rearrange("p b (j w) -> p (b j) w", w=V_W)
                wait(dve, pv_free, s + 1)
                nc.vector.reciprocal(denom[:].unsqueeze(2), part[:, :, DK:DK + 1])
                nc.vector.tensor_tensor(sums[:], part[:, :, 0:DK], part[:, :, DK + 1:V_W], ALU.add).then_inc(out_chain, 1)
                wait(dve, out_chain, 2 * s + 1)
                nc.vector.tensor_tensor(sums[:], sums[:], denom[:].unsqueeze(2).to_broadcast([P, 4, DK]),
                                        ALU.mult).then_inc(out_chain, 1)
                wait(dve, out_chain, 2 * s + 2)
                wait(dve, stored, 16 * s)
                bv = bv_bc[:, ds(head * DK, DK)].unsqueeze(1).to_broadcast([P, 4, DK])
                nc.vector.tensor_tensor(out_sb[:], sums[:], bv, ALU.add).then_inc(out_ready, 1)

            def stage(p, t, first, last):
                work, find = has_work(t, last), has_max(t, last)
                before = (p, t - 1) if t else (p - 1, 3)
                count = [aux_count(bank, p, t, last) for bank in range(2)]
                his = hi_count(p, t, last)
                s = stage_no(p, t)

                def chunk(c, odd):
                    opening = isinstance(c, int) and c == 0
                    closing = isinstance(c, int) and c == CHUNKS - 1
                    at = [count[bank] + before_chunk(c, work, find, bank) for bank in range(2)]
                    if closing and find:
                        row_maxima(s + 1, at[1])
                    if not opening:
                        rest_share(p, t, c - 1, 1 - odd)
                    for j, group in enumerate(items(c, work, find)):
                        for kind, of, tile, bank in group:
                            if kind == "max":
                                maxima(of, tile, bank, at[bank])
                            elif kind != "shift":
                                rest_part(kind, p + 1, of, his + of)
                                if kind == "k" and closing:
                                    pad_keys(at[bank] + 1)
                            at[bank] = at[bank] + 1
                    if closing and not first:
                        finish(*before)

                chunks(dve, chunk)

            for b in range(2):
                nc.vector.memset(k_step[b][DK:P, :], 0.0).then_inc(zeroed, 1)
            column = v_sb[:].rearrange("p h (i w) -> p h i w", w=V_W)[:, :, :, DK]
            nc.vector.memset(column[:, 0:2, KT - 1:KT], 0.0).then_inc(zeroed, 1)
            wait(dve, zeroed, 4)
            for b in range(2):
                nc.vector.memset(k_step[b][DK:DK + 1, :], MAX_STEP)
                nc.vector.memset(k_step[b][DK + 32:DK + 33, :], -1.0)
            nc.vector.memset(column[:, 0:2, 0:KT - 1], QKV_SCALE)
            nc.vector.memset(column[0:KEYS - (KT - 1) * P, 0:2, KT - 1:KT], QKV_SCALE)
            wait(dve, loaded_w, 64)
            nc.vector.tensor_scalar(bk8[:], bk8[:], QKV_SCALE, None, ALU.mult).then_inc(consts, 1)
            for n, (lo, hi) in enumerate(((wk_l, wk_h), (wv_l, wv_h))):
                wait(dve, w_hi, n + 1)
                split_lo(nc.vector, lo[:], prob[:, n * 2 * HALF:(n + 1) * 2 * HALF], W_SCALE, hi[:]).then_inc(w_split, 1)
            for c in range(CHUNKS):
                rest_part("k", 0, c, 2 * c)
                if c == CHUNKS - 1:
                    pad_keys(2 * c + 1)
                rest_part("v", 0, c, 2 * c + 1)
            for c in range(CHUNKS):
                for i in range(4):
                    maxima(c, i, i % 2, (0 if i % 2 else 2 * CHUNKS) + 2 * c + i // 2)
            row_maxima(0, 2 * CHUNKS)
            stages(dve, stage)
            finish(PAIRS - 1, 3)


def build(nc, x_tok, ctx_t, w1T_d, w2T_d, b_d, w_red_d, wg0_d, up0, b1_d, down0, b2_d,
          wqT_d, bq8_d, wkT_d, bk8_d, wvT_d, bv_d, woT_d, up1, gate1, down1, wg1_d, out_d,
          parts=("l0", "attn", "l1")):
    q_dram = nc.dram_tensor("q_parts", [PAIRS, 2, P, TOK], FP16, kind="Internal").ap()
    ctx_dram = nc.dram_tensor("attn_out", [HEADS, 2, P, TT // 2, DK], FP32, kind="Internal").ap()
    with ExitStack() as ctx:
        sb = lambda n, s, dt=FP32: ctx.enter_context(nc.sbuf_tensor(n, s, dt))
        x_res = sb("x_res", [P, TT, D])
        ident = sb("ident", [P, P])
        rank8 = sb("rank8", [P, 8])
        identity_block(nc, ident, rank8)
        with ExitStack() as held:
            hb = lambda n, s, dt=FP32: held.enter_context(nc.sbuf_tensor(n, s, dt))
            ctx_h, ctx_l = hb("ctx_h", [P, KPAD], FP16), hb("ctx_l", [P, KPAD], FP16)
            with ExitStack() as first:
                fb = lambda n, s, dt=FP32: first.enter_context(nc.sbuf_tensor(n, s, dt))
                xT, xTh, xTl = fb("l0_xT", [P, TOK]), fb("l0_xTh", [P, TOK], FP16), fb("l0_xTl", [P, TOK], FP16)
                w1T, w2T, b = fb("l0_w1T", [P, D]), fb("l0_w2T", [P, D]), fb("l0_b", [P, D])
                w_red, wg, b1, b2 = fb("w_red", [P, 16]), fb("wg0", [8, 16]), fb("b1", [P, 8 * FC]), fb("b2", [8, D])
                gates = fb("gates0", [P, 8 * TT])
                load_block(nc, "a", [(x_res[:], x_tok), (w1T[:], w1T_d), (w2T[:], w2T_d), (b[:], b_d.to_broadcast([P, D])),
                                (w_red[:], w_red_d), (wg[:], wg0_d), (b1[:], b1_d), (b2[:], b2_d)])
                layernorm_block(nc, "ln0", x_res, ident, xT, None, None)
                l0_linear_block(nc, x_res, xT, ctx_t, ctx_h, ctx_l, w1T, w2T, b)
                layernorm_block(nc, "ln1", x_res, ident, xT, xTh, xTl)
                l0_router_block(nc, x_res, xT, w_red, wg, b2, ident, rank8, gates)
                moe_block(nc, "moe0", 8, False, xTh, xTl, up0, None, down0, b1, gates, x_res)
            with ExitStack() as second:
                qb = lambda n, s, dt=FP32: second.enter_context(nc.sbuf_tensor(n, s, dt))
                xTh, xTl = qb("l1_xTh", [P, TOK], FP16), qb("l1_xTl", [P, TOK], FP16)
                wqT, bq8 = qb("wqT", [P, HEADS * DK]), qb("bq8", [P, PAIRS])
                load_block(nc, "b", [(wqT[:], wqT_d), (bq8[:], bq8_d)], scale=[(bq8, QKV_SCALE)])
                layernorm_block(nc, "ln2", x_res, ident, None, xTh, xTl)
                q_block(nc, xTh, xTl, wqT, bq8, q_dram)
            if "attn" in parts:
                attention_block(nc, ctx_h, ctx_l, wkT_d, wvT_d, bk8_d, bv_d, q_dram, ctx_dram, ident)
        with ExitStack() as third:
            tb = lambda n, s, dt=FP32: third.enter_context(nc.sbuf_tensor(n, s, dt))
            woT, wg = tb("woT", [P, HEADS * DK]), tb("wg1", [P, 8])
            xT, xTh, xTl = tb("l2_xT", [P, TOK]), tb("l2_xTh", [P, TOK], FP16), tb("l2_xTl", [P, TOK], FP16)
            gates = tb("gates1", [P, 9 * TT])
            load_block(nc, "c", [(woT[:], woT_d), (wg[:], wg1_d)])
            if "attn" in parts:
                wo_block(nc, x_res, ctx_dram, woT, ident)
            layernorm_block(nc, "ln3", x_res, ident, xT, xTh, xTl)
            l1_router_block(nc, xT, wg, rank8, gates)
            moe_block(nc, "moe1", 9, True, xTh, xTl, up1, gate1, down1, None, gates, x_res)
        store_block(nc, x_res, out_d)


def store_block(nc, x_res, out_d):
    with ExitStack() as ctx:
        stored = ctx.enter_context(nc.semaphore("stored"))
        block = ctx.enter_context(nc.Block())

        @block.sync
        def _(sp):
            sp.dma_start(out_d, x_res[:]).then_inc(stored, 16)
            sp.wait_ge(stored, 16)


def lay_out(x, ctx_1024, L0_xattn_W, L0_xattn_b, L0_ffn_w_red, L0_ffn_wg, L0_ffn_w1, L0_ffn_b1, L0_ffn_w2, L0_ffn_b2,
            L1_xattn_Wq, L1_xattn_bq, L1_xattn_Wk, L1_xattn_bk, L1_xattn_Wv, L1_xattn_bv, L1_xattn_Wo,
            L1_ffn_w1s, L1_ffn_w2s, L1_ffn_w3s, L1_ffn_W1, L1_ffn_W2, L1_ffn_W3, L1_ffn_Wg):
    import numpy as np
    up = lambda w: w.transpose(1, 0, 2).reshape(D, -1)
    down = lambda w: w.reshape(-1, FC, P, D).transpose(2, 0, 1, 3).reshape(P, -1)
    shared = lambda one, many: np.concatenate([one[None], many])
    by_pair = lambda v: v.reshape(PAIRS, P).T
    return {
        "x_tok": x.reshape(TT, P, D).transpose(1, 0, 2), "ctx_t": ctx_1024[0].T,
        "w1T": L0_xattn_W[:, :D].T, "w2T": L0_xattn_W[:, D:].T, "b": L0_xattn_b[None],
        "w_red": L0_ffn_w_red, "wg0": L0_ffn_wg, "up0": up(L0_ffn_w1),
        "b1": L0_ffn_b1.reshape(8, FC, P).transpose(2, 0, 1).reshape(P, -1), "down0": down(L0_ffn_w2), "b2": L0_ffn_b2,
        "wqT": L1_xattn_Wq.T, "bq": by_pair(L1_xattn_bq), "wkT": L1_xattn_Wk.T, "bk": by_pair(L1_xattn_bk),
        "wvT": L1_xattn_Wv.T, "bv": L1_xattn_bv[None],
        "woT": L1_xattn_Wo.T.reshape(HEADS * DK // P, P, D).transpose(1, 0, 2).reshape(P, -1),
        "up1": up(shared(L1_ffn_w1s, L1_ffn_W1)), "gate1": up(shared(L1_ffn_w2s, L1_ffn_W2)),
        "down1": down(shared(L1_ffn_w3s, L1_ffn_W3)), "wg1": L1_ffn_Wg,
    }


def kernel(**inputs):
    import numpy as np
    import concourse.bacc as bacc
    from concourse.bass_utils import run_bass_kernel_spmd

    arrays = {"in_" + n: np.ascontiguousarray(a) for n, a in lay_out(**{k: np.asarray(v) for k, v in inputs.items()}).items()}
    nc = bacc.Bacc("TRN2", target_bir_lowering=False, num_devices=1)
    args = [nc.dram_tensor(n, a.shape, mybir.dt.from_np(a.dtype), kind="ExternalInput").ap() for n, a in arrays.items()]
    out = nc.dram_tensor("out", (P, TT, D), FP32, kind="ExternalOutput").ap()
    build(nc, *args, out)
    r = run_bass_kernel_spmd(nc, [arrays], core_ids=[0])
    return r.results[0]["out"].transpose(1, 0, 2).reshape(1, TOK, D)
```

```python
import concourse.bass as bass
from concourse import mybir
from contextlib import ExitStack

FP32 = mybir.dt.float32
FP16 = mybir.dt.float16
BF16 = mybir.dt.bfloat16
ALU = mybir.AluOpType
ACT = mybir.ActivationFunctionType
AX = mybir.AxisListType.X

P = 128
D = 128
TOK = 1024
TT = TOK // P
HALF = 512
KEYS = 6404
KT = -(-KEYS // P)
KPAD = KT * P
HEADS, DK = 16, 64
PAIRS = HEADS // 2
FF = 512
FC = FF // P
EPS = 1e-5

QKV_SCALE = 8.0
MOE_SCALE = 16.0
EXP_SCALE = 1.0 / (QKV_SCALE * QKV_SCALE * DK ** 0.5)
MAX_STEP = 1024.0

CHUNK_TILES = 4
CHUNKS = -(-KT // CHUNK_TILES)
STEPS = -(-KT // 2)
SLOTS = 4
V_W = 2 * DK + 1


class Linear:

    def __init__(self, variable=None, terms=(), constant=0):
        self.terms = list(terms) if variable is None else [(1, variable)]
        self.constant = constant

    def __add__(self, other):
        if isinstance(other, Linear):
            terms = list(self.terms)
            for k, v in other.terms:
                same = [n for n, (_, w) in enumerate(terms) if w is v]
                if same:
                    terms[same[0]] = (terms[same[0]][0] + k, v)
                else:
                    terms.append((k, v))
            return Linear(terms=terms, constant=self.constant + other.constant)
        return Linear(terms=self.terms, constant=self.constant + other)

    def __sub__(self, other):
        return self + -other

    def __mul__(self, k):
        return Linear(terms=[(c * k, v) for c, v in self.terms], constant=self.constant * k)

    def halved(self):
        assert all(c % 2 == 0 for c, _ in self.terms) and self.constant % 2 == 0
        return Linear(terms=[(c // 2, v) for c, v in self.terms], constant=self.constant // 2)

    __radd__, __rmul__ = __add__, __mul__

    def value(self):
        total = self.constant
        for k, v in self.terms:
            total = v * k + total
        return total


def value(x):
    return x.value() if isinstance(x, Linear) else x


def ds(start, size):
    return bass.ds(value(start), size)


def wait(engine, semaphore, count):
    if not (isinstance(count, int) and count <= 0):
        engine.wait_ge(semaphore, value(count))


def passed(engine, semaphore):
    engine.sem_inc(semaphore, 1)


def chunk_tiles(last):
    return KT - CHUNK_TILES * (CHUNKS - 1) if last else CHUNK_TILES


def split_lo(vec, lo, src, scale, hi):
    return vec.scalar_tensor_tensor(out=lo, in0=src, scalar=scale, in1=hi, op0=ALU.mult, op1=ALU.subtract)


def layernorm_block(nc, name, x_res, ident, xT, xTh, xTl, loads=None):
    with ExitStack() as ctx:
        stats = ctx.enter_context(nc.sbuf_tensor(f"{name}_stats", [P, TT, 6], FP32))
        mv = ctx.enter_context(nc.sbuf_tensor(f"{name}_mv", [P, TT, 2], FP32))
        rstd = ctx.enter_context(nc.sbuf_tensor(f"{name}_rstd", [P, TT], FP32))
        xn = ctx.enter_context(nc.sbuf_tensor(f"{name}_xn", [P, TT, D], FP32))
        tp = [ctx.enter_context(nc.psum_tensor(f"{name}_tp{i}", [P, HALF], FP32)) for i in range(2)]
        chain = ctx.enter_context(nc.semaphore(f"{name}_chain"))
        var_ready = ctx.enter_context(nc.semaphore(f"{name}_var_ready"))
        rooted = ctx.enter_context(nc.semaphore(f"{name}_rooted"))
        normed = ctx.enter_context(nc.semaphore(f"{name}_normed"))
        turned = ctx.enter_context(nc.semaphore(f"{name}_turned"))
        hi_done = ctx.enter_context(nc.semaphore(f"{name}_hi_done"))
        block = ctx.enter_context(nc.Block())
        if loads is not None:
            block.sync(loads)

        @block.vector
        def _(dve):
            for t in range(TT):
                nc.vector.bn_stats(stats[:, t, :], x_res[:, t, :]).then_inc(chain, 1)
            dve.wait_ge(chain, TT)
            for t in range(TT):
                nc.vector.bn_aggr(mv[:, t, :], stats[:, t, :]).then_inc(chain, 1)
            dve.wait_ge(chain, 2 * TT)
            nc.vector.tensor_scalar(rstd[:], mv[:, :, 1], EPS, None, ALU.add).then_inc(var_ready, 1)
            dve.wait_ge(rooted, 1)
            nc.vector.reciprocal(rstd[:], rstd[:]).then_inc(chain, 1)
            dve.wait_ge(chain, 2 * TT + 1)
            for t in range(TT):
                nc.vector.tensor_scalar(xn[:, t, :], x_res[:, t, :], mv[:, t, 0:1], rstd[:, t:t + 1],
                                        ALU.subtract, ALU.mult).then_inc(normed, 1)
            if xTl is not None:
                for i in range(2):
                    dve.wait_ge(hi_done, i + 1)
                    split_lo(nc.vector, xTl[:, i * HALF:(i + 1) * HALF], tp[i][:], 1.0,
                             xTh[:, i * HALF:(i + 1) * HALF])

        @block.tensor
        def _(pe):
            for t in range(TT):
                pe.wait_ge(normed, t + 1)
                nc.tensor.transpose(tp[t // 4][:, (t % 4) * P:(t % 4 + 1) * P], xn[:, t, :],
                                    ident[:]).then_inc(turned, 1)

        @block.scalar
        def _(act):
            act.wait_ge(var_ready, 1)
            nc.scalar.activation(rstd[:], rstd[:], ACT.Sqrt).then_inc(rooted, 1)
            for i in range(2):
                act.wait_ge(turned, 4 * (i + 1))
                if xT is not None:
                    nc.scalar.activation(xT[:, i * HALF:(i + 1) * HALF], tp[i][:], ACT.Copy)
                if xTh is not None:
                    nc.scalar.activation(xTh[:, i * HALF:(i + 1) * HALF], tp[i][:], ACT.Copy).then_inc(hi_done, 1)


def one_hot_first_max(nc, link, logits, peak, rank, value, hot, E):
    bc = lambda ap: ap.unsqueeze(2).to_broadcast([P, TT, E])
    link(nc.vector.reduce_max(peak[:], logits[:], AX))
    link(nc.vector.tensor_tensor(hot[:], logits[:], bc(peak[:]), ALU.is_equal))
    link(nc.vector.tensor_tensor(value[:], hot[:], rank[:].unsqueeze(1).to_broadcast([P, TT, E]), ALU.mult))
    link(nc.vector.reduce_max(peak[:], value[:], AX))
    link(nc.vector.tensor_tensor(hot[:], value[:], bc(peak[:]), ALU.is_equal))



class Context:
    PIECES = 4

    def __init__(self, nc, held, first, source):
        self.source = source
        self.high, self.rest = (held.enter_context(nc.sbuf_tensor(n, [P, KPAD], FP16)) for n in ("ctx_h", "ctx_l"))
        self.raw = first.enter_context(nc.sbuf_tensor("ctx_raw", [P, KEYS], FP32))
        self.loaded = [first.enter_context(nc.semaphore(f"ctx_loaded{i}")) for i in range(self.PIECES)]

    def piece(self, i):
        return slice(i * (KEYS // self.PIECES), (i + 1) * (KEYS // self.PIECES))

    def load(self, sp):
        for i in range(self.PIECES):
            sp.dma_start(self.raw[:, self.piece(i)], self.source[:, self.piece(i)]).then_inc(self.loaded[i], 16)


class ExpertWeights:

    def __init__(self, nc, ctx, name, sources):
        sb = lambda n, s, dt: ctx.enter_context(nc.sbuf_tensor(f"{name}_{n}", s, dt))
        sem = lambda n: ctx.enter_context(nc.semaphore(f"{name}_{n}"))
        self.nc, self.sources, self.count = nc, sources, len(sources)
        self.raw = sb("raw", [P, 2 * self.count * FF], FP32)
        self.high = sb("w_high", [P, 2 * self.count * FF], FP16)
        self.rest = sb("w_rest", [P, 2 * self.count * FF], FP16)
        self.loaded, self.high_done, self.split = sem("w_loaded"), sem("w_high_done"), sem("w_split")

    def columns(self, e, n, start=0, size=FF):
        return ds(value(e) % 2 * (self.count * FF) + n * FF + start, size)

    def load(self, sp, e):
        for n, source in enumerate(self.sources):
            sp.dma_start(self.raw[:, self.columns(e, n)], source[:, ds(e * FF, FF)]).then_inc(self.loaded, 16)

    def split_high(self, act, e, n):
        wait(act, self.loaded, 16 * self.count * (e + 1))
        cols = self.columns(e, n)
        self.nc.scalar.activation(self.high[:, cols], self.raw[:, cols], ACT.Copy, scale=MOE_SCALE).then_inc(self.high_done, 1)

    def split_rest(self, dve, e, n):
        wait(dve, self.high_done, self.count * e + n + 1)
        cols = self.columns(e, n)
        split_lo(self.nc.vector, self.rest[:, cols], self.raw[:, cols], MOE_SCALE, self.high[:, cols]).then_inc(self.split, 1)


class AttentionOperands:

    def __init__(self, nc, ctx, wqT_d, bq_d, wkT_d, bk_d, wvT_d, bv_d, ident):
        sb = lambda n, s, dt=FP32: ctx.enter_context(nc.sbuf_tensor(n, s, dt))
        self.nc, self.ident, self.links = nc, ident, 0
        self.sources = (wqT_d, wkT_d, wvT_d)
        self.biases = (bq_d, bk_d, bv_d)
        self.k_step = [sb(f"k_step{i}", [P, KPAD], FP16) for i in range(2)]
        self.v_sb = sb("v", [P, 3, KT * V_W], FP16)
        self.max_cols, self.ident_h = sb("max_cols", [P, 4, P], FP16), sb("ident_h", [P, P], FP16)
        self.weights = [[sb(f"w{n}_{part}", [P, HEADS * DK], FP16) for part in "hl"] for n in "qkv"]
        self.q_weights, self.kv_weights = self.weights[0], self.weights[1:]
        self.bq8, self.bk8, self.bv_bc = sb("bq8", [P, PAIRS]), sb("bk8", [P, PAIRS]), sb("bv_bc", [P, HEADS * DK])
        self.loaded = ctx.enter_context(nc.semaphore("attn_w_loaded"))
        self.chain = ctx.enter_context(nc.semaphore("attn_w_chain"))

    def link(self, pool, instruction):
        self.links += 1
        instruction.then_inc(self.chain, 1)
        pool.wait_ge(self.chain, self.links)

    def prepare(self, raw, context):
        nc = self.nc

        def program(pool):
            link = lambda instruction: self.link(pool, instruction)
            for i, source in enumerate(self.sources):
                nc.gpsimd.dma_start(raw[:, i, :], source).then_inc(self.loaded, 16)
            nc.gpsimd.dma_start(self.bq8[:], self.biases[0]).then_inc(self.loaded, 16)
            nc.gpsimd.dma_start(self.bk8[:], self.biases[1]).then_inc(self.loaded, 16)
            nc.gpsimd.dma_start(self.bv_bc[:], self.biases[2].to_broadcast([P, HEADS * DK])).then_inc(self.loaded, 16)
            for tile in self.k_step:
                link(nc.gpsimd.memset(tile[DK:P, :], 0.0))
                link(nc.gpsimd.memset(tile[DK:DK + 1, :], MAX_STEP))
                link(nc.gpsimd.memset(tile[DK + 32:DK + 33, :], -1.0))
            column = self.v_sb[:].rearrange("p h (i w) -> p h i w", w=V_W)[:, :, :, DK]
            link(nc.gpsimd.memset(column[:, 0:2, KT - 1:KT], 0.0))
            link(nc.gpsimd.memset(column[:, 0:2, 0:KT - 1], QKV_SCALE))
            link(nc.gpsimd.memset(column[0:KEYS - (KT - 1) * P, 0:2, KT - 1:KT], QKV_SCALE))
            link(nc.gpsimd.memset(self.max_cols[:], 0.0))
            link(nc.gpsimd.tensor_copy(self.ident_h[:], self.ident[:]))
            pool.wait_ge(self.loaded, 16 * (len(self.sources) + len(self.biases)))
            for tile in (self.bq8, self.bk8):
                link(nc.gpsimd.tensor_scalar(tile[:], tile[:], QKV_SCALE, None, ALU.mult))
            for i, (high, rest) in enumerate(self.weights):
                link(nc.gpsimd.tensor_scalar(raw[:, i, :], raw[:, i, :], QKV_SCALE, None, ALU.mult))
                link(nc.gpsimd.tensor_copy(high[:], raw[:, i, :]))
                link(nc.gpsimd.tensor_tensor(rest[:], raw[:, i, :], high[:], ALU.subtract))

            link(nc.gpsimd.memset(context.high[:, KEYS:KPAD], 0.0))
            link(nc.gpsimd.memset(context.rest[:, KEYS:KPAD], 0.0))
            for i in range(context.PIECES):
                piece = context.piece(i)
                link(nc.gpsimd.tensor_tensor(context.rest[:, piece], context.raw[:, piece], context.high[:, piece],
                                             ALU.subtract))

        return program


def moe_block(nc, name, E, gated, xTh, xTl, weights, b_up, gates, x_res, beside=None):
    NW = weights.count
    with ExitStack() as ctx:
        sb = lambda n, s, dt: ctx.enter_context(nc.sbuf_tensor(f"{name}_{n}", s, dt))
        ps = lambda n: [ctx.enter_context(nc.psum_tensor(f"{name}_{n}{i}", [P, HALF], FP32)) for i in range(2)]
        sem = lambda n: ctx.enter_context(nc.semaphore(f"{name}_{n}"))
        wh, wl = weights.high, weights.rest
        hidden = sb("hidden", [P, 2, FC * HALF], FP32)
        gelu = sb("gelu", [P, 2, HALF], FP32) if gated else None
        hh = hidden[:].bitcast(BF16).rearrange("p h (n two) -> p h n two", two=2)[:, :, :, 1]
        hl = sb("hl", [P, 2, FC * HALF], FP16)
        up, down = ps("up"), ps("down")
        gate = ps("gate") if gated else None
        up_full, gelu_done, hidden_done = sem("up_full"), sem("gelu_done"), sem("hidden_done")
        lo_done = sem("lo_done")
        down_full, added = sem("down_full"), sem("added")
        act_passed, sp_passed = sem("act_passed"), sem("sp_passed")
        if not gated:
            hidden_done = gelu_done
        block = ctx.enter_context(nc.Block())
        if beside is not None:
            block.gpsimd(beside)

        @block.sync
        def _(sp):
            def load(e):
                wait(sp, weights.split, NW * (e - 1))
                weights.load(sp, e)
                wait(sp, weights.loaded, 16 * NW * (e + 1))
                passed(sp, sp_passed)

            load(1)
            with sp.Fori(0, E - 2) as n:
                load(Linear(n) + 2)

        @block.tensor
        def _(pe):
            def up_chunk(e, h, f):
                if h == 0 and f == 0:
                    wait(pe, weights.split, NW * (e + 1))
                wait(pe, hidden_done, (2 * e + h) * FC + f - 1)
                for n, bank in enumerate([up, gate] if gated else [up]):
                    col = weights.columns(e, n, f * P, P)
                    tok = slice(h * HALF, (h + 1) * HALF)
                    nc.tensor.matmul(bank[f % 2][:], wh[:, col], xTh[:, tok], start=True, stop=False)
                    nc.tensor.matmul(bank[f % 2][:], wh[:, col], xTl[:, tok], start=False, stop=False)
                    last = nc.tensor.matmul(bank[f % 2][:], wl[:, col], xTh[:, tok], start=False, stop=True)
                last.then_inc(up_full, 1)

            def down_tile(e, h, j):
                if j == 0:
                    wait(pe, lo_done, (2 * e + h + 1) * FC)
                    wait(pe, added, 2 * e + h - 1)
                out = down[h][:, j * P:(j + 1) * P]
                for f in range(FC):
                    lhs = slice(f * HALF + j * P, f * HALF + (j + 1) * P)
                    col = weights.columns(e, NW - 1, f * P, P)
                    nc.tensor.matmul(out, hh[:, h, lhs], wh[:, col], start=f == 0, stop=False)
                    nc.tensor.matmul(out, hh[:, h, lhs], wl[:, col], start=False, stop=False)
                    last = nc.tensor.matmul(out, hl[:, h, lhs], wh[:, col], start=False, stop=f == FC - 1)
                if j == HALF // P - 1:
                    last.then_inc(down_full, 1)

            def items(up_item, down_item):
                for f in range(FC):
                    if up_item is not None:
                        up_chunk(*up_item, f)
                    if down_item is not None and f:
                        down_tile(*down_item, f - 1)
                if down_item is not None:
                    down_tile(*down_item, FC - 1)

            items((0, 0), None)
            items((0, 1), (0, 0))
            with pe.Fori(0, E - 1) as n:
                e = Linear(n) + 1
                items((e, 0), (e - 1, 1))
                items((e, 1), (e, 0))
            items(None, (E - 1, 1))

        @block.scalar
        def _(act):
            def split_high(e, n):
                wait(act, down_full, 2 * (e - 1))
                weights.split_high(act, e, n)

            def item(e, h, following=None):
                for f in range(FC):
                    n = (2 * e + h) * FC + f
                    wait(act, up_full, n + 1)
                    if gated:
                        wait(act, hidden_done, n - 1)
                        out = gelu[:, f % 2, :]
                    else:
                        if f == 0:
                            wait(act, down_full, 2 * e + h - 1)
                        out = hidden[:, h, f * HALF:(f + 1) * HALF]
                    if b_up is not None:
                        passed(act, act_passed)
                    bias = b_up[:, ds(e * FC + f, 1)] if b_up is not None else 0.0
                    nc.scalar.activation(out, up[f % 2][:], ACT.Gelu, bias=bias,
                                         scale=1.0 / MOE_SCALE).then_inc(gelu_done, 1)
                    if following is not None and f < NW:
                        split_high(following, f)

            item(0, 0)
            item(0, 1, following=1)
            with act.Fori(0, E - 2) as n:
                e = Linear(n) + 1
                item(e, 0)
                item(e, 1, following=e + 1)
            item(E - 1, 0)
            item(E - 1, 1)

        @block.vector
        def _(dve):
            def rest(e, h, f):
                wait(dve, hidden_done, (2 * e + h) * FC + f + 1)
                cols = slice(f * HALF, (f + 1) * HALF)
                nc.vector.tensor_tensor(hl[:, h, cols], hidden[:, h, cols], hh[:, h, cols],
                                        ALU.subtract).then_inc(lo_done, 1)

            def add(e, h):
                wait(dve, down_full, 2 * e + h + 1)
                wait(dve, added, 2 * e + h - 1)
                for j in range(HALF // P):
                    t = h * (HALF // P) + j
                    last = nc.vector.scalar_tensor_tensor(
                        out=x_res[:, t, :], in0=down[h][:, j * P:(j + 1) * P],
                        scalar=gates[:, ds(e * TT + t, 1)], in1=x_res[:, t, :], op0=ALU.mult, op1=ALU.add)
                last.then_inc(added, 1)

            def item(e, h, before, following=None):
                for f in range(FC):
                    if gated:
                        n = (2 * e + h) * FC + f
                        wait(dve, gelu_done, n + 1)
                        if f == 0:
                            wait(dve, down_full, 2 * e + h - 1)
                        nc.vector.scalar_tensor_tensor(out=hidden[:, h, f * HALF:(f + 1) * HALF], in0=gate[f % 2][:],
                                                       scalar=1.0 / MOE_SCALE, in1=gelu[:, f % 2, :],
                                                       op0=ALU.mult, op1=ALU.mult).then_inc(hidden_done, 1)
                    if f:
                        rest(e, h, f - 1)
                    if f == 1 and before is not None:
                        add(*before)
                    if following is not None and f < NW:
                        weights.split_rest(dve, following, f)
                rest(e, h, FC - 1)

            item(0, 0, None)
            item(0, 1, None, following=1)
            item(1, 0, (0, 0))
            item(1, 1, (0, 1), following=2)
            with dve.Fori(0, E - 3) as n:
                e = Linear(n) + 2
                item(e, 0, (e - 1, 0))
                item(e, 1, (e - 1, 1), following=e + 1)
            item(E - 1, 0, (E - 2, 0))
            item(E - 1, 1, (E - 2, 1))
            add(E - 1, 0)
            add(E - 1, 1)


def load_block(nc, x_res, x_tok, context):
    with ExitStack() as ctx:
        x_loaded = ctx.enter_context(nc.semaphore("x_loaded"))
        block = ctx.enter_context(nc.Block())

        @block.sync
        def _(sp):
            sp.dma_start(x_res[:], x_tok).then_inc(x_loaded, 16)
            context.load(sp)
            sp.wait_ge(x_loaded, 16)


def identity_block(nc, ident, rank8):
    with ExitStack() as ctx:
        made = ctx.enter_context(nc.semaphore("identity_made"))
        block = ctx.enter_context(nc.Block())

        @block.gpsimd
        def _(pool):
            nc.gpsimd.memset(ident[:], 0.0).then_inc(made, 1)
            pool.wait_ge(made, 1)
            nc.gpsimd.affine_select(out=ident[:], in_=ident[:], compare_op=ALU.not_equal, fill=1.0, base=0,
                                    pattern=[[-1, P]], channel_multiplier=1)

        @block.vector
        def _(dve):
            for e in range(8):
                nc.vector.memset(rank8[:, e:e + 1], float(8 - e))


def l0_linear_block(nc, x_res, xT, context, w1T, w2T, bias, operands_loaded, count, weights):
    PIECES, piece, raw, ctx_h, loaded = context.PIECES, context.piece, context.raw, context.high, context.loaded
    with ExitStack() as ctx:
        sb = lambda n, s, dt: ctx.enter_context(nc.sbuf_tensor(f"l0_{n}", s, dt))
        sums = sb("ctx_sums", [P, PIECES], FP32)
        mean = sb("ctx_mean", [P, 1], FP32)
        mean_rows = sb("mean_rows", [P, P], FP32)
        ones = sb("ones", [P, P], FP32)
        out = [ctx.enter_context(nc.psum_tensor(f"l0_out{i}", [P, HALF], FP32)) for i in range(2)]
        chain = ctx.enter_context(nc.semaphore("l0_chain"))
        mean_ready = ctx.enter_context(nc.semaphore("l0_mean_ready"))
        product = ctx.enter_context(nc.semaphore("l0_product"))
        block = ctx.enter_context(nc.Block())

        @block.scalar
        def _(act):
            for i in range(PIECES):
                act.wait_ge(loaded[i], 16)
                nc.scalar.activation(ctx_h[:, piece(i)], raw[:, piece(i)], ACT.Copy)
            for n in range(weights.count):
                weights.split_high(act, 0, n)

        @block.vector
        def _(dve):
            nc.vector.memset(ones[:], 1.0).then_inc(chain, 1)
            dve.wait_ge(operands_loaded, count)
            for i in range(PIECES):
                dve.wait_ge(loaded[i], 16)
                nc.vector.reduce_sum(sums[:, i:i + 1], raw[:, piece(i)], AX).then_inc(chain, 1)
            dve.wait_ge(chain, PIECES + 1)
            nc.vector.reduce_sum(mean[:], sums[:], AX).then_inc(chain, 1)
            dve.wait_ge(chain, PIECES + 2)
            nc.vector.tensor_scalar(mean_rows[:], ones[:], mean[:], 1.0 / KEYS, ALU.mult, ALU.mult).then_inc(mean_ready, 1)
            for t in range(TT):
                nc.vector.tensor_tensor(x_res[:, t, :], x_res[:, t, :], bias[:], ALU.add).then_inc(chain, 1)
            for n in range(weights.count):
                weights.split_rest(dve, 0, n)
            for t in range(TT):
                dve.wait_ge(product, 4 * (t // 4 + 1))
                dve.wait_ge(chain, PIECES + 3 + t)
                nc.vector.tensor_tensor(x_res[:, t, :], x_res[:, t, :], out[t // 4][:, (t % 4) * P:(t % 4 + 1) * P], ALU.add)

        @block.tensor
        def _(pe):
            pe.wait_ge(mean_ready, 1)
            for t in range(TT):
                o = out[t // 4][:, (t % 4) * P:(t % 4 + 1) * P]
                nc.tensor.matmul(o, xT[:, t * P:(t + 1) * P], w1T[:], start=True, stop=False)
                nc.tensor.matmul(o, mean_rows[:], w2T[:], start=False, stop=True).then_inc(product, 1)


def l0_router_block(nc, x_res, xT, w_red, wg, b2, ident, rank8, gates):
    E, G = 8, 16
    with ExitStack() as ctx:
        sb = lambda n, s: ctx.enter_context(nc.sbuf_tensor(f"r0_{n}", s, FP32))
        sq, ss, wgn, wgnT, redT = sb("sq", [E, G]), sb("ss", [E, 1]), sb("wgn", [E, G]), sb("wgnT", [G, E]), sb("redT", [G, TOK])
        logits, value, hot, ex, score = sb("logits", [P, TT, E]), sb("value", [P, TT, E]), sb("hot", [P, TT, E]), sb("ex", [P, TT, E]), sb("score", [P, TT])
        peak, top, scoreT = sb("peak", [P, TT]), sb("top", [P, TT]), sb("scoreT", [E, TOK])
        wT_ps = ctx.enter_context(nc.psum_tensor("r0_wT", [P, HALF], FP32))
        red_ps = [ctx.enter_context(nc.psum_tensor(f"r0_red{i}", [P, HALF], FP32)) for i in range(2)]
        lg_ps = ctx.enter_context(nc.psum_tensor("r0_lg", [P, HALF], FP32))
        sT_ps = [ctx.enter_context(nc.psum_tensor(f"r0_sT{i}", [P, HALF], FP32)) for i in range(2)]
        b2_ps = [ctx.enter_context(nc.psum_tensor(f"r0_b2{i}", [P, HALF], FP32)) for i in range(2)]
        chain = ctx.enter_context(nc.semaphore("r0_chain"))
        squared = ctx.enter_context(nc.semaphore("r0_squared"))
        rooted = ctx.enter_context(nc.semaphore("r0_rooted"))
        wgn_ready = ctx.enter_context(nc.semaphore("r0_wgn_ready"))
        turned = ctx.enter_context(nc.semaphore("r0_turned"))
        red_done = ctx.enter_context(nc.semaphore("r0_red_done"))
        evacuated = ctx.enter_context(nc.semaphore("r0_evacuated"))
        logits_done = ctx.enter_context(nc.semaphore("r0_logits_done"))
        shifted = ctx.enter_context(nc.semaphore("r0_shifted"))
        exped = ctx.enter_context(nc.semaphore("r0_exped"))
        scored = ctx.enter_context(nc.semaphore("r0_scored"))
        sT_done = ctx.enter_context(nc.semaphore("r0_sT_done"))
        sT_copied = ctx.enter_context(nc.semaphore("r0_sT_copied"))
        b2_done = ctx.enter_context(nc.semaphore("r0_b2_done"))
        block = ctx.enter_context(nc.Block())
        col = lambda t: slice((t % 4) * P, (t % 4 + 1) * P)

        @block.vector
        def _(dve):
            n = [0]

            def link(instruction):
                n[0] += 1
                instruction.then_inc(chain, 1)
                dve.wait_ge(chain, n[0])

            link(nc.vector.tensor_tensor(sq[:], wg[:], wg[:], ALU.mult))
            nc.vector.reduce_sum(ss[:], sq[:], AX).then_inc(squared, 1)
            dve.wait_ge(rooted, 1)
            link(nc.vector.tensor_scalar(ss[:], ss[:], 1e-4, None, ALU.max))
            link(nc.vector.reciprocal(ss[:], ss[:]))
            nc.vector.tensor_scalar(wgn[:], wg[:], ss[:], None, ALU.mult).then_inc(wgn_ready, 1)
            dve.wait_ge(turned, 1)
            nc.vector.tensor_copy(wgnT[:], wT_ps[0:G, 0:E]).then_inc(evacuated, 1)
            for i in range(2):
                dve.wait_ge(red_done, i + 1)
                nc.vector.tensor_copy(redT[:, i * HALF:(i + 1) * HALF], red_ps[i][0:G, :]).then_inc(evacuated, 1)
            dve.wait_ge(logits_done, 1)
            link(nc.vector.tensor_copy(logits[:], lg_ps[:, 0:TT * E].rearrange("p (t e) -> p t e", e=E)))
            link(nc.vector.reduce_max(top[:], logits[:], AX))
            nc.vector.tensor_tensor(ex[:], logits[:], top[:].unsqueeze(2).to_broadcast([P, TT, E]),
                                    ALU.subtract).then_inc(shifted, 1)
            one_hot_first_max(nc, link, logits, peak, rank8, value, hot, E)
            dve.wait_ge(exped, 1)
            link(nc.vector.reduce_sum(score[:], ex[:], AX))
            link(nc.vector.reciprocal(score[:], score[:]))
            link(nc.vector.tensor_tensor(hot[:], hot[:], score[:].unsqueeze(2).to_broadcast([P, TT, E]), ALU.mult))
            nc.vector.tensor_scalar(gates[:, 0:E * TT].rearrange("p (e t) -> p t e", t=TT), hot[:], 1.0 / MOE_SCALE,
                                    None, ALU.mult).then_inc(scored, 1)
            for i in range(2):
                dve.wait_ge(sT_done, i + 1)
                nc.vector.tensor_copy(scoreT[:, i * HALF:(i + 1) * HALF], sT_ps[i][0:E, :]).then_inc(sT_copied, 1)
            for t in range(TT):
                dve.wait_ge(b2_done, 4 * (t // 4 + 1))
                nc.vector.tensor_tensor(x_res[:, t, :], x_res[:, t, :], b2_ps[t // 4][:, col(t)], ALU.add)

        @block.scalar
        def _(act):
            act.wait_ge(squared, 1)
            nc.scalar.activation(ss[:], ss[:], ACT.Sqrt).then_inc(rooted, 1)
            act.wait_ge(shifted, 1)
            nc.scalar.activation(ex[:], ex[:], ACT.Exp).then_inc(exped, 1)

        @block.tensor
        def _(pe):
            pe.wait_ge(wgn_ready, 1)
            nc.tensor.transpose(wT_ps[0:G, 0:E], wgn[:], ident[0:E, 0:E]).then_inc(turned, 1)
            for i in range(2):
                nc.tensor.matmul(red_ps[i][0:G, :], w_red[:], xT[:, i * HALF:(i + 1) * HALF],
                                 start=True, stop=True).then_inc(red_done, 1)
            pe.wait_ge(evacuated, 3)
            for t in range(TT):
                last = nc.tensor.matmul(lg_ps[:, t * E:(t + 1) * E], redT[:, t * P:(t + 1) * P], wgnT[:],
                                        start=True, stop=True)
            last.then_inc(logits_done, 1)
            pe.wait_ge(scored, 1)
            for t in range(TT):
                last = nc.tensor.transpose(sT_ps[t // 4][0:E, col(t)], hot[:, t, :], ident[:])
                if t % 4 == 3:
                    last.then_inc(sT_done, 1)
            for t in range(TT):
                pe.wait_ge(sT_copied, t // 4 + 1)
                nc.tensor.matmul(b2_ps[t // 4][:, col(t)], scoreT[:, t * P:(t + 1) * P], b2[:],
                                 start=True, stop=True).then_inc(b2_done, 1)


def l1_router_block(nc, xT, wg, rank8, gates):
    E = 8
    with ExitStack() as ctx:
        sb = lambda n, s: ctx.enter_context(nc.sbuf_tensor(f"r1_{n}", s, FP32))
        logits, value, hot, peak = sb("logits", [P, TT, E]), sb("value", [P, TT, E]), sb("hot", [P, TT, E]), sb("peak", [P, TT])
        lg_ps = ctx.enter_context(nc.psum_tensor("r1_lg", [P, HALF], FP32))
        chain = ctx.enter_context(nc.semaphore("r1_chain"))
        logits_done = ctx.enter_context(nc.semaphore("r1_logits_done"))
        block = ctx.enter_context(nc.Block())

        @block.tensor
        def _(pe):
            for t in range(TT):
                last = nc.tensor.matmul(lg_ps[:, t * E:(t + 1) * E], xT[:, t * P:(t + 1) * P], wg[:],
                                        start=True, stop=True)
            last.then_inc(logits_done, 1)

        @block.vector
        def _(dve):
            n = [0]

            def link(instruction):
                n[0] += 1
                instruction.then_inc(chain, 1)
                dve.wait_ge(chain, n[0])

            nc.vector.memset(gates[:, 0:TT], 1.0 / MOE_SCALE)
            dve.wait_ge(logits_done, 1)
            link(nc.vector.tensor_copy(logits[:], lg_ps[:, 0:TT * E].rearrange("p (t e) -> p t e", e=E)))
            one_hot_first_max(nc, link, logits, peak, rank8, value, hot, E)
            nc.vector.tensor_scalar(gates[:, TT:(E + 1) * TT].rearrange("p (e t) -> p t e", t=TT), hot[:],
                                    1.0 / MOE_SCALE, None, ALU.mult)


def q_block(nc, xTh, xTl, weights, bq8, q_dram):
    BANKS, BUFFERS = 4, 4
    with ExitStack() as ctx:
        wh, wl = weights
        qh, ql = (ctx.enter_context(nc.sbuf_tensor(f"q_{n}", [P, BUFFERS, TOK], FP16)) for n in ("qh", "ql"))
        stored = [ctx.enter_context(nc.semaphore(f"q_stored{i}")) for i in range(BUFFERS)]
        ps = [ctx.enter_context(nc.psum_tensor(f"q_ps{i}", [P, HALF], FP32)) for i in range(BANKS)]
        full, hi_done, lo_done = (ctx.enter_context(nc.semaphore(f"q_{n}")) for n in ("full", "hi_done", "lo_done"))
        block = ctx.enter_context(nc.Block())

        @block.scalar
        def _(act):
            for p in range(PAIRS):
                for i in range(2):
                    act.wait_ge(full, 2 * p + i + 1)
                    if p >= BUFFERS and i == 0:
                        act.wait_ge(stored[p % BUFFERS], 32 * (p // BUFFERS))
                    nc.scalar.activation(qh[:, p % BUFFERS, i * HALF:(i + 1) * HALF], ps[(2 * p + i) % BANKS][:],
                                         ACT.Identity, bias=bq8[:, p:p + 1]).then_inc(hi_done, 1)

        @block.vector
        def _(dve):
            for p in range(PAIRS):
                for i in range(2):
                    dve.wait_ge(hi_done, 2 * p + i + 1)
                    cols = slice(i * HALF, (i + 1) * HALF)
                    nc.vector.scalar_tensor_tensor(out=ql[:, p % BUFFERS, cols], in0=ps[(2 * p + i) % BANKS][:],
                                                   scalar=bq8[:, p:p + 1], in1=qh[:, p % BUFFERS, cols],
                                                   op0=ALU.add, op1=ALU.subtract).then_inc(lo_done, 1)

        @block.tensor
        def _(pe):
            for p in range(PAIRS):
                w = slice(p * P, (p + 1) * P)
                for i in range(2):
                    n = 2 * p + i
                    x = slice(i * HALF, (i + 1) * HALF)
                    if n >= BANKS:
                        pe.wait_ge(lo_done, n - BANKS + 1)
                    out = ps[n % BANKS][:]
                    nc.tensor.matmul(out, wh[:, w], xTh[:, x], start=True, stop=False)
                    nc.tensor.matmul(out, wh[:, w], xTl[:, x], start=False, stop=False)
                    nc.tensor.matmul(out, wl[:, w], xTh[:, x], start=False, stop=True).then_inc(full, 1)

        @block.sync
        def _(sp):
            for p in range(PAIRS):
                sp.wait_ge(lo_done, 2 * p + 2)
                for part, tile in enumerate((qh, ql)):
                    sp.dma_start(q_dram[p, part], tile[:, p % BUFFERS, :]).then_inc(stored[p % BUFFERS], 16)
            for i in range(BUFFERS):
                sp.wait_ge(stored[i], 32 * (PAIRS // BUFFERS))


def wo_block(nc, x_res, ctx_dram, woT, woT_d, wg, wg_d, ident, weights):
    ITEMS = 2 * PAIRS
    GROUP = 2
    JT = TT // 2
    with ExitStack() as ctx:
        sb = lambda n, s, dt: ctx.enter_context(nc.sbuf_tensor(f"wo_{n}", s, dt))
        rows = sb("rows", [P, 2, JT, HEADS * DK], FP32)
        turned_sb = sb("turned", [P, 2, JT * P], FP32)
        tp = [ctx.enter_context(nc.psum_tensor(f"wo_tp{i}", [P, HALF], FP32)) for i in range(2)]
        out = [ctx.enter_context(nc.psum_tensor(f"wo_out{i}", [P, HALF], FP32)) for i in range(2)]
        loaded = [ctx.enter_context(nc.semaphore(f"wo_loaded{i}")) for i in range(ITEMS // GROUP)]
        w_loaded, turned, copied, product = (ctx.enter_context(nc.semaphore(f"wo_{n}"))
                                             for n in ("w_loaded", "turned_s", "copied", "product"))
        block = ctx.enter_context(nc.Block())

        @block.sync
        def _(sp):
            for g in range(ITEMS // GROUP):
                i, first = g * GROUP // PAIRS, g * GROUP % PAIRS
                cols = slice(first * P, (first + GROUP) * P)
                sp.dma_start(rows[:, i, :, cols], ctx_dram[i, :, :, cols]).then_inc(loaded[g], 16)
                if g == 0:
                    sp.dma_start(woT[:], woT_d).then_inc(w_loaded, 16)
                    sp.dma_start(wg[:], wg_d).then_inc(w_loaded, 16)
            weights.load(sp, 0)

        @block.tensor
        def _(pe):
            def turn(n):
                i, e = n // PAIRS, n % PAIRS
                if n % GROUP == 0:
                    pe.wait_ge(loaded[n // GROUP], 16)
                if n >= 2:
                    pe.wait_ge(copied, n - 1)
                for j in range(JT):
                    last = nc.tensor.transpose(tp[n % 2][:, j * P:(j + 1) * P], rows[:, i, j, e * P:(e + 1) * P], ident[:])
                last.then_inc(turned, 1)

            turn(0)
            pe.wait_ge(w_loaded, 32)
            for n in range(ITEMS):
                i, e = n // PAIRS, n % PAIRS
                if n + 1 < ITEMS:
                    turn(n + 1)
                pe.wait_ge(copied, n + 1)
                for j in range(JT):
                    last = nc.tensor.matmul(out[i][:, j * P:(j + 1) * P], turned_sb[:, n % 2, j * P:(j + 1) * P],
                                            woT[:, e * P:(e + 1) * P], start=e == 0 and j == 0, stop=e == PAIRS - 1,
                                            skip_group_check=True)
                last.then_inc(product, 1)

        @block.scalar
        def _(act):
            for n in range(ITEMS):
                act.wait_ge(turned, n + 1)
                if n >= 2:
                    act.wait_ge(product, n - 1)
                nc.scalar.activation(turned_sb[:, n % 2, :], tp[n % 2][:], ACT.Copy).then_inc(copied, 1)
            for n in range(weights.count):
                weights.split_high(act, 0, n)

        @block.vector
        def _(dve):
            for i in range(2):
                dve.wait_ge(product, (i + 1) * PAIRS)
                half = x_res[:, i * JT:(i + 1) * JT, :]
                nc.vector.tensor_tensor(half, half, out[i][:].rearrange("p (j d) -> p j d", d=D), ALU.add)
            for n in range(weights.count):
                weights.split_rest(dve, 0, n)


def attention_block(nc, ctx_h, ctx_l, ops, q_dram, ctx_dram):
    with ExitStack() as ctx:
        sb = lambda n, s, dt=FP32: ctx.enter_context(nc.sbuf_tensor(n, s, dt))
        ps = lambda n, s: ctx.enter_context(nc.psum_tensor(n, s, FP32))
        sem = lambda n: ctx.enter_context(nc.semaphore(n))

        k_both = [sb(f"k_both{i}", [P, KPAD], FP16) for i in range(2)]
        k_step = ops.k_step
        k_hi, k_lo = sb("k_hi", [P, KPAD], FP16), sb("k_lo", [P, KPAD], FP16)
        q_both = [sb(f"q_both{i}", [P, TOK], FP16) for i in range(2)]
        q_step = [sb(f"q_step{i}", [P, TOK], FP16) for i in range(2)]
        v_sb = ops.v_sb
        wk_h, wk_l, wv_h, wv_l = (part for pair in ops.kv_weights for part in pair)
        bk8, bv_bc, max_cols, ident_h = ops.bk8, ops.bv_bc, ops.max_cols, ops.ident_h
        prob, prob_l = sb("prob", [P, SLOTS * 2 * HALF]), sb("prob_l", [P, SLOTS * 2 * HALF], FP16)
        prob_h = prob[:].bitcast(BF16).rearrange("p (n two) -> p n two", two=2)[:, :, 1]
        chunk_max, row_max = sb("chunk_max", [P, 4 * CHUNKS]), sb("row_max", [P, 4])
        projected = sb("projected", [P, 2, HALF])
        acc = sb("acc", [P, 2, 2 * V_W])
        denom, sums, out_sb = sb("denom", [P, 4]), sb("sums", [P, 4, DK]), sb("out_sb", [P, 4, DK])

        score = [ps(f"score{i}", [P, 2 * HALF]) for i in range(2)]
        pv = ps("pv", [P, 2, HALF])
        aux = [ps(f"aux{i}", [P, HALF]) for i in range(2)]

        head_loaded = [sem("head_a_loaded"), sem("head_b_loaded")]
        v_loaded = sem("v_loaded")
        score_full, exp_done = sem("score_full"), sem("exp_done")
        rest_pool, rest_dve, pv_done = sem("rest_pool"), sem("rest_dve"), sem("pv_done")
        aux_full = [sem("aux_full0"), sem("aux_full1")]
        aux_free = [sem("aux_free0"), sem("aux_free1")]
        rest_done, hi_done, k_padded = sem("rest_done"), sem("hi_done"), sem("k_padded")
        max_ready, pv_free, out_ready, stored = sem("max_ready"), sem("pv_free"), sem("out_ready"), sem("out_stored")
        shift_chain, out_chain = sem("shift_chain"), sem("out_chain")
        act_passed, sp_passed = sem("act_passed"), sem("sp_passed")
        block = ctx.enter_context(nc.Block())

        WORK = (None, "k", "v", None)
        LOADS = 6
        PROLOGUE = ([("k", c, None) for c in range(CHUNKS)] + [("v", c, None) for c in range(CHUNKS)]
                    + [("max", c, i) for c in range(CHUNKS) for i in range(4)])
        PRO_AUX0, PRO_AUX1 = len(PROLOGUE) // 2, len(PROLOGUE) // 2 + 1

        def stage_no(p, t):
            return 4 * p + t

        def items(c, odd, work, find):
            opening, closing = isinstance(c, int) and c < 2, isinstance(c, int) and c == CHUNKS - 1
            flip = odd if work else 0
            beside = [[], [], [], []]
            if find and not closing:
                for i in range(4):
                    beside[i].append(("max", c, i, (i % 2 if i or not work else 1) ^ flip))
                if opening:
                    beside[2].append(("max", CHUNKS - 1, 2 * c, 1 ^ flip))
                    beside[3].insert(0, ("max", CHUNKS - 1, 2 * c + 1, 0 ^ flip))
            if work:
                beside[0].append((work, c, None, 0 ^ flip))
            if find and closing:
                beside[1].append(("shift", None, None, 1))
            return beside

        def bank_items(c, odd, work, find, bank):
            return sum(1 for group in items(c, odd, work, find) for item in group if item[3] == bank)

        def before_chunk(c, odd, work, find, bank):
            if isinstance(c, int):
                return sum(bank_items(n, n % 2, work, find, bank) for n in range(c))
            even, uneven = (bank_items(2, 0, work, find, bank), bank_items(3, 1, work, find, bank))
            pairs = (c + (-2 - odd)).halved()
            return before_chunk(2, 0, work, find, bank) + pairs * (even + uneven) + (even if odd else 0)

        def aux_count(bank, p, t, last):
            of = lambda u, l: before_chunk(CHUNKS, 1, has_work(u, l), has_max(u, l), bank)
            return ((PRO_AUX1 if bank else PRO_AUX0) + sum(of(u, False) for u in range(4)) * p
                    + sum(of(u, last) for u in range(t)))

        def has_work(t, last):
            return WORK[t] if not last else None

        def has_max(t, last):
            return not (last and t == 3)

        def hi_count(p, t, last):
            return 2 * CHUNKS + 2 * CHUNKS * p + sum(CHUNKS for u in range(t) if has_work(u, last))

        def width(c):
            return P * chunk_tiles(isinstance(c, int) and c == CHUNKS - 1)

        def step_tiles(g):
            return 1 if isinstance(g, int) and g == STEPS - 1 else 2

        def chunks(engine, body):
            body(0, 0)
            body(1, 1)
            with engine.Fori(0, (CHUNKS - 3) // 2) as m:
                body(2 * Linear(m) + 2, 0)
                body(2 * Linear(m) + 3, 1)
            body(CHUNKS - 1, 0)

        def stages(engine, stage):
            stage(0, 0, True, False)
            with engine.Fori(0, PAIRS - 1) as pair:
                p = Linear(pair)
                for t in (1, 2, 3):
                    stage(p, t, False, False)
                stage(p + 1, 0, False, False)
            for t in (1, 2, 3):
                stage(PAIRS - 1, t, False, True)

        def share_tile(c):
            return (1, 0) if isinstance(c, int) and c == CHUNKS - 1 else (1, 1)

        def pool_rests(s, c, k, i):
            return (3 * CHUNKS - 1) * s + 3 * c + 2 * k + i

        def v_rows(c):
            n = width(c) // P
            return v_sb[:, 0:2, ds(c * CHUNK_TILES * V_W, n * V_W)].rearrange("p h (i w) -> p h i w", w=V_W)

        def v_projected(c, buffer):
            return projected[:, buffer, 0:width(c)].rearrange("p (i h w) -> p h i w", h=2, w=DK)

        def slot(odd, t, k):
            return (((odd + t) % 2) * 2 + k) * 2 * HALF

        @block.sync
        def _(sp):
            def load_head(p, b):
                rows = slice(b * DK, (b + 1) * DK)
                done = head_loaded[b]
                sp.dma_start(k_both[b][0:DK, :], k_hi[rows, :]).then_inc(done, 16)
                sp.dma_start(k_both[b][DK:P, :], k_lo[rows, :]).then_inc(done, 16)
                sp.dma_start(k_step[b][0:DK, :], k_hi[rows, :]).then_inc(done, 16)
                q = q_dram[ds(p, 1), :, rows, :].rearrange("o c r n -> (o c) r n")
                sp.dma_start(q_both[b][0:DK, :], q[0]).then_inc(done, 16)
                sp.dma_start(q_both[b][DK:P, :], q[0]).then_inc(done, 16)
                sp.dma_start(q_step[b][0:DK, :], q[1]).then_inc(done, 16)

            def store(p, t):
                wait(sp, out_ready, stage_no(p, t) + 1)
                head = 2 * p + t // 2
                sp.dma_start(ctx_dram[t % 2, :, :, ds(head * DK, DK)], out_sb[:]).then_inc(stored, 16)

            def stage(p, t, first, last):
                if t in (0, 2) and not (last and t):
                    b = 1 if t == 0 else 0
                    wait(sp, score_full, STEPS * stage_no(p, t) + 1)
                    passed(sp, sp_passed)
                    wait(sp, k_padded, p + (1 if t == 0 else 2))
                    passed(sp, sp_passed)
                    load_head(p if t == 0 else p + 1, b)
                if t == 0:
                    wait(sp, pv_done, STEPS * stage_no(p, 0))
                    wait(sp, rest_done, hi_count(p, 0, last))
                    sp.dma_start(v_sb[:, 2, :], v_sb[:, 1, :]).then_inc(v_loaded, 16)
                if t:
                    store(p, t - 1)
                elif not first:
                    store(p - 1, 3)

            wait(sp, k_padded, 1)
            load_head(0, 0)
            stages(sp, stage)
            store(PAIRS - 1, 3)
            wait(sp, stored, 16 * 4 * PAIRS)

        @block.tensor
        def _(pe):
            def scores(p, t, c, k, i, last):
                g = 2 * c + k
                n = STEPS * stage_no(p, t) + g
                b = t // 2
                if i == 0:
                    wait(pe, exp_done, n - 1)
                q = slice((t % 2) * HALF, (t % 2 + 1) * HALF)
                keys = ds((2 * g + i) * P, P)
                out = score[k][:, i * HALF:(i + 1) * HALF]
                nc.tensor.matmul(out, k_both[b][:, keys], q_both[b][:, q], start=True, stop=False)
                if isinstance(g, int) and g == 0 and i == 0:
                    wait(pe, aux_free[1], aux_count(1, p, t, last))
                done = nc.tensor.matmul(out, k_step[b][:, keys], q_step[b][:, q], start=False, stop=True)
                if i == step_tiles(g) - 1:
                    done.then_inc(score_full, 1)

            def maxima(p, t, c, i, bank, base):
                tile = (t % 2) * 4 + i
                wait(pe, aux_free[bank], base)
                nc.tensor.matmul(aux[bank][:, 0:width(c)], q_both[t // 2][:, tile * P:(tile + 1) * P],
                                 k_both[t // 2][:, ds(c * HALF, width(c))],
                                 start=True, stop=True).then_inc(aux_full[bank], 1)

            def project_k(p, c, bank, base):
                wait(pe, aux_free[bank], base)
                w, keys = ds(p * P, P), ds(c * HALF, width(c))
                out = aux[bank][:, 0:width(c)]
                nc.tensor.matmul(out, wk_h[:, w], ctx_h[:, keys], start=True, stop=False)
                nc.tensor.matmul(out, wk_h[:, w], ctx_l[:, keys], start=False, stop=False)
                nc.tensor.matmul(out, wk_l[:, w], ctx_h[:, keys], start=False, stop=True).then_inc(aux_full[bank], 1)

            def project_v(pair, c, bank, base):
                wait(pe, aux_free[bank], base)
                w = ds(pair * P, P)
                for i in range(width(c) // P):
                    keys = ds(c * HALF + i * P, P)
                    out = aux[bank][:, i * P:(i + 1) * P]
                    nc.tensor.matmul(out, ctx_h[:, keys], wv_h[:, w], start=True, stop=False)
                    nc.tensor.matmul(out, ctx_h[:, keys], wv_l[:, w], start=False, stop=False)
                    last = nc.tensor.matmul(out, ctx_l[:, keys], wv_h[:, w], start=False, stop=True)
                last.then_inc(aux_full[bank], 1)

            project = {"k": project_k, "v": project_v}

            def shift(s, base):
                wait(pe, max_ready, s + 1)
                wait(pe, aux_free[1], base)
                for i in range(4):
                    last = nc.tensor.matmul(aux[1][:, i * P:(i + 1) * P], max_cols[:, i, :], ident_h[:],
                                            start=True, stop=True)
                last.then_inc(aux_full[1], 1)

            def weigh(p, t, c, odd, k, i, last):
                g = 2 * c + k
                s = stage_no(p, t)
                b = t // 2
                if isinstance(g, int) and g == 0 and i == 0:
                    wait(pe, pv_free, s)
                    if b == 0:
                        wait(pe, rest_done, hi_count(p, t, last))
                    else:
                        wait(pe, v_loaded, 16 * (p + 1))
                if (k, i) == share_tile(c):
                    wait(pe, rest_dve, CHUNKS * s + c + 1)
                else:
                    wait(pe, rest_pool, pool_rests(s, c, k, i) + 1)
                for j in range(4):
                    cols = ds(slot(odd, t, k) + i * HALF + j * P, P)
                    out = pv[:, j // 2, (j % 2) * V_W:(j % 2 + 1) * V_W]
                    v = (2 * g + i) * V_W
                    start = isinstance(g, int) and g == 0 and i == 0 and j % 2 == 0
                    stop = isinstance(g, int) and g == STEPS - 1
                    nc.tensor.matmul(out, prob_h[:, cols], v_sb[:, 2 * b, ds(v, V_W)],
                                     start=start, stop=False, skip_group_check=True)
                    done = nc.tensor.matmul(out[:, 0:DK + 1], prob_l[:, cols], v_sb[:, 2 * b, ds(v, DK + 1)],
                                            start=False, stop=stop, skip_group_check=True)
                if i == step_tiles(g) - 1:
                    done.then_inc(pv_done, 1)

            def stage(p, t, first, last):
                work, find = has_work(t, last), has_max(t, last)
                before = (p, t - 1) if t else (p - 1, 3)
                after = (p, t + 1) if t < 3 else (p + 1, 0)
                count = [aux_count(bank, p, t, last) for bank in range(2)]
                if find and t in (1, 3):
                    wait(pe, head_loaded[after[1] // 2], 16 * LOADS * (after[0] + 1))

                def chunk(c, odd):
                    opening = isinstance(c, int) and c == 0
                    closing = isinstance(c, int) and c == CHUNKS - 1
                    at = [count[bank] + before_chunk(c, odd, work, find, bank) for bank in range(2)]
                    for j, group in enumerate(items(c, odd, work, find)):
                        k, i = j // 2, j % 2
                        if not (closing and j == 3):
                            scores(p, t, c, k, i, last)
                        for kind, of, tile, bank in group:
                            if kind == "max":
                                maxima(*after, of, tile, bank, at[bank])
                            elif kind == "shift":
                                shift(stage_no(p, t) + 1, at[bank])
                            else:
                                project[kind](p + 1, of, bank, at[bank])
                            at[bank] = at[bank] + 1
                        if not opening:
                            weigh(p, t, c - 1, 1 - odd, k, i, last)
                        elif not first and j < 3:
                            weigh(*before, CHUNKS - 1, 0, k, i, False)

                chunks(pe, chunk)

            for n, (kind, c, i) in enumerate(PROLOGUE):
                if kind == "max":
                    if (c, i) == (0, 0):
                        wait(pe, head_loaded[0], 16 * LOADS)
                    maxima(0, 0, c, i, n % 2, n // 2)
                else:
                    project[kind](0, c, n % 2, n // 2)
            shift(0, PRO_AUX1 - 1)
            stages(pe, stage)
            for j in range(KT - CHUNK_TILES * (CHUNKS - 1)):
                weigh(PAIRS - 1, 3, CHUNKS - 1, 0, j // 2, j % 2, True)

        @block.scalar
        def _(act):
            def probabilities(p, t, c, odd, k):
                g = 2 * c + k
                s = stage_no(p, t)
                n = STEPS * s + g
                w = step_tiles(g) * HALF
                wait(act, score_full, n + 1)
                wait(act, pv_done, n - SLOTS + 1)
                nc.scalar.activation(prob[:, ds(slot(odd, t, k), w)], score[k][:, 0:w], ACT.Exp,
                                     scale=EXP_SCALE).then_inc(exp_done, 1)

            def high_part(kind, p, c, bank, base, buffer, his):
                wait(act, rest_done, his - (0 if isinstance(c, int) and c == 0 else 1))
                wait(act, aux_full[bank], base + 1)
                passed(act, act_passed)
                w = width(c)
                bias = bk8[:, ds(p, 1)] if kind == "k" else 0.0
                nc.scalar.activation(projected[:, buffer, 0:w], aux[bank][:, 0:w], ACT.Identity,
                                     bias=bias).then_inc(aux_free[bank], 1)
                wait(act, aux_free[bank], base + 1)
                out, projection = (k_hi[:, ds(c * HALF, w)], projected[:, buffer, 0:w]) if kind == "k" else (
                    v_rows(c)[:, :, :, 0:DK], v_projected(c, buffer))
                nc.scalar.activation(out, projection, ACT.Copy).then_inc(hi_done, 1)

            def shift(s, t, n1):
                wait(act, aux_full[1], n1 + 1)
                q = slice((t % 2) * HALF, (t % 2 + 1) * HALF)
                nc.scalar.activation(q_step[t // 2][DK:P, q], aux[1][DK:P, :], ACT.Copy).then_inc(aux_free[1], 1)

            def evacuate(s):
                wait(act, pv_done, STEPS * (s + 1))
                wait(act, out_ready, s)
                nc.scalar.activation(acc[:], pv[:, :, 0:2 * V_W], ACT.Copy).then_inc(pv_free, 1)

            def stage(p, t, first, last):
                work = has_work(t, last)
                count = [aux_count(bank, p, t, last) for bank in range(2)]
                find = has_max(t, last)
                if work == "k":
                    wait(act, head_loaded[1], 16 * LOADS * (p + 1))
                if work == "v":
                    wait(act, v_loaded, 16 * (p + 1))

                def chunk(c, odd):
                    if work:
                        high_part(work, p + 1, c, odd, count[odd] + before_chunk(c, odd, work, find, odd),
                                  odd, hi_count(p, t, last) + c)
                    probabilities(p, t, c, odd, 0)
                    if isinstance(c, int) and c == 0 and not first:
                        evacuate(stage_no(p, t) - 1)
                    if isinstance(c, int) and c == CHUNKS - 1 and find:
                        shift(stage_no(p, t) + 1, (t + 1) % 4,
                              count[1] + before_chunk(c, odd, work, find, 1))
                    probabilities(p, t, c, odd, 1)

                chunks(act, chunk)

            for n, (kind, c, i) in enumerate(PROLOGUE):
                if kind != "max":
                    high_part(kind, 0, c, n % 2, n // 2, n % 2, n)
            shift(0, 0, PRO_AUX1 - 1)
            stages(act, stage)
            evacuate(4 * PAIRS - 1)

        @block.gpsimd
        def _(pool):
            def stage(p, t, first, last):
                def chunk(c, odd):
                    for k, i in ((0, 0), (0, 1), (1, 0)):
                        if (k, i) == share_tile(c):
                            continue
                        if i == 0:
                            wait(pool, exp_done, STEPS * stage_no(p, t) + 2 * c + k + 1)
                        hl = ds(slot(odd, t, k) + i * HALF, HALF)
                        nc.gpsimd.tensor_tensor(prob_l[:, hl], prob[:, hl], prob_h[:, hl],
                                                ALU.subtract).then_inc(rest_pool, 1)

                chunks(pool, chunk)

            stages(pool, stage)

        @block.vector
        def _(dve):
            def rest_share(p, t, c, odd):
                s = stage_no(p, t)
                wait(dve, exp_done, STEPS * s + 2 * c + 2)
                hl = ds(slot(odd, t, 1) + share_tile(c)[1] * HALF, HALF)
                nc.vector.tensor_tensor(prob_l[:, hl], prob[:, hl], prob_h[:, hl],
                                        ALU.subtract).then_inc(rest_dve, 1)

            def maxima(c, i, bank, base):
                wait(dve, aux_full[bank], base + 1)
                nc.vector.reduce_max(chunk_max[:, ds(i * CHUNKS + c, 1)],
                                     aux[bank][:, 0:width(c)], AX).then_inc(aux_free[bank], 1)

            def rest_part(kind, c, buffer, his):
                wait(dve, hi_done, his + 1)
                w = width(c)
                if kind == "k":
                    keys = ds(c * HALF, w)
                    nc.vector.tensor_tensor(k_lo[:, keys], projected[:, buffer, 0:w], k_hi[:, keys],
                                            ALU.subtract).then_inc(rest_done, 1)
                else:
                    rows = v_rows(c)
                    nc.vector.tensor_tensor(rows[:, :, :, DK + 1:V_W], v_projected(c, buffer), rows[:, :, :, 0:DK],
                                            ALU.subtract).then_inc(rest_done, 1)

            def pad_keys(n):
                wait(dve, rest_done, n)
                for m, tile in enumerate((k_hi, k_lo)):
                    last = nc.vector.tensor_copy(tile[:, KEYS:KPAD], tile[:, KEYS - 1:KEYS].to_broadcast([P, KPAD - KEYS]))
                last.then_inc(k_padded, 1)

            def row_maxima(s, counts):
                for bank in range(2):
                    wait(dve, aux_free[bank], counts[bank])
                nc.vector.reduce_max(row_max[:], chunk_max[:].rearrange("p (i c) -> p i c", c=CHUNKS),
                                     AX).then_inc(shift_chain, 1)
                wait(dve, shift_chain, 2 * s + 1)
                m = row_max[:].unsqueeze(2).to_broadcast([P, 4, 32])
                high, rest = max_cols[:, :, DK:DK + 32], max_cols[:, :, DK + 32:P]
                nc.vector.tensor_scalar(high, m, -1.0 / MAX_STEP, None, ALU.mult).then_inc(shift_chain, 1)
                wait(dve, shift_chain, 2 * s + 2)
                nc.vector.scalar_tensor_tensor(out=rest, in0=high, scalar=MAX_STEP, in1=m,
                                               op0=ALU.mult, op1=ALU.add).then_inc(max_ready, 1)

            def finish(p, t):
                s = stage_no(p, t)
                head = 2 * p + t // 2
                part = acc[:].rearrange("p b (j w) -> p (b j) w", w=V_W)
                wait(dve, pv_free, s + 1)
                nc.vector.reciprocal(denom[:].unsqueeze(2), part[:, :, DK:DK + 1])
                nc.vector.tensor_tensor(sums[:], part[:, :, 0:DK], part[:, :, DK + 1:V_W], ALU.add).then_inc(out_chain, 1)
                wait(dve, out_chain, 2 * s + 1)
                nc.vector.tensor_tensor(sums[:], sums[:], denom[:].unsqueeze(2).to_broadcast([P, 4, DK]),
                                        ALU.mult).then_inc(out_chain, 1)
                wait(dve, out_chain, 2 * s + 2)
                wait(dve, stored, 16 * s)
                bv = bv_bc[:, ds(head * DK, DK)].unsqueeze(1).to_broadcast([P, 4, DK])
                nc.vector.tensor_tensor(out_sb[:], sums[:], bv, ALU.add).then_inc(out_ready, 1)

            def stage(p, t, first, last):
                work, find = has_work(t, last), has_max(t, last)
                before = (p, t - 1) if t else (p - 1, 3)
                count = [aux_count(bank, p, t, last) for bank in range(2)]
                his = hi_count(p, t, last)
                s = stage_no(p, t)

                def chunk(c, odd):
                    opening = isinstance(c, int) and c == 0
                    closing = isinstance(c, int) and c == CHUNKS - 1
                    at = [count[bank] + before_chunk(c, odd, work, find, bank) for bank in range(2)]
                    if closing and find:
                        row_maxima(s + 1, at)
                    if not opening:
                        rest_share(p, t, c - 1, 1 - odd)
                    elif not first:
                        rest_share(*before, CHUNKS - 1, 0)
                    for j, group in enumerate(items(c, odd, work, find)):
                        for kind, of, tile, bank in group:
                            if kind == "max":
                                maxima(of, tile, bank, at[bank])
                            at[bank] = at[bank] + 1
                        if work and j == 1:
                            rest_part(work, c, odd, his + c)
                            if work == "k" and closing:
                                pad_keys(his + c + 1)
                    if closing and not first:
                        finish(*before)

                chunks(dve, chunk)

            for n, (kind, c, i) in enumerate(PROLOGUE):
                if kind == "max":
                    maxima(c, i, n % 2, n // 2)
                    continue
                rest_part(kind, c, n % 2, n)
                if (kind, c) == ("k", CHUNKS - 1):
                    pad_keys(n + 1)
            row_maxima(0, (PRO_AUX0, PRO_AUX1 - 1))
            stages(dve, stage)
            rest_share(PAIRS - 1, 3, CHUNKS - 1, 0)
            finish(PAIRS - 1, 3)


def build(nc, x_tok, ctx_t, w1T_d, w2T_d, b_d, w_red_d, wg0_d, up0, b1_d, down0, b2_d,
          wqT_d, bq8_d, wkT_d, bk8_d, wvT_d, bv_d, woT_d, up1, gate1, down1, wg1_d, out_d):
    q_dram = nc.dram_tensor("q_parts", [PAIRS, 2, P, TOK], FP16, kind="Internal").ap()
    ctx_dram = nc.dram_tensor("attn_out", [2, P, TT // 2, HEADS * DK], FP32, kind="Internal").ap()
    with ExitStack() as ctx:
        sb = lambda n, s, dt=FP32: ctx.enter_context(nc.sbuf_tensor(n, s, dt))
        x_res = sb("x_res", [P, TT, D])
        ident = sb("ident", [P, P])
        rank8 = sb("rank8", [P, 8])
        identity_block(nc, ident, rank8)
        with ExitStack() as held:
            hb = lambda n, s, dt=FP32: held.enter_context(nc.sbuf_tensor(n, s, dt))
            ops = AttentionOperands(nc, held, wqT_d, bq8_d, wkT_d, bk8_d, wvT_d, bv_d, ident)
            with ExitStack() as first:
                context = Context(nc, held, first, ctx_t)
                experts = ExpertWeights(nc, first, "moe0", (up0, down0))
                fb = lambda n, s, dt=FP32: first.enter_context(nc.sbuf_tensor(n, s, dt))
                xT, xTh, xTl = fb("l0_xT", [P, TOK]), fb("l0_xTh", [P, TOK], FP16), fb("l0_xTl", [P, TOK], FP16)
                w1T, w2T, b = fb("l0_w1T", [P, D]), fb("l0_w2T", [P, D]), fb("l0_b", [P, D])
                w_red, wg, b1, b2 = fb("w_red", [P, 16]), fb("wg0", [8, 16]), fb("b1", [P, 8 * FC]), fb("b2", [8, D])
                gates = fb("gates0", [P, 8 * TT])
                loaded = first.enter_context(nc.semaphore("loaded"))
                loads = [(w1T[:], w1T_d), (w2T[:], w2T_d), (b[:], b_d.to_broadcast([P, D])),
                         (w_red[:], w_red_d), (wg[:], wg0_d), (b1[:], b1_d), (b2[:], b2_d)]

                def start_loads(sp):
                    for dst, src in loads:
                        sp.dma_start(dst, src).then_inc(loaded, 16)
                    experts.load(sp, 0)

                load_block(nc, x_res, x_tok, context)
                layernorm_block(nc, "ln0", x_res, ident, xT, None, None, loads=start_loads)
                l0_linear_block(nc, x_res, xT, context, w1T, w2T, b, loaded, 16 * len(loads), experts)
                layernorm_block(nc, "ln1", x_res, ident, xT, xTh, xTl)
                raw = fb("attn_w_raw", [P, 3, HEADS * DK])
                l0_router_block(nc, x_res, xT, w_red, wg, b2, ident, rank8, gates)
                moe_block(nc, "moe0", 8, False, xTh, xTl, experts, b1, gates, x_res, beside=ops.prepare(raw, context))
            with ExitStack() as second:
                qb = lambda n, s, dt=FP32: second.enter_context(nc.sbuf_tensor(n, s, dt))
                xTh, xTl = qb("l1_xTh", [P, TOK], FP16), qb("l1_xTl", [P, TOK], FP16)
                layernorm_block(nc, "ln2", x_res, ident, None, xTh, xTl)
                q_block(nc, xTh, xTl, ops.q_weights, ops.bq8, q_dram)
            attention_block(nc, context.high, context.rest, ops, q_dram, ctx_dram)
        with ExitStack() as third:
            tb = lambda n, s, dt=FP32: third.enter_context(nc.sbuf_tensor(n, s, dt))
            woT, wg = tb("woT", [P, HEADS * DK]), tb("wg1", [P, 8])
            xT, xTh, xTl = tb("l2_xT", [P, TOK]), tb("l2_xTh", [P, TOK], FP16), tb("l2_xTl", [P, TOK], FP16)
            gates = tb("gates1", [P, 9 * TT])
            experts = ExpertWeights(nc, third, "moe1", (up1, gate1, down1))
            wo_block(nc, x_res, ctx_dram, woT, woT_d, wg, wg1_d, ident, experts)
            layernorm_block(nc, "ln3", x_res, ident, xT, xTh, xTl)
            l1_router_block(nc, xT, wg, rank8, gates)
            moe_block(nc, "moe1", 9, True, xTh, xTl, experts, None, gates, x_res)
        store_block(nc, x_res, out_d)


def store_block(nc, x_res, out_d):
    with ExitStack() as ctx:
        stored = ctx.enter_context(nc.semaphore("stored"))
        block = ctx.enter_context(nc.Block())

        @block.sync
        def _(sp):
            sp.dma_start(out_d, x_res[:]).then_inc(stored, 16)
            sp.wait_ge(stored, 16)


def lay_out(x, ctx_1024, L0_xattn_W, L0_xattn_b, L0_ffn_w_red, L0_ffn_wg, L0_ffn_w1, L0_ffn_b1, L0_ffn_w2, L0_ffn_b2,
            L1_xattn_Wq, L1_xattn_bq, L1_xattn_Wk, L1_xattn_bk, L1_xattn_Wv, L1_xattn_bv, L1_xattn_Wo,
            L1_ffn_w1s, L1_ffn_w2s, L1_ffn_w3s, L1_ffn_W1, L1_ffn_W2, L1_ffn_W3, L1_ffn_Wg):
    import numpy as np
    up = lambda w: w.transpose(1, 0, 2).reshape(D, -1)
    down = lambda w: w.reshape(-1, FC, P, D).transpose(2, 0, 1, 3).reshape(P, -1)
    shared = lambda one, many: np.concatenate([one[None], many])
    by_pair = lambda v: v.reshape(PAIRS, P).T
    return {
        "x_tok": x.reshape(TT, P, D).transpose(1, 0, 2), "ctx_t": ctx_1024[0].T,
        "w1T": L0_xattn_W[:, :D].T, "w2T": L0_xattn_W[:, D:].T, "b": L0_xattn_b[None],
        "w_red": L0_ffn_w_red, "wg0": L0_ffn_wg, "up0": up(L0_ffn_w1),
        "b1": L0_ffn_b1.reshape(8, FC, P).transpose(2, 0, 1).reshape(P, -1), "down0": down(L0_ffn_w2), "b2": L0_ffn_b2,
        "wqT": L1_xattn_Wq.T, "bq": by_pair(L1_xattn_bq), "wkT": L1_xattn_Wk.T, "bk": by_pair(L1_xattn_bk),
        "wvT": L1_xattn_Wv.T, "bv": L1_xattn_bv[None],
        "woT": L1_xattn_Wo.T.reshape(HEADS * DK // P, P, D).transpose(1, 0, 2).reshape(P, -1),
        "up1": up(shared(L1_ffn_w1s, L1_ffn_W1)), "gate1": up(shared(L1_ffn_w2s, L1_ffn_W2)),
        "down1": down(shared(L1_ffn_w3s, L1_ffn_W3)), "wg1": L1_ffn_Wg,
    }


def kernel(**inputs):
    import numpy as np
    import concourse.bacc as bacc
    from concourse.bass_utils import run_bass_kernel_spmd

    arrays = {"in_" + n: np.ascontiguousarray(a) for n, a in lay_out(**{k: np.asarray(v) for k, v in inputs.items()}).items()}
    nc = bacc.Bacc("TRN2", target_bir_lowering=False, num_devices=1)
    args = [nc.dram_tensor(n, a.shape, mybir.dt.from_np(a.dtype), kind="ExternalInput").ap() for n, a in arrays.items()]
    out = nc.dram_tensor("out", (P, TT, D), FP32, kind="ExternalOutput").ap()
    build(nc, *args, out)
    r = run_bass_kernel_spmd(nc, [arrays], core_ids=[0])
    return r.results[0]["out"].transpose(1, 0, 2).reshape(1, TOK, D)
```
